# Optimizing a Trainium2 kernel written in Bass

```python
import numpy as np
import jax
import jax.numpy as jnp

def _softmax(x, axis=-1):
    return jax.nn.softmax(x, axis=axis)
def _gelu(x):
    return jax.nn.gelu(x, approximate=True)
def _silu(x):
    return jax.nn.silu(x)
def _sigmoid(x):
    return jax.nn.sigmoid(x)
def _layernorm(x, axis=-1, eps=1e-5):
    m = jnp.mean(x, axis=axis, keepdims=True)
    v = jnp.var(x, axis=axis, keepdims=True)
    return (x - m) / jnp.sqrt(v + eps)
def _scatter_add(tgt, idx, src, axis=0):
    return tgt.at[idx].add(src)
def _segment_sum(src, seg, n):
    return jax.ops.segment_sum(src, seg, n)

kernel_name = 'mk_audio_tower_d1_tok_audfeat256_8b3ab7'

def setup_inputs(seed: int = 0):
    np.random.seed(seed)
    _w = jnp.asarray
    def _rec_inputs():
        import jax
        import jax.numpy as jnp
        _rk = jax.random.key(seed)
        x = (1.50771e-05 + 1.00003 * jax.random.normal(jax.random.fold_in(_rk, 1), (8, 3000, 256), jnp.float32))
        return x
    x = _rec_inputs()
    def _L0_tok_setup():
        import jax, jax.numpy as jnp
        import numpy as np
        POOL_SIZE = 2
        KERNEL_SIZE = 3

        def _blur_weights(channels):
            k = jnp.array([2.0, 4.0, 2.0], dtype=jnp.float32) / 8.0
            return jnp.tile(k[:, None, None], (1, 1, channels))
        key = jax.random.key(seed)
        B, W, C = (16, 16384, 256)
        x = jax.random.normal(key, (B, W, C), dtype=jnp.float32)
        blur_kernel = _blur_weights(C)
        return {'x': x, 'blur_kernel': blur_kernel}
    _L0_tok_all = _L0_tok_setup()
    _L0_tok_in = {k: v for k, v in _L0_tok_all.items() if k in ('blur_kernel', )}
    del _L0_tok_all

    def _L0_attn_setup():
        import jax, jax.numpy as jnp
        import numpy as np
        D = 256
        L = 2
        B, S = (8, 4096)
        LR = 0.001
        WD = 0.01
        MAX_ALR = 0.1
        EPS = 1e-08

        def _lmm(Ws, bs, x):
            for i in range(L):
                x = x + jax.nn.silu(x @ Ws[i] + bs[i])
            return x

        def _reference_tuple_inner(x, Wk, Wq, Wv, Wlr, blr, Ws, bs):
            keys = x @ Wk
            queries = x @ Wq
            values = x @ Wv
            alr = (jax.nn.sigmoid(x @ Wlr + blr) * MAX_ALR).reshape(-1)

            def loss_fn(params):
                Ws_, bs_ = params
                preds = _lmm(Ws_, bs_, keys).reshape(-1, D)
                tgt = values.reshape(-1, D)
                per_tok = jnp.mean((preds - tgt) ** 2, axis=-1)
                return jnp.sum(per_tok * alr)
            gWs, gbs = jax.grad(loss_fn)((Ws, bs))

            def adamw_step(p, g):
                return p * (1.0 - LR * WD) - LR * g / (jnp.sqrt(g * g) + EPS)
            nWs = adamw_step(Ws, gWs)
            nbs = adamw_step(bs, gbs)
            retrieved = _lmm(nWs, nbs, queries)
            return (retrieved, -gWs, -gbs)
        key = jax.random.key(seed)
        ks = jax.random.split(key, 9)
        scale = 0.05
        return {'x': jax.random.normal(ks[0], (B, S, D), dtype=jnp.float32), 'Wk': jax.random.normal(ks[1], (D, D), dtype=jnp.float32) * scale, 'Wq': jax.random.normal(ks[2], (D, D), dtype=jnp.float32) * scale, 'Wv': jax.random.normal(ks[3], (D, D), dtype=jnp.float32) * scale, 'Wlr': jax.random.normal(ks[4], (D, 1), dtype=jnp.float32) * scale, 'blr': jnp.zeros((1,), dtype=jnp.float32), 'Ws': jax.random.normal(ks[5], (L, D, D), dtype=jnp.float32) * scale, 'bs': jnp.zeros((L, D), dtype=jnp.float32)}
    _L0_attn_all = _L0_attn_setup()
    _L0_attn_in = {k: v for k, v in _L0_attn_all.items() if k in ('Wk', 'Wq', 'Wv', 'Wlr', 'blr', 'Ws', 'bs', )}
    del _L0_attn_all

    def _L0_ffn_setup():
        import jax, jax.numpy as jnp
        import numpy as np
        BN_EPS = 0.001

        def _bn(h, g, b, m, v):
            return g * (h - m) * jax.lax.rsqrt(v + BN_EPS) + b
        key = jax.random.key(seed)
        ks = jax.random.split(key, 8)
        B, F, Df = (256, 64, 256)
        E, H, D = (8, 256, 256)
        s1 = 1.0 / np.sqrt(Df)
        s2 = 1.0 / np.sqrt(H)
        return {'x': jax.random.normal(ks[0], (B, F, Df), jnp.float32), 'Wr': jax.random.normal(ks[1], (Df, E), jnp.float32) * s1, 'br': jnp.zeros((E,), jnp.float32), 'W1': jax.random.normal(ks[2], (E, Df, H), jnp.float32) * s1, 'b1': jnp.zeros((E, H), jnp.float32), 'g1': jnp.ones((E, H), jnp.float32), 'be1': jnp.zeros((E, H), jnp.float32), 'm1': jnp.zeros((E, H), jnp.float32), 'v1': jnp.ones((E, H), jnp.float32), 'W2': jax.random.normal(ks[3], (E, H, H), jnp.float32) * s2, 'b2': jnp.zeros((E, H), jnp.float32), 'g2': jnp.ones((E, H), jnp.float32), 'be2': jnp.zeros((E, H), jnp.float32), 'm2': jnp.zeros((E, H), jnp.float32), 'v2': jnp.ones((E, H), jnp.float32), 'Wo': jax.random.normal(ks[4], (E, H, D), jnp.float32) * s2, 'bo': jnp.zeros((E, D), jnp.float32)}
    _L0_ffn_all = _L0_ffn_setup()
    _L0_ffn_in = {k: v for k, v in _L0_ffn_all.items() if k in ('Wr', 'br', 'W1', 'b1', 'g1', 'be1', 'm1', 'v1', 'W2', 'b2', 'g2', 'be2', 'm2', 'v2', 'Wo', 'bo', )}
    del _L0_ffn_all

    return {
        "x": x,
        "L0_tok_blur_kernel": _L0_tok_in["blur_kernel"],
        "L0_attn_Wk": _L0_attn_in["Wk"],
        "L0_attn_Wq": _L0_attn_in["Wq"],
        "L0_attn_Wv": _L0_attn_in["Wv"],
        "L0_attn_Wlr": _L0_attn_in["Wlr"],
        "L0_attn_blr": _L0_attn_in["blr"],
        "L0_attn_Ws": _L0_attn_in["Ws"],
        "L0_attn_bs": _L0_attn_in["bs"],
        "L0_ffn_Wr": _L0_ffn_in["Wr"],
        "L0_ffn_br": _L0_ffn_in["br"],
        "L0_ffn_W1": _L0_ffn_in["W1"],
        "L0_ffn_b1": _L0_ffn_in["b1"],
        "L0_ffn_g1": _L0_ffn_in["g1"],
        "L0_ffn_be1": _L0_ffn_in["be1"],
        "L0_ffn_m1": _L0_ffn_in["m1"],
        "L0_ffn_v1": _L0_ffn_in["v1"],
        "L0_ffn_W2": _L0_ffn_in["W2"],
        "L0_ffn_b2": _L0_ffn_in["b2"],
        "L0_ffn_g2": _L0_ffn_in["g2"],
        "L0_ffn_be2": _L0_ffn_in["be2"],
        "L0_ffn_m2": _L0_ffn_in["m2"],
        "L0_ffn_v2": _L0_ffn_in["v2"],
        "L0_ffn_Wo": _L0_ffn_in["Wo"],
        "L0_ffn_bo": _L0_ffn_in["bo"],
    }

def reference(x, L0_tok_blur_kernel, L0_attn_Wk, L0_attn_Wq, L0_attn_Wv, L0_attn_Wlr, L0_attn_blr, L0_attn_Ws, L0_attn_bs, L0_ffn_Wr, L0_ffn_br, L0_ffn_W1, L0_ffn_b1, L0_ffn_g1, L0_ffn_be1, L0_ffn_m1, L0_ffn_v1, L0_ffn_W2, L0_ffn_b2, L0_ffn_g2, L0_ffn_be2, L0_ffn_m2, L0_ffn_v2, L0_ffn_Wo, L0_ffn_bo):
    import jax
    import jax.numpy as jnp
    def _L0_tok_ref(x, blur_kernel):
        import jax, jax.numpy as jnp
        import numpy as np
        POOL_SIZE = 2
        KERNEL_SIZE = 3

        def _blur_weights(channels):
            k = jnp.array([2.0, 4.0, 2.0], dtype=jnp.float32) / 8.0
            return jnp.tile(k[:, None, None], (1, 1, channels))
        p = jax.lax.reduce_window(x, -jnp.inf, jax.lax.max, window_dimensions=(1, POOL_SIZE, 1), window_strides=(1, 1, 1), padding='SAME')
        C = x.shape[-1]
        out = jax.lax.conv_general_dilated(p, blur_kernel, window_strides=(POOL_SIZE,), padding='SAME', dimension_numbers=('NWC', 'WIO', 'NWC'), feature_group_count=C)
        return out

    def _L0_attn_ref(x, Wk, Wq, Wv, Wlr, blr, Ws, bs):
        import jax, jax.numpy as jnp
        import numpy as np
        D = 256
        L = 2
        B, S = (8, 4096)
        LR = 0.001
        WD = 0.01
        MAX_ALR = 0.1
        EPS = 1e-08

        def _lmm(Ws, bs, x):
            for i in range(L):
                x = x + jax.nn.silu(x @ Ws[i] + bs[i])
            return x

        def _reference_tuple_inner(x, Wk, Wq, Wv, Wlr, blr, Ws, bs):
            keys = x @ Wk
            queries = x @ Wq
            values = x @ Wv
            alr = (jax.nn.sigmoid(x @ Wlr + blr) * MAX_ALR).reshape(-1)

            def loss_fn(params):
                Ws_, bs_ = params
                preds = _lmm(Ws_, bs_, keys).reshape(-1, D)
                tgt = values.reshape(-1, D)
                per_tok = jnp.mean((preds - tgt) ** 2, axis=-1)
                return jnp.sum(per_tok * alr)
            gWs, gbs = jax.grad(loss_fn)((Ws, bs))

            def adamw_step(p, g):
                return p * (1.0 - LR * WD) - LR * g / (jnp.sqrt(g * g) + EPS)
            nWs = adamw_step(Ws, gWs)
            nbs = adamw_step(bs, gbs)
            retrieved = _lmm(nWs, nbs, queries)
            return (retrieved, -gWs, -gbs)
        return _reference_tuple_inner(x, Wk, Wq, Wv, Wlr, blr, Ws, bs)[0]

    def _L0_ffn_ref(x, Wr, br, W1, b1, g1, be1, m1, v1, W2, b2, g2, be2, m2, v2, Wo, bo):
        import jax, jax.numpy as jnp
        import numpy as np
        BN_EPS = 0.001

        def _bn(h, g, b, m, v):
            return g * (h - m) * jax.lax.rsqrt(v + BN_EPS) + b
        feat = jnp.mean(x, axis=0)
        w = jax.nn.softmax(feat @ Wr + br, axis=-1)
        h = jnp.einsum('bfd,edh->bfeh', x, W1) + b1
        h = jax.nn.relu(_bn(h, g1, be1, m1, v1))
        h = jnp.einsum('bfeh,ehk->bfek', h, W2) + b2
        h = jax.nn.relu(_bn(h, g2, be2, m2, v2))
        y = jnp.einsum('bfeh,ehd->bfed', h, Wo) + bo
        return jnp.einsum('bfed,fe->bfd', y, w)

    h = _L0_tok_ref(x, L0_tok_blur_kernel)
    h = h + _L0_attn_ref(_layernorm(h, axis=-1), L0_attn_Wk, L0_attn_Wq, L0_attn_Wv, L0_attn_Wlr, L0_attn_blr, L0_attn_Ws, L0_attn_bs)
    h = h + _L0_ffn_ref(_layernorm(h, axis=-1), L0_ffn_Wr, L0_ffn_br, L0_ffn_W1, L0_ffn_b1, L0_ffn_g1, L0_ffn_be1, L0_ffn_m1, L0_ffn_v1, L0_ffn_W2, L0_ffn_b2, L0_ffn_g2, L0_ffn_be2, L0_ffn_m2, L0_ffn_v2, L0_ffn_Wo, L0_ffn_bo)
    return h


_drawn_inputs = setup_inputs


def setup_inputs(seed=0):
    import zlib

    import numpy as np

    out = dict(_drawn_inputs(seed))
    spreads = {'L0_attn_bs': (0.0, 0.1),
     'L0_ffn_br': (0.0, 0.333),
     'L0_ffn_b1': (0.0, 0.558),
     'L0_ffn_g1': (1.0, 0.538),
     'L0_ffn_be1': (0.0, 0.57),
     'L0_ffn_m1': (0.0, 0.55),
     'L0_ffn_v1': (1.0, 0.6),
     'L0_ffn_b2': (0.0, 0.398),
     'L0_ffn_g2': (1.0, 0.2),
     'L0_ffn_be2': (0.0, 0.404),
     'L0_ffn_m2': (0.0, 0.409),
     'L0_ffn_v2': (1.0, 0.6),
     'L0_ffn_bo': (0.0, 0.295)}
    factors = {'L0_attn_Wk': 6.077, 'L0_attn_Wv': 8.0, 'L0_attn_Wlr': 8.0}
    for name, (base, spread) in spreads.items():
        noise = np.random.default_rng([zlib.crc32(name.encode()), seed]).standard_normal(out[name].shape)
        drawn = base * np.exp(spread * noise) if base else spread * noise
        out[name] = jnp.asarray(drawn.astype(out[name].dtype))
    for name, factor in factors.items():
        out[name] = (out[name] * factor).astype(out[name].dtype)
    return out
```

```python
from contextlib import ExitStack

import concourse.bass as bass
from concourse import mybir

F32 = mybir.dt.float32
F32R = mybir.dt.float32r
ALU = mybir.AluOpType
ACT = mybir.ActivationFunctionType
AX_X = mybir.AxisListType.X

B = 8
D = 256
KT = D // 128
TOK = 125
NJ = 12
TILES = B * NJ
TOKENS = NJ * TOK
CH = 4
CHUNKS = NJ // CH
E = 8
GRP = 4
NTOK = GRP * TOK
TP = TOK + 1
HI, LO = 0, 1

LR, WD, ADAM_EPS, MAX_ALR = 0.001, 0.01, 1e-8, 0.1
LN_EPS, BN_EPS = 1e-5, 1e-3
GRAD_SCALE = MAX_ALR * 2.0 / D

STATS, NORM, X_T, LAYER0, LAYER1, BACK1, GRAD0 = 4, 5, 6, 7, 8, 9, 10


class Step:

    def __init__(self, b, t):
        self.b, self.t = b, t

    def has(self, lag):
        return not isinstance(self.b, int) or 0 <= NJ * self.b + self.t - lag < TILES

    def n(self, lag):
        return self.b * NJ + (self.t - lag + 1)

    def slot(self, lag, ring):
        return (self.t - lag) % ring

    def chunk(self, lag):
        return (self.t - lag) // CH

    def part(self, lag):
        return (self.t - lag) % CH


class Pace:

    def __init__(self, J, n):
        self.J, self.i = J, n

    def has(self, lag=0):
        return not isinstance(self.J, int) or 0 <= 16 * (self.J - 1) + self.i - lag < 16 * NJ

    def n(self, lag=0, per=1):
        return self.J * (16 * per) + per * (self.i - lag + 1 - 16)

    def expert(self, lag=0):
        return (self.i - lag) % E

    def group(self, lag=0):
        return (self.i - lag) // E % 2

    def tile(self, lag):
        b = self.i - lag
        return b if 0 <= b < B and not (isinstance(self.J, int) and self.J >= NJ) else None

    def m(self, b, per=1):
        return self.J * (B * per) + (b + 1) * per

    def has_m(self, b):
        return not isinstance(self.J, int) or self.J * B + b >= 0


def audio_tower(nc, x, blur, wk, wq, wv, wlr, blr, ws, bs, wr, br, w1, b1, g1, be1, m1, v1,
                w2, b2, g2, be2, m2, v2, wo, bo, out):
    h_dram = nc.dram_tensor("h_dram", (B, TOKENS, D), F32, kind="Internal").ap()
    q_dram = nc.dram_tensor("q_dram", (B, TOKENS, D), F32, kind="Internal").ap()
    s_dram = nc.dram_tensor("s_dram", (2, E * D), F32, kind="Internal").ap()

    with ExitStack() as keep:
        def sb_keep(name, shape, dt=F32):
            return keep.enter_context(nc.sbuf_tensor(name, shape, dt))

        eye = sb_keep("eye", [128, 128])
        eye_r = sb_keep("eye_r", [128, TP], F32R)
        bias_on = sb_keep("bias_on", [128, TOK], F32R)
        new_w = sb_keep("new_w", [128, 2, 2, KT, D], F32R)
        new_bias = sb_keep("new_bias", [128, 2, D], F32R)
        minus_half = sb_keep("minus_half", [128, 128])
        ln_eps = sb_keep("ln_eps", [128, 1])

        gradient_sweep(nc, x, blur, wk, wq, wv, wlr, blr, ws, bs, h_dram, q_dram,
                       eye, eye_r, bias_on, new_w, new_bias, minus_half, ln_eps)
        with ExitStack() as ex:
            def sb_ex(name, shape, dt=F32):
                return ex.enter_context(nc.sbuf_tensor(name, shape, dt))
            ffn_w = [sb_ex(f"ffn_w{i}", [128, E, 2, KT, D], F32R) for i in range(3)]
            ffn_bias = sb_ex("ffn_bias", [128, 2, KT * E])
            expert_weights(nc, w1, b1, g1, be1, m1, v1, w2, b2, g2, be2, m2, v2, wo, s_dram,
                           ffn_w, ffn_bias, eye, minus_half)
            block_sweep(nc, wr, br, bo, h_dram, q_dram, out, ffn_w, ffn_bias,
                        eye, eye_r, bias_on, new_w, new_bias, minus_half, ln_eps)


def gradient_sweep(nc, x, blur, wk, wq, wv, wlr, blr, ws, bs, h_dram, q_dram,
                   eye, eye_r, bias_on, new_w, new_bias, minus_half, ln_eps):
    x_rows = x.rearrange("b (p r) d -> b p (r d)", r=2 * NJ)
    h_tok = h_dram.rearrange("b (p j) d -> b p (j d)", j=NJ)
    q_tok = q_dram.rearrange("b (p j) d -> b p (j d)", j=NJ)

    with ExitStack() as ctx:
        def sb(name, shape, dt=F32):
            return ctx.enter_context(nc.sbuf_tensor(name, shape, dt))

        def psum(name, shape):
            return ctx.enter_context(nc.psum_tensor(name, shape, F32))

        def sem(name):
            return ctx.enter_context(nc.semaphore(name))

        raw_k = sb("raw_k", [128, KT, D])
        raw_q = sb("raw_q", [128, KT, D])
        raw_v = sb("raw_v", [128, KT, D])
        raw_w = sb("raw_w", [128, 2, KT, D])
        raw_lr = sb("raw_lr", [128, KT, 2])
        raw_b = sb("raw_b", [33, 2, D + 2])
        wk_t = sb("wk_t", [128, KT, D])
        w_kz = sb("w_kz", [128, 2, KT, 2 * D], F32R)
        w_vq = sb("w_vq", [128, 2, KT, 2 * D], F32R)
        w_1 = sb("w_1", [128, 2, KT, D], F32R)
        w_1t = sb("w_1t", [128, 2, KT, D], F32R)
        w_lr = sb("w_lr", [128, 2, KT, 2], F32R)
        bias_h = sb("bias_h", [33, 2, D + 2], F32R)
        bias_l = sb("bias_l", [33, 2, D + 2], F32R)
        bias = sb("bias", [128, 2, D + 2], F32R)
        ones2 = sb("ones2", [128, 2], F32R)
        ones33 = sb("ones33", [128, 33])
        blur_w = sb("blur_w", [TOK, 3, D])
        blur_end = sb("blur_end", [TOK, D])

        rows = sb("rows", [TOK, 2 * CH + 2, D])
        pool = sb("pool", [TOK, 2 * CH + 1, D])
        tap1 = sb("tap1", [TOK, CH, D])
        tap2 = sb("tap2", [TOK, CH, D])
        hbuf = sb("hbuf", [TOK, 3, CH, D])
        qbuf = sb("qbuf", [TOK, 3, CH, D])
        stats = sb("stats", [TOK, 2, 6])
        mv = sb("mv", [TOK, 2, 2])
        var_eps = sb("var_eps", [TOK, 2, 1])
        rstd = sb("rstd", [TOK, 2, 1])
        xn = sb("xn", [TOK, 2, D])
        xs = sb("xs", [TOK, 6, 2, D], F32R)
        x_t = sb("x_t", [128, 3, 2, KT, TP], F32R)
        sg0 = sb("sg0", [TOK, 2, D])
        s0 = sb("s0", [TOK, 2, D])
        m0 = sb("m0", [TOK, 2, D])
        f0 = sb("f0", [TOK, 4, D])
        x1 = sb("x1", [TOK, 2, D])
        x1s = sb("x1s", [TOK, 3, 2, D], F32R)
        x1_t = sb("x1_t", [128, 2, 2, KT, TP], F32R)
        u = sb("u", [TOK, 2, D])
        sg1 = sb("sg1", [TOK, 2, D + 2])
        s1 = sb("s1", [TOK, 2, D])
        mm1 = sb("mm1", [TOK, 2, D])
        f1 = sb("f1", [TOK, 2, D])
        diff = sb("diff", [TOK, 2, D])
        dz1 = sb("dz1", [TOK, 2, D])
        dz1s = sb("dz1s", [TOK, 2, 2, D], F32R)
        dz1_t = sb("dz1_t", [128, 2, 2, KT, TP], F32R)
        back = sb("back", [TOK, 2, D])
        dz0 = sb("dz0", [TOK, 2, D])
        dz0s = sb("dz0s", [TOK, 2, 2, D], F32R)
        g0_raw = sb("g0_raw", [128, KT, D])
        gb_col = sb("gb_col", [128, 8])
        gb_wide = sb("gb_wide", [128, 4, 33])
        mag = sb("mag", [128, KT * D])
        ratio = sb("ratio", [128, KT * D])
        stepped = sb("stepped", [128, KT * D])

        p_t = psum("p_t", [128, 512])
        p_kz = psum("p_kz", [128, 512])
        p_vq = psum("p_vq", [128, 512])
        p_z1 = psum("p_z1", [128, 512])
        p_dx = psum("p_dx", [128, 512])
        p_g0 = psum("p_g0", [128, 512])
        p_g1 = psum("p_g1", [128, 512])
        p_gb = psum("p_gb", [128, 512])

        loaded = sem("loaded")
        consts = sem("consts")
        eye_zero = sem("eye_zero")
        setup_t = sem("setup_t")
        setup_v = sem("setup_v")
        wk_t_done = sem("wk_t_done")
        kw0_filled = sem("kw0_filled")
        chain = sem("chain")
        x_loaded = sem("x_loaded")
        pooled = sem("pooled")
        tok_ops = sem("tok_ops")
        h_stored = [sem(f"h_stored{c}") for c in range(CHUNKS)]
        q_stored = [sem(f"q_stored{c}") for c in range(CHUNKS)]
        stats_ready = sem("stats_ready")
        mv_ready = sem("mv_ready")
        eps_added = sem("eps_added")
        rstd_ready = sem("rstd_ready")
        xn_ready = sem("xn_ready")
        xh_ready = sem("xh_ready")
        xl_ready = sem("xl_ready")
        xt_filled = sem("xt_filled")
        xt_ready = sem("xt_ready")
        kz_filled = sem("kz_filled")
        vq_filled = sem("vq_filled")
        sg0_ready = sem("sg0_ready")
        s0_ready = sem("s0_ready")
        x1_ready = sem("x1_ready")
        m0_ready = sem("m0_ready")
        f0_ready = sem("f0_ready")
        q_copied = sem("q_copied")
        u_ready = sem("u_ready")
        x1h_ready = sem("x1h_ready")
        x1l_ready = sem("x1l_ready")
        x1t_filled = sem("x1t_filled")
        x1t_ready = sem("x1t_ready")
        z1_filled = sem("z1_filled")
        sg1_ready = sem("sg1_ready")
        s1_ready = sem("s1_ready")
        m1_ready = sem("m1_ready")
        f1_ready = sem("f1_ready")
        diff_ready = sem("diff_ready")
        dz1_ready = sem("dz1_ready")
        dz1h_ready = sem("dz1h_ready")
        dz1l_ready = sem("dz1l_ready")
        dz1t_filled = sem("dz1t_filled")
        dz1t_ready = sem("dz1t_ready")
        dx_filled = sem("dx_filled")
        g1_added = sem("g1_added")
        back_ready = sem("back_ready")
        dz0_ready = sem("dz0_ready")
        dz0h_ready = sem("dz0h_ready")
        dz0l_ready = sem("dz0l_ready")
        g0_added = sem("g0_added")
        adam_v = sem("adam_v")
        adam_t = sem("adam_t")

        LOADS = 18

        def gradient_steps(engine, step):
            for t in range(NJ):
                step(Step(0, t))
            with engine.Fori(1, B) as b:
                for t in range(NJ):
                    step(Step(b, t))
            for t in range(GRAD0):
                step(Step(B, t))

        with nc.Block() as block:

            @block.sync
            def _(sp):
                for dst, src in ((raw_k, wk), (raw_q, wq), (raw_v, wv)):
                    sp.dma_start(dst[:, :, :], src.rearrange("(k p) n -> p k n", p=128)).then_inc(loaded, 16)
                for l in range(2):
                    sp.dma_start(raw_w[:, l], ws[l].rearrange("(k p) n -> p k n", p=128)).then_inc(loaded, 16)
                for c in range(2):
                    sp.dma_start(raw_lr[:, :, c:c + 1],
                                 wlr.rearrange("(k p) n -> p k n", p=128),
                                 allow_slow_non_contiguous=True).then_inc(loaded, 16)
                sp.wait_ge(consts, 1)
                for p in (0, 32):
                    for l in range(2):
                        sp.dma_start(raw_b[p:p + 1, l, 0:D], bs[l:l + 1, :]).then_inc(loaded, 16)
                    for c in range(2):
                        sp.dma_start(raw_b[p:p + 1, 1, D + c:D + c + 1],
                                     blr.rearrange("(a n) -> a n", a=1)).then_inc(loaded, 16)
                for c in range(3):
                    if c < 2:
                        sp.dma_start(blur_w[:, c, :], blur[c].broadcast_to([TOK, D])).then_inc(loaded, 16)
                    else:
                        sp.dma_start(blur_w[:, c, :], blur[c].broadcast_to([TOK, D])).then_inc(loaded, 16)
                        sp.dma_start(blur_end[0:TOK - 1, :],
                                     blur[c].broadcast_to([TOK - 1, D])).then_inc(loaded, 16)

                def load_rows(b, jc):
                    one = slice(b, b + 1) if isinstance(b, int) else bass.ds(b, 1)
                    src = x_rows[one].rearrange("a p n -> p (a n)")
                    if jc < CHUNKS - 1:
                        sp.dma_start(rows[:, :, :].rearrange("p r d -> p (r d)"),
                                     src[:, 8 * jc * D:(8 * jc + 10) * D]).then_inc(x_loaded, 16)
                        return
                    sp.dma_start(rows[:, 0:8, :].rearrange("p r d -> p (r d)"),
                                 src[:, 16 * D:24 * D]).then_inc(x_loaded, 16)
                    sp.dma_start(rows[0:TOK - 1, 8:10, :].rearrange("p r d -> p (r d)"),
                                 src[1:TOK, 0:2 * D]).then_inc(x_loaded, 16)
                    for r in (8, 9):
                        sp.dma_start(rows[TOK - 1:TOK, r, :],
                                     src[TOK - 1:TOK, 23 * D:24 * D]).then_inc(x_loaded, 16)

                def io_step(s):
                    b, t = s.b, s.t
                    one = slice(b, b + 1) if isinstance(b, int) else bass.ds(b, 1)
                    if t % CH == 0 and s.has(0):
                        if not (isinstance(b, int) and b == 0 and t == 0):
                            sp.wait_ge(pooled, b * CHUNKS + t // CH)
                        load_rows(b, t // CH)
                    for lag, buf, dram, ready, stored in ((STATS, hbuf, h_tok, tok_ops, h_stored),
                                                          (LAYER0 + 1, qbuf, q_tok, q_copied, q_stored)):
                        if s.part(lag) == 0 and s.has(lag) and lag == STATS:
                            c = s.chunk(lag)
                            sp.wait_ge(ready, b * (6 * CHUNKS) + 6 * (c + 1))
                            store(buf, dram, b, c, stored)
                        elif s.part(lag) == CH - 1 and s.has(lag) and lag != STATS:
                            c = s.chunk(lag)
                            sp.wait_ge(ready, s.n(lag))
                            store(buf, dram, b, c, stored)

                def store(buf, dram, b, c, stored):
                    bb = b if c >= 0 else b - 1
                    one = slice(bb, bb + 1) if isinstance(bb, int) else bass.ds(bb, 1)
                    c = c % CHUNKS
                    sp.dma_start(dram[one].rearrange("a p n -> p (a n)")[:, c * CH * D:(c + 1) * CH * D],
                                 buf[:, c, :, :].rearrange("p u d -> p (u d)")).then_inc(stored[c], 16)

                gradient_steps(sp, io_step)
                for stored in (*h_stored, *q_stored):
                    sp.wait_ge(stored, 16 * B)

            @block.gpsimd
            def _(po):
                po.memset(raw_b[:, :, :], 0.0)
                po.memset(blur_end[:, :], 0.0).then_inc(consts, 1)
                po.memset(eye[:, :], 0.0).then_inc(eye_zero, 1)
                po.memset(bias_on[:, :].bitcast(F32), 0.0)
                po.memset(bias[:, :, :].bitcast(F32), 0.0)
                po.memset(new_bias[:, :, :].bitcast(F32), 0.0)
                po.memset(ones2[:, :].bitcast(F32), 1.0)
                po.memset(ones33[:, :], 1.0)
                po.memset(minus_half[:, :], -0.5)
                po.memset(ln_eps[:, :], LN_EPS).then_inc(eye_zero, 1)
                po.wait_ge(eye_zero, 2)
                po.affine_select(out=eye[:, :], in_=eye[:, :], compare_op=ALU.not_equal, fill=1.0, base=0,
                                 pattern=[[-1, 128]], channel_multiplier=1).then_inc(consts, 1)
                po.wait_ge(consts, 2)
                po.wait_ge(loaded, 16 * (LOADS + 1))

                def tokenize(s):
                    c = s.t // CH
                    h = hbuf[:, c, :, :]

                    def tap(k, n=CH, at=0):
                        return pool[:, 2 * at + k:2 * (at + n - 1) + k + 1:2, :]

                    def w(ap, n):
                        return ap.unsqueeze(1).broadcast_to([TOK, n, D])

                    def done(k):
                        return s.b * (6 * CHUNKS) + (6 * c + k)

                    u_ = s.t % CH
                    if u_ == 0:
                        po.wait_ge(pooled, s.b * CHUNKS + (c + 1))
                        if s.has(NJ):
                            po.wait_ge(xn_ready, s.n(NJ - CH + 1))
                            po.wait_ge(h_stored[c], s.b * 16)
                        po.tensor_tensor(h, tap(0), w(blur_w[:, 0, :], CH), ALU.mult).then_inc(tok_ops, 1)
                        po.tensor_tensor(tap1[:, :, :], tap(1), w(blur_w[:, 1, :], CH),
                                         ALU.mult).then_inc(tok_ops, 1)
                    elif u_ == 1:
                        po.tensor_tensor(tap2[:, 0:CH - 1, :], tap(2, CH - 1), w(blur_w[:, 2, :], CH - 1),
                                         ALU.mult).then_inc(tok_ops, 1)
                        last = blur_end[:, :] if c == CHUNKS - 1 else blur_w[:, 2, :]
                        po.tensor_tensor(tap2[:, CH - 1:CH, :], tap(2, 1, CH - 1), w(last, 1),
                                         ALU.mult).then_inc(tok_ops, 1)
                    elif u_ == 2:
                        po.wait_ge(tok_ops, done(2))
                        po.tensor_tensor(h, h, tap1[:, :, :], ALU.add).then_inc(tok_ops, 1)
                    else:
                        po.wait_ge(tok_ops, done(5))
                        po.tensor_tensor(h, h, tap2[:, :, :], ALU.add).then_inc(tok_ops, 1)

                def step(s):
                    if s.has(GRAD0):
                        k = s.slot(GRAD0, 2)
                        po.wait_ge(dz0h_ready, s.n(GRAD0))
                        if s.has(GRAD0 + 2):
                            po.wait_ge(g0_added, s.n(GRAD0 + 2))
                        po.tensor_tensor(dz0s[:, k, LO, :], dz0[:, k, :], dz0s[:, k, HI, :],
                                         ALU.subtract).then_inc(dz0l_ready, 1)
                    if s.has(0):
                        tokenize(s)
                    if s.has(STATS):
                        k = s.slot(STATS, 2)
                        po.wait_ge(mv_ready, s.n(STATS))
                        po.tensor_tensor(var_eps[:, k, :], mv[:, k, 1:2], ln_eps[0:TOK, :],
                                         ALU.add).then_inc(eps_added, 1)
                        po.wait_ge(eps_added, s.n(STATS))
                        if s.has(STATS + 2):
                            po.wait_ge(xn_ready, s.n(STATS + 2))
                        po.tensor_tensor(rstd[:, k, :], var_eps[:, k, :], minus_half[0:TOK, 0:1],
                                         ALU.pow).then_inc(rstd_ready, 1)
                    if s.has(NORM):
                        k, r = s.slot(NORM, 2), s.slot(NORM, 6)
                        po.wait_ge(xh_ready, s.n(NORM))
                        po.tensor_tensor(xs[:, r, LO, :], xn[:, k, :], xs[:, r, HI, :],
                                         ALU.subtract).then_inc(xl_ready, 1)

                gradient_steps(po, step)

            @block.scalar
            def _(act):
                def step(s):
                    if s.has(LAYER1):
                        k = s.slot(LAYER1, 2)
                        act.wait_ge(z1_filled, s.n(LAYER1))
                        if s.has(LAYER1 + 2):
                            act.wait_ge(back_ready, s.n(LAYER1 + 2))
                        nc.scalar.activation(sg1[:, k, :], p_z1[0:TOK, 0:D + 2],
                                             ACT.Sigmoid).then_inc(sg1_ready, 1)
                    if s.has(X_T):
                        act.wait_ge(xt_filled, s.n(X_T))
                        if s.has(X_T + 3):
                            act.wait_ge(z1_filled, s.n(X_T + 3))
                        nc.scalar.copy(x_t[:, s.slot(X_T, 3)].rearrange("p h k t -> p (h k t)"),
                                       p_t[:, 0:4 * TP]).then_inc(xt_ready, 1)
                    if s.has(LAYER0):
                        act.wait_ge(kz_filled, s.n(LAYER0))
                        if s.has(LAYER0 + 2):
                            act.wait_ge(f0_ready, s.n(LAYER0 + 2))
                        nc.scalar.activation(sg0[:, s.slot(LAYER0, 2), :], p_kz[0:TOK, D:2 * D],
                                             ACT.Sigmoid).then_inc(sg0_ready, 1)
                    if s.has(LAYER1):
                        k = s.slot(LAYER1, 2)
                        act.wait_ge(dz1_ready, s.n(LAYER1))
                        if s.has(LAYER1 + 2):
                            act.wait_ge(g1_added, s.n(LAYER1 + 2))
                        nc.scalar.copy(dz1s[:, k, HI, :], dz1[:, k, :]).then_inc(dz1h_ready, 1)
                    if s.has(LAYER0):
                        k, r = s.slot(LAYER0, 2), s.slot(LAYER0, 3)
                        act.wait_ge(x1_ready, s.n(LAYER0))
                        if s.has(LAYER0 + 3):
                            act.wait_ge(g1_added, s.n(LAYER0 + 3))
                        nc.scalar.copy(x1s[:, r, HI, :], x1[:, k, :]).then_inc(x1h_ready, 1)
                        act.wait_ge(vq_filled, s.n(LAYER0))
                        c = s.chunk(LAYER0)
                        if s.part(LAYER0) == 0 and s.has(LAYER0 + NJ):
                            act.wait_ge(q_stored[c % CHUNKS], s.b * 16 + (0 if c >= 0 else -16))
                        nc.scalar.copy(qbuf[:, c % CHUNKS, s.part(LAYER0), :],
                                       p_vq[0:TOK, D:2 * D]).then_inc(q_copied, 1)
                    if s.has(LAYER1):
                        act.wait_ge(dz1t_filled, s.n(LAYER1))
                        if s.has(LAYER1 + 2):
                            act.wait_ge(dx_filled, s.n(LAYER1 + 2))
                        nc.scalar.copy(dz1_t[:, s.slot(LAYER1, 2)].rearrange("p h k t -> p (h k t)"),
                                       p_t[:, 0:4 * TP]).then_inc(dz1t_ready, 1)
                    if s.has(NORM):
                        act.wait_ge(xn_ready, s.n(NORM))
                        if s.has(NORM + 6):
                            act.wait_ge(g0_added, s.n(NORM + 6))
                        nc.scalar.copy(xs[:, s.slot(NORM, 6), HI, :],
                                       xn[:, s.slot(NORM, 2), :]).then_inc(xh_ready, 1)
                    if s.has(LAYER0):
                        act.wait_ge(x1t_filled, s.n(LAYER0))
                        if s.has(LAYER0 + 2):
                            act.wait_ge(z1_filled, s.n(LAYER0 + 2))
                        nc.scalar.copy(x1_t[:, s.slot(LAYER0, 2)].rearrange("p h k t -> p (h k t)"),
                                       p_t[:, 0:4 * TP]).then_inc(x1t_ready, 1)
                    if s.has(BACK1):
                        k = s.slot(BACK1, 2)
                        act.wait_ge(dz0_ready, s.n(BACK1))
                        if s.has(BACK1 + 2):
                            act.wait_ge(g0_added, s.n(BACK1 + 2))
                        nc.scalar.copy(dz0s[:, k, HI, :], dz0[:, k, :]).then_inc(dz0h_ready, 1)

                gradient_steps(act, step)

            @block.vector
            def _(dve):
                count = [0]

                def link(ins, s=chain):
                    count[0] += 1
                    ins.then_inc(s, 1)
                    dve.wait_ge(s, count[0])

                def split(high, low, src):
                    link(nc.vector.tensor_copy(high, src))
                    link(nc.vector.tensor_tensor(low, src, high, ALU.subtract))

                dve.wait_ge(loaded, 16 * (LOADS + 1))
                dve.wait_ge(consts, 2)
                link(nc.vector.tensor_copy(eye_r[:, :], eye[:, 0:TP]))
                for p in (0, 32):
                    link(nc.vector.memset(bias_on[p:p + 1, :].bitcast(F32), 1.0))
                dve.wait_ge(setup_t, 1)
                link(nc.vector.tensor_copy(wk_t[:, :, :].rearrange("p k n -> p (k n)"), p_kz[:, :]))
                dve.sem_inc(wk_t_done, 1)
                split(w_1t[:, HI].rearrange("p k n -> p (k n)"), w_1t[:, LO].rearrange("p k n -> p (k n)"),
                      p_vq[:, :])
                split(w_kz[:, HI, :, 0:D], w_kz[:, LO, :, 0:D], raw_k[:, :, :])
                split(w_vq[:, HI, :, 0:D], w_vq[:, LO, :, 0:D], raw_v[:, :, :])
                split(w_vq[:, HI, :, D:], w_vq[:, LO, :, D:], raw_q[:, :, :])
                split(w_1[:, HI], w_1[:, LO], raw_w[:, 1])
                split(w_lr[:, HI], w_lr[:, LO], raw_lr[:, :, :])
                split(bias_h[:, :, :], bias_l[:, :, :], raw_b[:, :, :])
                link(nc.vector.tensor_copy(bias[0:1], bias_h[0:1]))
                link(nc.vector.tensor_copy(bias[32:33], bias_l[32:33]))
                dve.wait_ge(kw0_filled, 1)
                split(w_kz[:, HI, :, D:], w_kz[:, LO, :, D:], p_z1[:, :].rearrange("p (k n) -> p k n", k=KT))
                dve.sem_inc(setup_v, 1)

                def step(s):
                    if s.has(LAYER1):
                        k = s.slot(LAYER1, 2)
                        a = sg1[:, k, D:D + 1]
                        dve.wait_ge(sg1_ready, s.n(LAYER1))
                        nc.vector.tensor_tensor(s1[:, k, :], p_z1[0:TOK, 0:D], sg1[:, k, 0:D],
                                                ALU.mult).then_inc(s1_ready, 1)
                        dve.wait_ge(s1_ready, s.n(LAYER1))
                        nc.vector.scalar_tensor_tensor(out=mm1[:, k, :], in0=sg1[:, k, 0:D], scalar=1.0,
                                                       in1=s1[:, k, :], op0=ALU.subtract,
                                                       op1=ALU.mult).then_inc(m1_ready, 1)
                        nc.vector.tensor_tensor(diff[:, k, :], u[:, k, :], s1[:, k, :],
                                                ALU.add).then_inc(diff_ready, 1)
                        dve.wait_ge(m1_ready, s.n(LAYER1))
                        nc.vector.tensor_tensor(f1[:, k, :], sg1[:, k, 0:D], mm1[:, k, :],
                                                ALU.subtract).then_inc(f1_ready, 1)
                        dve.wait_ge(f1_ready, s.n(LAYER1))
                        if s.has(LAYER1 + 2):
                            dve.wait_ge(dz1l_ready, s.n(LAYER1 + 2))
                        nc.vector.scalar_tensor_tensor(out=dz1[:, k, :], in0=diff[:, k, :], scalar=a,
                                                       in1=f1[:, k, :], op0=ALU.mult,
                                                       op1=ALU.mult).then_inc(dz1_ready, 1)
                    if s.has(LAYER0):
                        k = s.slot(LAYER0, 2)
                        dve.wait_ge(sg0_ready, s.n(LAYER0))
                        nc.vector.tensor_tensor(s0[:, k, :], p_kz[0:TOK, D:2 * D], sg0[:, k, :],
                                                ALU.mult).then_inc(s0_ready, 1)
                        dve.wait_ge(s0_ready, s.n(LAYER0))
                        if s.has(LAYER0 + 2):
                            dve.wait_ge(x1h_ready, s.n(LAYER0 + 2))
                        nc.vector.tensor_tensor(x1[:, k, :], p_kz[0:TOK, 0:D], s0[:, k, :],
                                                ALU.add).then_inc(x1_ready, 1)
                    if s.has(LAYER1):
                        k = s.slot(LAYER1, 2)
                        dve.wait_ge(dz1h_ready, s.n(LAYER1))
                        nc.vector.tensor_tensor(dz1s[:, k, LO, :], dz1[:, k, :], dz1s[:, k, HI, :],
                                                ALU.subtract).then_inc(dz1l_ready, 1)
                    if s.has(LAYER0):
                        k, r = s.slot(LAYER0, 2), s.slot(LAYER0, 3)
                        nc.vector.scalar_tensor_tensor(out=m0[:, k, :], in0=sg0[:, k, :], scalar=1.0,
                                                       in1=s0[:, k, :], op0=ALU.subtract,
                                                       op1=ALU.mult).then_inc(m0_ready, 1)
                        dve.wait_ge(x1h_ready, s.n(LAYER0))
                        nc.vector.tensor_tensor(x1s[:, r, LO, :], x1[:, k, :], x1s[:, r, HI, :],
                                                ALU.subtract).then_inc(x1l_ready, 1)
                        dve.wait_ge(m0_ready, s.n(LAYER0))
                        nc.vector.tensor_tensor(f0[:, s.slot(LAYER0, 4), :], sg0[:, k, :], m0[:, k, :],
                                                ALU.subtract).then_inc(f0_ready, 1)
                        dve.wait_ge(q_copied, s.n(LAYER0))
                        nc.vector.tensor_tensor(u[:, k, :], x1[:, k, :], p_vq[0:TOK, 0:D],
                                                ALU.subtract).then_inc(u_ready, 1)
                    if s.has(STATS):
                        k = s.slot(STATS, 2)
                        h = hbuf[:, s.chunk(STATS) % CHUNKS, s.part(STATS), :]
                        dve.wait_ge(tok_ops, s.b * (6 * CHUNKS) + 6 * (s.chunk(STATS) + 1))
                        nc.vector.bn_stats(stats[:, k, :], h).then_inc(stats_ready, 1)
                    if s.has(STATS):
                        dve.wait_ge(stats_ready, s.n(STATS))
                    if s.has(NORM):
                        k = s.slot(NORM, 2)
                        h = hbuf[:, s.chunk(NORM) % CHUNKS, s.part(NORM), :]
                        dve.wait_ge(rstd_ready, s.n(NORM))
                        if s.has(NORM + 2):
                            dve.wait_ge(xl_ready, s.n(NORM + 2))
                        nc.vector.tensor_scalar(xn[:, k, :], h, mv[:, k, 0:1], rstd[:, k, :],
                                                ALU.subtract, ALU.mult).then_inc(xn_ready, 1)
                    if s.has(STATS):
                        k = s.slot(STATS, 2)
                        nc.vector.bn_aggr(mv[:, k, :], stats[:, k, :]).then_inc(mv_ready, 1)
                    if s.has(0) and s.t % CH == 0:
                        c = s.t // CH
                        dve.wait_ge(x_loaded, s.b * 96 + 16 * (c + 1 if c < CHUNKS - 1 else c + 4))
                        if s.has(CH):
                            dve.wait_ge(tok_ops, s.b * (6 * CHUNKS) + (6 * (c - 1) + 4))
                        nc.vector.tensor_tensor(pool[:, :, :], rows[:, 0:2 * CH + 1, :],
                                                rows[:, 1:2 * CH + 2, :], ALU.max).then_inc(pooled, 1)
                    if s.has(BACK1):
                        k = s.slot(BACK1, 2)
                        dve.wait_ge(dx_filled, s.n(BACK1))
                        nc.vector.scalar_tensor_tensor(out=back[:, k, :], in0=diff[:, k, :],
                                                       scalar=sg1[:, k, D:D + 1], in1=p_dx[0:TOK, 0:D],
                                                       op0=ALU.mult, op1=ALU.add).then_inc(back_ready, 1)
                        dve.wait_ge(back_ready, s.n(BACK1))
                        if s.has(BACK1 + 2):
                            dve.wait_ge(dz0l_ready, s.n(BACK1 + 2))
                        nc.vector.tensor_tensor(dz0[:, k, :], back[:, k, :], f0[:, s.slot(BACK1, 4), :],
                                                ALU.mult).then_inc(dz0_ready, 1)

                gradient_steps(dve, step)

                count[0] = 0
                A = adam_v
                dve.wait_ge(g0_added, TILES)
                link(nc.vector.tensor_copy(g0_raw[:, :, :].rearrange("p k n -> p (k n)"), p_g0[:, :]), A)
                link(nc.vector.tensor_copy(gb_col[:, :], p_gb[:, 0:8]), A)
                for i in range(4):
                    link(nc.vector.tensor_scalar(gb_wide[:, i, :], ones33[:, :], gb_col[:, 2 * i:2 * i + 1],
                                                 None, ALU.mult), A)

                def adam(g, p, rows_=128, two=None):
                    mag_, ratio_, new = (t[0:rows_, :] if two is None else
                                         t[0:rows_, :].rearrange("p (l n) -> p l n", l=two)
                                         for t in (mag, ratio, stepped))
                    link(nc.vector.tensor_scalar(ratio_, g, GRAD_SCALE, None, ALU.mult), A)
                    link(nc.vector.scalar_tensor_tensor(out=mag_, in0=ratio_, scalar=-1.0, in1=ratio_,
                                                        op0=ALU.mult, op1=ALU.max), A)
                    link(nc.vector.tensor_scalar(mag_, mag_, ADAM_EPS, None, ALU.add), A)
                    link(nc.vector.reciprocal(mag_, mag_), A)
                    link(nc.vector.scalar_tensor_tensor(out=ratio_, in0=ratio_, scalar=LR, in1=mag_,
                                                        op0=ALU.mult, op1=ALU.mult), A)
                    link(nc.vector.scalar_tensor_tensor(out=new, in0=p, scalar=1.0 - LR * WD, in1=ratio_,
                                                        op0=ALU.mult, op1=ALU.subtract), A)
                    return new

                for l, grad in ((1, p_g1), (0, p_kz)):
                    if l == 0:
                        dve.wait_ge(adam_t, 1)
                    new = adam(grad[:, :], raw_w[:, l].rearrange("p k n -> p (k n)"))
                    src = new.rearrange("p (k n) -> p k n", k=KT)
                    link(nc.vector.tensor_copy(new_w[:, l, HI], src), A)
                    link(nc.vector.tensor_tensor(new_w[:, l, LO], src, new_w[:, l, HI], ALU.subtract), A)
                dve.wait_ge(adam_t, 2)
                new = adam(p_vq[0:33, :].rearrange("p (l n) -> p l n", l=2), raw_b[:, :, 0:D], 33, 2)
                nb_h, nb_l = bias_h[:, :, 0:D], bias_l[:, :, 0:D]
                link(nc.vector.tensor_copy(nb_h, new), A)
                link(nc.vector.tensor_tensor(nb_l, new, nb_h, ALU.subtract), A)
                link(nc.vector.tensor_copy(new_bias[0:1], nb_h[0:1]), A)
                link(nc.vector.tensor_copy(new_bias[32:33], nb_l[32:33]), A)

            @block.tensor
            def _(pe):
                mm = nc.tensor.matmul

                pe.wait_ge(loaded, 16 * (LOADS + 1))
                pe.wait_ge(consts, 2)
                for dst, src in ((p_kz, raw_k), (p_vq, raw_w[:, 1])):
                    for k in range(KT):
                        for m in range(KT):
                            last = nc.tensor.transpose(dst[:, m * D + k * 128:m * D + (k + 1) * 128],
                                                       src[:, k, m * 128:(m + 1) * 128], eye[:, :])
                last.then_inc(setup_t, 1)
                pe.wait_ge(wk_t_done, 1)
                for m in range(KT):
                    for k in range(KT):
                        last = mm(p_z1[:, m * D:(m + 1) * D], wk_t[:, k, m * 128:(m + 1) * 128],
                                  raw_w[:, 0, k, :], start=(k == 0), stop=(k == KT - 1))
                last.then_inc(kw0_filled, 1)
                pe.wait_ge(setup_v, 1)

                def product(dst, left, right, start=True, stop=True):
                    n = 0
                    for k in range(KT):
                        for h, g in ((HI, HI), (HI, LO), (LO, HI)):
                            n += 1
                            last = mm(dst, left(h, k), right(g, k), start=start and n == 1,
                                      stop=stop and n == 3 * KT, skip_group_check=True)
                    return last

                def transposes(src):
                    for h in (HI, LO):
                        for k in range(KT):
                            at = (h * KT + k) * TP
                            last = mm(p_t[:, at:at + TP], src[:, h, k * 128:(k + 1) * 128],
                                      eye_r[0:TOK, :], start=True, stop=True, skip_group_check=True)
                    return last

                def gradient(dst, left, right, col, first, first_col):
                    n = 0
                    for m in range(KT):
                        for h, g in ((HI, HI), (HI, LO), (LO, HI)):
                            mm(dst[:, m * D:(m + 1) * D], left[:, h, m * 128:(m + 1) * 128],
                               right[:, g, :], start=first and n == 0, stop=True, skip_group_check=True)
                            n += 1
                    n = 0
                    for m in range(KT):
                        for h in (HI, LO):
                            c = col + 2 * m
                            last = mm(p_gb[:, c:c + 2], right[:, h, m * 128:(m + 1) * 128],
                                      ones2[0:TOK, :], start=first_col and n == 0, stop=True,
                                      skip_group_check=True)
                            n += 1
                    return last

                def step(s):
                    known = isinstance(s.b, int)
                    if s.has(LAYER1):
                        pe.wait_ge(x1t_ready, s.n(LAYER1))
                        if s.has(LAYER1 + 1):
                            pe.wait_ge(s1_ready, s.n(LAYER1 + 1))
                        xt, x1t = x_t[:, s.slot(LAYER1, 3)], x1_t[:, s.slot(LAYER1, 2)]
                        product(p_z1[0:TOK, 0:D], lambda h, k: x1t[:, h, k, 0:TOK],
                                lambda h, k: w_1[:, h, k, :], stop=False)
                        product(p_z1[0:TOK, D:D + 2], lambda h, k: xt[:, h, k, 0:TOK],
                                lambda h, k: w_lr[:, h, k, :], start=False, stop=False)
                        mm(p_z1[0:TOK, 0:D + 2], bias_on[:, :], bias[:, 1, :], start=False, stop=True,
                           skip_group_check=True).then_inc(z1_filled, 1)
                    if s.has(X_T):
                        pe.wait_ge(xl_ready, s.n(X_T))
                        if s.has(X_T + 1):
                            pe.wait_ge(xt_ready, s.n(X_T + 1))
                        if s.has(LAYER0 + 1):
                            pe.wait_ge(x1t_ready, s.n(LAYER0 + 1))
                        transposes(xs[:, s.slot(X_T, 6)]).then_inc(xt_filled, 1)
                    if s.has(LAYER0):
                        xt = x_t[:, s.slot(LAYER0, 3)]
                        pe.wait_ge(xt_ready, s.n(LAYER0))
                        if s.has(LAYER0 + 1):
                            pe.wait_ge(x1_ready, s.n(LAYER0 + 1))
                        product(p_kz[0:TOK, :], lambda h, k: xt[:, h, k, 0:TOK],
                                lambda h, k: w_kz[:, h, k, :], stop=False)
                        mm(p_kz[0:TOK, D:2 * D], bias_on[:, :], bias[:, 0, 0:D], start=False, stop=True,
                           skip_group_check=True).then_inc(kz_filled, 1)
                        if s.has(LAYER0 + 1):
                            pe.wait_ge(u_ready, s.n(LAYER0 + 1))
                        product(p_vq[0:TOK, :], lambda h, k: xt[:, h, k, 0:TOK],
                                lambda h, k: w_vq[:, h, k, :]).then_inc(vq_filled, 1)
                    if s.has(LAYER1):
                        pe.wait_ge(dz1l_ready, s.n(LAYER1))
                        if s.has(X_T):
                            pe.wait_ge(xt_ready, s.n(X_T))
                        else:
                            pe.wait_ge(x1t_ready, s.n(LAYER1))
                        transposes(dz1s[:, s.slot(LAYER1, 2)]).then_inc(dz1t_filled, 1)
                    if s.has(BACK1):
                        dt = dz1_t[:, s.slot(BACK1, 2)]
                        pe.wait_ge(dz1t_ready, s.n(BACK1))
                        if s.has(BACK1 + 1):
                            pe.wait_ge(back_ready, s.n(BACK1 + 1))
                        product(p_dx[0:TOK, 0:D], lambda h, k: dt[:, h, k, 0:TOK],
                                lambda h, k: w_1t[:, h, k, :]).then_inc(dx_filled, 1)
                        first = known and s.b * NJ + s.t == BACK1
                        gradient(p_g1, x1s[:, s.slot(BACK1, 3)], dz1s[:, s.slot(BACK1, 2)], 4,
                                 first, first).then_inc(g1_added, 1)
                    if s.has(LAYER0):
                        pe.wait_ge(x1l_ready, s.n(LAYER0))
                        if s.has(LAYER1):
                            pe.wait_ge(dz1t_ready, s.n(LAYER1))
                        elif s.has(X_T):
                            pe.wait_ge(xt_ready, s.n(X_T))
                        transposes(x1s[:, s.slot(LAYER0, 3)]).then_inc(x1t_filled, 1)
                    if s.has(GRAD0):
                        pe.wait_ge(dz0l_ready, s.n(GRAD0))
                        gradient(p_g0, xs[:, s.slot(GRAD0, 6)], dz0s[:, s.slot(GRAD0, 2)], 0,
                                 known and s.b * NJ + s.t == GRAD0, False).then_inc(g0_added, 1)

                gradient_steps(pe, step)

                pe.wait_ge(adam_v, 1)
                for m in range(KT):
                    for k in range(KT):
                        last = mm(p_kz[:, m * D:(m + 1) * D], raw_k[:, k, m * 128:(m + 1) * 128],
                                  g0_raw[:, k, :], start=(k == 0), stop=(k == KT - 1))
                last.then_inc(adam_t, 1)
                pe.wait_ge(adam_v, 6)
                for i in range(4):
                    last = mm(p_vq[0:33, i * 128:(i + 1) * 128], gb_wide[:, i, :], eye[:, :],
                              start=True, stop=True)
                last.then_inc(adam_t, 1)


def expert_weights(nc, w1, b1, g1, be1, m1, v1, w2, b2, g2, be2, m2, v2, wo, s_dram,
                   ffn_w, ffn_bias, eye, minus_half):
    RING = 4
    with ExitStack() as ctx:
        def sb(name, shape, dt=F32):
            return ctx.enter_context(nc.sbuf_tensor(name, shape, dt))

        def sem(name):
            return ctx.enter_context(nc.semaphore(name))

        par = sb("par", [KT * E, 2, 5, 128])
        bn_eps = sb("bn_eps", [KT * E, 128])
        scale = sb("scale", [KT * E, 2, 128])
        shift = sb("shift", [KT * E, 2, 128])
        scale_b = sb("scale_b", [128, 2, E, D])
        staged = sb("staged", [128, RING, KT, D])
        scaled = sb("scaled", [128, 2, KT, D])
        p_b = ctx.enter_context(nc.psum_tensor("p_b", [128, 2, KT * E], F32))

        par_loaded = sem("par_loaded")
        eps_set = sem("eps_set")
        pow_done = sem("pow_done")
        bn_v = sem("bn_v")
        bias_t = sem("bias_t")
        s_stored = sem("s_stored")
        s_loaded = sem("s_loaded")
        w_loaded = [sem(f"w_loaded{i}") for i in range(RING)]
        w_scaled = sem("w_scaled")
        w_high = sem("w_high")
        w_low = sem("w_low")
        jobs = [(i, e) for e in range(E) for i in range(3)]
        scales = [n for n, (i, e) in enumerate(jobs) if i < 2]

        def scaled_by(n):
            return sum(m <= n for m in scales)

        def source(n):
            return scaled[:, scales.index(n) % 2] if n in scales else staged[:, n % RING]

        with nc.Block() as block:
            @block.sync
            def _(sp):
                for l, arrays in enumerate(((g1, v1, b1, m1, be1), (g2, v2, b2, m2, be2))):
                    for i, a in enumerate(arrays):
                        sp.dma_start(par[:, l, i, :],
                                     a.rearrange("e (m p) -> (e m) p", p=128)).then_inc(par_loaded, 16)
                for n, (i, e) in enumerate(jobs):
                    if n == 1:
                        sp.wait_ge(bn_v, 4)
                        for l in range(2):
                            sp.dma_start(s_dram[l].rearrange("(r p) -> r p", p=128),
                                         scale[:, l, :]).then_inc(s_stored, 16)
                        sp.wait_ge(s_stored, 32)
                        for l in range(2):
                            sp.dma_start(scale_b[:, l].rearrange("p e n -> p (e n)"),
                                         s_dram[l:l + 1].broadcast_to([128, E * D])).then_inc(s_loaded, 16)
                    if n >= RING:
                        m = n - RING
                        if m in scales:
                            sp.wait_ge(w_scaled, scaled_by(m))
                        else:
                            sp.wait_ge(w_low, m + 1)
                    src = (w1, w2, wo)[i][e].rearrange("(k p) n -> p k n", p=128)
                    sp.dma_start(staged[:, n % RING], src).then_inc(w_loaded[n % RING], 16)

            @block.gpsimd
            def _(po):
                po.memset(bn_eps[:, :], BN_EPS).then_inc(eps_set, 1)
                for l in range(2):
                    po.wait_ge(bn_v, 2 * l + 1)
                    po.tensor_tensor(scale[:, l, :], par[:, l, 1, :], minus_half[0:KT * E, :],
                                     ALU.pow).then_inc(pow_done, 1)

            @block.vector
            def _(dve):
                count = [0]

                def link(ins):
                    count[0] += 1
                    ins.then_inc(bn_v, 1)
                    dve.wait_ge(bn_v, count[0])

                dve.wait_ge(par_loaded, 160)
                dve.wait_ge(eps_set, 1)
                for l in range(2):
                    link(nc.vector.tensor_tensor(par[:, l, 1, :], par[:, l, 1, :], bn_eps[:, :], ALU.add))
                    dve.wait_ge(pow_done, l + 1)
                    link(nc.vector.tensor_tensor(scale[:, l, :], scale[:, l, :], par[:, l, 0, :], ALU.mult))
                for l in range(2):
                    link(nc.vector.tensor_tensor(shift[:, l, :], par[:, l, 2, :], par[:, l, 3, :],
                                                 ALU.subtract))
                    link(nc.vector.tensor_tensor(shift[:, l, :], shift[:, l, :], scale[:, l, :], ALU.mult))
                    link(nc.vector.tensor_tensor(shift[:, l, :], shift[:, l, :], par[:, l, 4, :], ALU.add))
                dve.wait_ge(bias_t, 1)
                link(nc.vector.tensor_copy(ffn_bias[:, :, :], p_b[:, :, :]))
                dve.wait_ge(s_loaded, 32)

                def low(n):
                    i, e = jobs[n]
                    dve.wait_ge(w_high, n + 1)
                    nc.vector.tensor_tensor(ffn_w[i][:, e, LO], source(n), ffn_w[i][:, e, HI],
                                            ALU.subtract).then_inc(w_low, 1)

                for n, (i, e) in enumerate(jobs):
                    if i < 2:
                        s = scaled_by(n)
                        dve.wait_ge(w_loaded[n % RING], 16 * (n // RING + 1))
                        if s > 2:
                            dve.wait_ge(w_low, scales[s - 3] + 1)
                        nc.vector.tensor_tensor(scaled[:, (s - 1) % 2], staged[:, n % RING],
                                                scale_b[:, i, e, :].unsqueeze(1).broadcast_to([128, KT, D]),
                                                ALU.mult).then_inc(w_scaled, 1)
                    if n >= 1:
                        low(n - 1)
                low(len(jobs) - 1)

            @block.scalar
            def _(act):
                for n, (i, e) in enumerate(jobs):
                    if i < 2:
                        act.wait_ge(w_scaled, scaled_by(n))
                    else:
                        act.wait_ge(w_loaded[n % RING], 16 * (n // RING + 1))
                    nc.scalar.copy(ffn_w[i][:, e, HI], source(n)).then_inc(w_high, 1)

            @block.tensor
            def _(pe):
                pe.wait_ge(bn_v, 10)
                for l in range(2):
                    last = nc.tensor.transpose(p_b[:, l, :], shift[:, l, :], eye[0:KT * E, 0:KT * E])
                last.then_inc(bias_t, 1)


def block_sweep(nc, wr, br, bo, h_dram, q_dram, out, ffn_w, ffn_bias,
                eye, eye_r, bias_on, new_w, new_bias, minus_half, ln_eps):
    h_j = h_dram.rearrange("b (p j) d -> b j p d", j=NJ)
    q_j = q_dram.rearrange("b (p j) d -> b j p d", j=NJ)
    out_j = out.rearrange("b (p j) d -> j p b d", j=NJ)

    with ExitStack() as ctx:
        def sb(name, shape, dt=F32):
            return ctx.enter_context(nc.sbuf_tensor(name, shape, dt))

        def psum(name, shape):
            return ctx.enter_context(nc.psum_tensor(name, shape, F32))

        def sem(name):
            return ctx.enter_context(nc.semaphore(name))

        xt_new = sb("xt_new", [128, 2, KT, B, TOK], F32R)
        xt_use = sb("xt_use", [128, 2, KT, B, TOK], F32R)
        h1f = sb("h1f", [128, KT, NTOK])
        h1s = sb("h1s", [128, 2, KT, NTOK], F32R)
        h2f = sb("h2f", [128, KT, NTOK])
        h2s = sb("h2s", [128, 2, KT, NTOK], F32R)
        res = sb("res", [TOK, B, D])
        acc = sb("acc", [TOK, B, D])
        yb = sb("yb", [TOK, D])
        qin = sb("qin", [TOK, 4, D])
        hin = sb("hin", [TOK, 4, D])
        qs = sb("qs", [TOK, 2, D], F32R)
        q_t = sb("q_t", [128, 2, KT, TP], F32R)
        rsg = sb("rsg", [TOK, 2, D])
        rs = sb("rs", [TOK, D])
        q1 = sb("q1", [TOK, 3, D])
        q1s = sb("q1s", [TOK, 2, D], F32R)
        q1_t = sb("q1_t", [128, 2, KT, TP], F32R)
        xn2 = sb("xn2", [TOK, D])
        xn2s = sb("xn2s", [TOK, 2, D], F32R)
        stats = sb("stats2", [TOK, 6])
        mv = sb("mv2", [TOK, 2, 2])
        var_eps = sb("var_eps2", [TOK, 1])
        rstd = sb("rstd2", [TOK, 2, 1])
        raw_r = sb("raw_r", [128, KT, E])
        w_r = sb("w_r", [128, 2, KT, E], F32R)
        br_b = sb("br_b", [TOK, E])
        bo_s = sb("bo_s", [E, D])
        logit = sb("logit", [TOK, E])
        top = sb("top", [TOK, 1])
        sig = sb("sig", [TOK, 2, E])
        total = sb("total", [TOK, 1])
        gate_new = sb("gate_new", [TOK, E])
        gate = sb("gate", [TOK, E])
        gate_t = sb("gate_t", [E, TOK])

        p_1 = [psum(f"p_1{m}", [128, 512]) for m in range(KT)]
        p_2 = [psum(f"p_2{m}", [128, 512]) for m in range(KT)]
        p_3 = [psum(f"p_3{m}", [128, 2, D]) for m in range(2)]
        p_t = psum("p_t2", [128, 512])
        p_z = psum("p_z", [128, 512])

        const_loaded = sem("const_loaded")
        const_v = sem("const_v")
        q_loaded = [sem(f"q_loaded{i}") for i in range(4)]
        h_loaded = [sem(f"h_loaded{i}") for i in range(4)]
        qh_ready = sem("qh_ready")
        ql_ready = sem("ql_ready")
        qt_filled = sem("qt_filled")
        qt_ready = sem("qt_ready")
        za_filled = sem("za_filled")
        sga_ready = sem("sga_ready")
        sa_ready = sem("sa_ready")
        q1_ready = sem("q1_ready")
        q1h_ready = sem("q1h_ready")
        q1l_ready = sem("q1l_ready")
        q1t_filled = sem("q1t_filled")
        q1t_ready = sem("q1t_ready")
        zb_filled = sem("zb_filled")
        sgb_ready = sem("sgb_ready")
        sb_ready = sem("sb_ready")
        r_ready = sem("r_ready")
        res_ready = sem("res_ready")
        stat_ready = sem("stat_ready")
        mv_ready = sem("mv2_ready")
        eps_added = sem("eps2_added")
        rstd_ready = sem("rstd2_ready")
        xn_ready = sem("xn2_ready")
        xnh_ready = sem("xn2h_ready")
        xnl_ready = sem("xn2l_ready")
        xt_filled = sem("xt2_filled")
        xt_ready = sem("xt2_ready")
        logits_filled = sem("logits_filled")
        soft_v = sem("soft_v")
        sig_ready = sem("sig_ready")
        gate_t_filled = sem("gate_t_filled")
        yb_filled = sem("yb_filled")
        yb_ready = sem("yb_ready")
        gate_ready = sem("gate_ready")
        acc_ready = sem("acc_ready")
        copied = [sem(f"copied{g}") for g in range(2)]
        l1_filled = sem("l1_filled")
        h1h_ready = sem("h1h_ready")
        h1l_ready = sem("h1l_ready")
        l2_filled = sem("l2_filled")
        h2h_ready = sem("h2h_ready")
        h2l_ready = sem("h2l_ready")
        l3_filled = sem("l3_filled")
        mixed = sem("mixed")
        out_stored = [sem(f"out_stored{g}") for g in range(2)]

        SOFT = 8

        def macros(engine, step):
            for J in (0, 1):
                for n in range(16):
                    step(Pace(J, n))
            with engine.Fori(2, NJ) as J:
                for n in range(16):
                    step(Pace(J, n))
            for n in range(16):
                step(Pace(NJ, n))
            for n in range(2):
                step(Pace(NJ + 1, n))

        def retrieves(s):
            return not isinstance(s.J, int) or s.J < NJ

        def col(J, shift):
            j = J + shift
            return slice(j, j + 1) if isinstance(j, int) else bass.ds(j, 1)

        with nc.Block() as block:
            @block.sync
            def _(sp):
                sp.dma_start(raw_r[:, :, :], wr.rearrange("(k p) n -> p k n", p=128)).then_inc(const_loaded, 16)
                sp.dma_start(br_b[:, :], br.rearrange("(a n) -> a n", a=1).broadcast_to([TOK, E])).then_inc(const_loaded, 16)
                sp.dma_start(bo_s[:, :], bo).then_inc(const_loaded, 16)

                def load(s, b):
                    if s.has_m(b - 4):
                        sp.wait_ge(q1_ready, s.m(b - 4))
                    sp.dma_start(qin[:, b % 4, :], q_j[b, col(s.J, 0)].rearrange("a p d -> p (a d)")
                                 ).then_inc(q_loaded[b % 4], 16)
                    if s.has_m(b - 4):
                        sp.wait_ge(res_ready, s.m(b - 4))
                    sp.dma_start(hin[:, b % 4, :], h_j[b, col(s.J, 0)].rearrange("a p d -> p (a d)")
                                 ).then_inc(h_loaded[b % 4], 16)

                def hand_over(s, g):
                    sp.wait_ge(xt_ready, s.m(GRP * g + GRP - 1))
                    if s.has():
                        sp.wait_ge(l1_filled, Pace(s.J, 8 * g + 7).n(0, 2))
                    at = slice(GRP * g, GRP * g + GRP)
                    sp.dma_start(xt_use[:, :, :, at, :].rearrange("p h k b t -> p (h k) (b t)").bitcast(F32),
                                 xt_new[:, :, :, at, :].rearrange("p h k b t -> p (h k) (b t)").bitcast(F32)
                                 ).then_inc(copied[g], 16)

                def store(s, g, shift):
                    sp.wait_ge(mixed, s.n(2, 4))
                    sp.dma_start(out_j[col(s.J, shift), :, GRP * g:GRP * g + GRP, :].rearrange("a p b d -> p (a b) d"),
                                 acc[:, GRP * g:GRP * g + GRP, :]).then_inc(out_stored[g], 16)

                def step(s):
                    if retrieves(s) and s.i < B:
                        load(s, s.i)
                    if s.i == 1 and s.has(2):
                        store(s, 1, -2)
                    if retrieves(s) and s.i == 8:
                        hand_over(s, 0)
                    if s.i == 9 and s.has(2):
                        store(s, 0, -1)
                    if retrieves(s) and s.i == 15:
                        hand_over(s, 1)

                macros(sp, step)
                for g in range(2):
                    sp.wait_ge(out_stored[g], 16 * NJ)

            @block.gpsimd
            def _(po):
                def step(s):
                    if s.has() and s.i < B:
                        b = s.i
                        if b == 0:
                            po.wait_ge(yb_ready, s.J)
                        g = b // GRP
                        if b % GRP == 0 and s.has(16):
                            po.wait_ge(out_stored[g], s.J * 16 - 16)
                        po.tensor_tensor(acc[:, b, :], res[:, b, :], yb[:, :], ALU.add).then_inc(acc_ready, 1)
                    b = s.tile(4)
                    if b is not None:
                        po.wait_ge(mv_ready, s.m(b))
                        po.tensor_tensor(var_eps[:, :], mv[:, b % 2, 1:2], ln_eps[0:TOK, :],
                                         ALU.add).then_inc(eps_added, 1)
                        po.wait_ge(eps_added, s.m(b))
                        if s.has_m(b - 2):
                            po.wait_ge(xn_ready, s.m(b - 2))
                        po.tensor_tensor(rstd[:, b % 2, :], var_eps[:, :], minus_half[0:TOK, 0:1],
                                         ALU.pow).then_inc(rstd_ready, 1)

                macros(po, step)

            @block.scalar
            def _(act):
                def evacuate(dst, bank, filled, ready):
                    pass

                def relu(s, lag, bank, layer, full, parts, filled, reader, low, high):
                    for m in range(KT):
                        c = m + KT * s.expert(lag)
                        bias = ffn_bias[:, layer, c:c + 1]
                        act.wait_ge(filled, s.n(lag, 2) - (KT - 1 - m))
                        if s.has(lag + 1):
                            act.wait_ge(low, s.n(lag + 1, 2) - (KT - 1 - m))
                        nc.scalar.activation(full[:, m, :], bank[m][:, 0:NTOK], ACT.Relu, bias=bias)
                        if m == 0 and s.has(lag + 1):
                            act.wait_ge(*reader)
                        nc.scalar.activation(parts[:, HI, m, :], bank[m][:, 0:NTOK], ACT.Relu,
                                             bias=bias).then_inc(high, 1)

                def step(s):
                    b = s.tile(2)
                    if b is not None:
                        act.wait_ge(za_filled, s.m(b))
                        if s.has_m(b - 1):
                            act.wait_ge(sa_ready, s.m(b - 1))
                        nc.scalar.activation(rsg[:, 0, :], p_z[0:TOK, 0:D], ACT.Sigmoid).then_inc(sga_ready, 1)
                    b = s.tile(1)
                    if b is not None:
                        act.wait_ge(qt_filled, s.m(b))
                        if s.has_m(b - 1):
                            act.wait_ge(za_filled, s.m(b - 1))
                        nc.scalar.copy(q_t[:, :, :, :].rearrange("p h k t -> p (h k t)"),
                                       p_t[:, 0:4 * TP]).then_inc(qt_ready, 1)
                    b = s.tile(0)
                    if b is not None:
                        act.wait_ge(q_loaded[b % 4], s.J * 32 + 16 * (b // 4 + 1))
                        if s.has_m(b - 1):
                            act.wait_ge(qt_filled, s.m(b - 1))
                        nc.scalar.copy(qs[:, HI, :], qin[:, b % 4, :]).then_inc(qh_ready, 1)
                    if s.has(1):
                        relu(s, 1, p_2, 1, h2f, h2s, l2_filled, (l3_filled, s.n(2, 2)), h2l_ready, h2h_ready)
                    b = s.tile(4)
                    if b is not None:
                        act.wait_ge(zb_filled, s.m(b))
                        if s.has_m(b - 1):
                            act.wait_ge(sb_ready, s.m(b - 1))
                        nc.scalar.activation(rsg[:, 1, :], p_z[0:TOK, 0:D], ACT.Sigmoid).then_inc(sgb_ready, 1)
                    b = s.tile(3)
                    if b is not None:
                        act.wait_ge(q1t_filled, s.m(b))
                        if s.has_m(b - 1):
                            act.wait_ge(zb_filled, s.m(b - 1))
                        nc.scalar.copy(q1_t[:, :, :, :].rearrange("p h k t -> p (h k t)"),
                                       p_t[:, 0:4 * TP]).then_inc(q1t_ready, 1)
                    b = s.tile(2)
                    if b is not None:
                        act.wait_ge(q1_ready, s.m(b))
                        if s.has_m(b - 1):
                            act.wait_ge(q1t_filled, s.m(b - 1))
                        nc.scalar.copy(q1s[:, HI, :], q1[:, b % 3, :]).then_inc(q1h_ready, 1)
                    if s.has(0):
                        relu(s, 0, p_1, 0, h1f, h1s, l1_filled, (l2_filled, s.n(1, 2)), h1l_ready, h1h_ready)
                    b = s.tile(5)
                    if b is not None:
                        act.wait_ge(xn_ready, s.m(b))
                        if s.has_m(b - 1):
                            act.wait_ge(xt_filled, s.m(b - 1))
                        nc.scalar.copy(xn2s[:, HI, :], xn2[:, :]).then_inc(xnh_ready, 1)
                        act.wait_ge(xt_filled, s.m(b))
                        if b % GRP == 0 and s.has_m(b - 8):
                            act.wait_ge(copied[b // GRP], s.J * 16)
                        if b == 0 and s.has_m(b - 8):
                            act.wait_ge(logits_filled, s.J)
                        nc.scalar.copy(xt_new[:, :, :, b, :].rearrange("p h k t -> p (h k) t"),
                                       p_t[:, 0:4 * TP].rearrange("p (c t) -> p c t", t=TP)[:, :, 0:TOK]
                                       ).then_inc(xt_ready, 1)
                    if retrieves(s) and s.i == 14:
                        act.wait_ge(soft_v, s.J * SOFT + 3)
                        nc.scalar.activation(sig[:, 0, :], logit[:, :], ACT.Sigmoid)
                        nc.scalar.activation(sig[:, 1, :], logit[:, :], ACT.Sigmoid,
                                             scale=-1.0).then_inc(sig_ready, 1)

                macros(act, step)

            @block.vector
            def _(dve):
                dve.wait_ge(const_loaded, 48)
                nc.vector.tensor_copy(w_r[:, HI], raw_r[:, :, :]).then_inc(const_v, 1)
                dve.wait_ge(const_v, 1)
                nc.vector.tensor_tensor(w_r[:, LO], raw_r[:, :, :], w_r[:, HI], ALU.subtract).then_inc(const_v, 1)

                def mix(s, half):
                    e, g = s.expert(2), s.group(2)
                    dve.wait_ge(l3_filled, s.n(2, 2) - (1 - half))
                    for t in range(2):
                        b = GRP * g + 2 * half + t
                        if e == 0:
                            dve.wait_ge(acc_ready, s.J * B + (b + 1 - B - (B if s.i < 2 else 0)))
                        else:
                            dve.wait_ge(mixed, s.n(3, 4) - (3 - 2 * half - t))
                        nc.vector.scalar_tensor_tensor(out=acc[:, b, :], in0=p_3[half][0:TOK, t, :],
                                                       scalar=gate[:, e:e + 1], in1=acc[:, b, :],
                                                       op0=ALU.mult, op1=ALU.add).then_inc(mixed, 1)

                def low(s, lag, full, parts, high, low_):
                    for m in range(KT):
                        dve.wait_ge(high, s.n(lag, 2) - (KT - 1 - m))
                        nc.vector.tensor_tensor(parts[:, LO, m, :], full[:, m, :], parts[:, HI, m, :],
                                                ALU.subtract).then_inc(low_, 1)

                def soft(k, s, ins):
                    ins.then_inc(soft_v, 1)
                    dve.wait_ge(soft_v, s.J * SOFT + k)

                def step(s):
                    if s.has(2) and s.i == 2:
                        dve.wait_ge(soft_v, s.J * SOFT)
                        if s.has(3):
                            dve.wait_ge(mixed, s.n(3, 4))
                        nc.vector.tensor_copy(gate[:, :], gate_new[:, :]).then_inc(gate_ready, 1)
                        dve.wait_ge(gate_ready, s.J)
                    if s.has(2):
                        mix(s, 0)
                    b = s.tile(2)
                    if b is not None:
                        if s.has_m(max(b - 3, -1)):
                            dve.wait_ge(r_ready, s.m(max(b - 3, -1)))
                        dve.wait_ge(sga_ready, s.m(b))
                        nc.vector.tensor_tensor(rs[:, :], p_z[0:TOK, 0:D], rsg[:, 0, :],
                                                ALU.mult).then_inc(sa_ready, 1)
                        dve.wait_ge(sa_ready, s.m(b))
                        nc.vector.tensor_tensor(q1[:, b % 3, :], qin[:, b % 4, :], rs[:, :],
                                                ALU.add).then_inc(q1_ready, 1)
                    if s.has(2):
                        mix(s, 1)
                    b = s.tile(0)
                    if b is not None:
                        dve.wait_ge(qh_ready, s.m(b))
                        nc.vector.tensor_tensor(qs[:, LO, :], qin[:, b % 4, :], qs[:, HI, :],
                                                ALU.subtract).then_inc(ql_ready, 1)
                    if s.has(1):
                        low(s, 1, h2f, h2s, h2h_ready, h2l_ready)
                    b = s.tile(4)
                    if b is not None:
                        dve.wait_ge(q1_ready, s.m(min(b + 2, B - 1)))
                        dve.wait_ge(sgb_ready, s.m(b))
                        nc.vector.tensor_tensor(rs[:, :], p_z[0:TOK, 0:D], rsg[:, 1, :],
                                                ALU.mult).then_inc(sb_ready, 1)
                        dve.wait_ge(sb_ready, s.m(b))
                        if s.has_m(b - 8) and s.has():
                            dve.wait_ge(acc_ready, s.J * B + (b + 1 - B))
                        nc.vector.tensor_tensor(res[:, b, :], q1[:, b % 3, :], rs[:, :],
                                                ALU.add).then_inc(r_ready, 1)
                        dve.wait_ge(r_ready, s.m(b))
                        dve.wait_ge(h_loaded[b % 4], s.J * 32 + 16 * (b // 4 + 1))
                        nc.vector.tensor_tensor(res[:, b, :], hin[:, b % 4, :], res[:, b, :],
                                                ALU.add).then_inc(res_ready, 1)
                        dve.wait_ge(res_ready, s.m(b))
                        nc.vector.bn_stats(stats[:, :], res[:, b, :]).then_inc(stat_ready, 1)
                    b = s.tile(2)
                    if b is not None:
                        dve.wait_ge(q1h_ready, s.m(b))
                        nc.vector.tensor_tensor(q1s[:, LO, :], q1[:, b % 3, :], q1s[:, HI, :],
                                                ALU.subtract).then_inc(q1l_ready, 1)
                    b = s.tile(5)
                    if b is not None:
                        dve.wait_ge(rstd_ready, s.m(b))
                        if s.has_m(b - 1):
                            dve.wait_ge(xnl_ready, s.m(b - 1))
                        nc.vector.tensor_scalar(xn2[:, :], res[:, b, :], mv[:, b % 2, 0:1], rstd[:, b % 2, :],
                                                ALU.subtract, ALU.mult).then_inc(xn_ready, 1)
                    b4 = s.tile(4)
                    if b4 is not None:
                        dve.wait_ge(stat_ready, s.m(b4))
                    if s.has(0):
                        low(s, 0, h1f, h1s, h1h_ready, h1l_ready)
                    if b4 is not None:
                        nc.vector.bn_aggr(mv[:, b4 % 2, :], stats[:, :]).then_inc(mv_ready, 1)
                    if b is not None:
                        dve.wait_ge(xnh_ready, s.m(b))
                        nc.vector.tensor_tensor(xn2s[:, LO, :], xn2[:, :], xn2s[:, HI, :],
                                                ALU.subtract).then_inc(xnl_ready, 1)
                    if retrieves(s) and s.i == 14:
                        dve.wait_ge(logits_filled, s.J + 1)
                        soft(1, s, nc.vector.scalar_tensor_tensor(out=logit[:, :], in0=p_z[0:TOK, 0:E],
                                                                  scalar=1.0 / B, in1=br_b[:, :],
                                                                  op0=ALU.mult, op1=ALU.add))
                        soft(2, s, nc.vector.reduce_max(top[:, :], logit[:, :], AX_X))
                        soft(3, s, nc.vector.tensor_scalar(logit[:, :], logit[:, :], top[:, :], None,
                                                           ALU.subtract))
                        dve.wait_ge(sig_ready, s.J + 1)
                        soft(4, s, nc.vector.reciprocal(sig[:, 1, :], sig[:, 1, :]))
                        soft(5, s, nc.vector.tensor_tensor(logit[:, :], sig[:, 0, :], sig[:, 1, :], ALU.mult))
                        soft(6, s, nc.vector.reduce_sum(total[:, :], logit[:, :], AX_X))
                        soft(7, s, nc.vector.reciprocal(total[:, :], total[:, :]))
                        soft(8, s, nc.vector.tensor_scalar(gate_new[:, :], logit[:, :], total[:, :], None,
                                                           ALU.mult))
                    if retrieves(s) and s.i == 15:
                        dve.wait_ge(gate_t_filled, s.J + 1)
                        nc.vector.tensor_copy(gate_t[:, :], p_z[0:E, 0:TOK]).then_inc(const_v, 1)
                        dve.wait_ge(yb_filled, s.J + 1)
                        if s.has(0):
                            dve.wait_ge(acc_ready, s.J * B)
                        nc.vector.tensor_copy(yb[:, :], p_z[0:TOK, 0:D]).then_inc(yb_ready, 1)

                macros(dve, step)

            @block.tensor
            def _(pe):
                mm = nc.tensor.matmul

                def product(dst, left, right, start=True, stop=True):
                    n = 0
                    for k in range(KT):
                        for h, g in ((HI, HI), (HI, LO), (LO, HI)):
                            n += 1
                            last = mm(dst, left(h, k), right(g, k), start=start and n == 1,
                                      stop=stop and n == 3 * KT, skip_group_check=True)
                    return last

                def transposes(src):
                    for h in (HI, LO):
                        for k in range(KT):
                            at = (h * KT + k) * TP
                            last = mm(p_t[:, at:at + TP], src[:, h, k * 128:(k + 1) * 128],
                                      eye_r[0:TOK, :], start=True, stop=True, skip_group_check=True)
                    return last

                def layer(s, lag, bank, w, rhs, filled):
                    e = s.expert(lag)
                    for m in range(KT):
                        cols = slice(m * 128, (m + 1) * 128)
                        product(bank[m][:, 0:NTOK], lambda h, k: w[:, e, h, k, cols], rhs).then_inc(filled, 1)

                def layer3(s, half):
                    e = s.expert(2)
                    if s.has(3):
                        pe.wait_ge(mixed, s.n(3, 4) - 2 * (1 - half))
                    for t in range(2):
                        at = (2 * half + t) * TOK
                        last = product(p_3[half][0:TOK, t, :], lambda h, k: h2s[:, h, k, at:at + TOK],
                                       lambda h, k: ffn_w[2][:, e, h, k, :])
                    last.then_inc(l3_filled, 1)

                def retrieval_layer(l, src, filled):
                    product(p_z[0:TOK, 0:D], lambda h, k: src[:, h, k, 0:TOK],
                            lambda h, k: new_w[:, l, h, k, :], stop=False)
                    mm(p_z[0:TOK, 0:D], bias_on[:, :], new_bias[:, l, :], start=False, stop=True,
                       skip_group_check=True).then_inc(filled, 1)

                def step(s):
                    if s.has(2):
                        pe.wait_ge(h2l_ready, s.n(2, 2))
                        layer3(s, 0)
                    b = s.tile(2)
                    if b is not None:
                        pe.wait_ge(qt_ready, s.m(b))
                        if b == 0:
                            if s.has_m(b - 8):
                                pe.wait_ge(yb_ready, s.J)
                        elif b < 3:
                            pe.wait_ge(sa_ready, s.m(b - 1))
                        else:
                            pe.wait_ge(sb_ready, s.m(b - 3))
                        retrieval_layer(0, q_t, za_filled)
                    b = s.tile(1)
                    if b is not None:
                        pe.wait_ge(ql_ready, s.m(b))
                        if s.has_m(b - 1) and b < 5:
                            pe.wait_ge(qt_ready, s.m(b - 1))
                        if b == 0 and s.has_m(-1):
                            pe.wait_ge(xt_ready, s.m(-1))
                        if 3 <= b < 5:
                            pe.wait_ge(q1t_ready, s.m(b - 3))
                        if b >= 5:
                            pe.wait_ge(xt_ready, s.m(b - 5))
                        transposes(qs).then_inc(qt_filled, 1)
                    if s.has(2):
                        layer3(s, 1)
                    if s.has(1):
                        pe.wait_ge(h1l_ready, s.n(1, 2))
                        if s.has(2):
                            pe.wait_ge(h2h_ready, s.n(2, 2))
                        layer(s, 1, p_2, ffn_w[1], lambda h, k: h1s[:, h, k, :], l2_filled)
                    b = s.tile(4)
                    if b is not None:
                        pe.wait_ge(q1t_ready, s.m(b))
                        if b + 2 < B:
                            pe.wait_ge(sa_ready, s.m(b + 2))
                        else:
                            pe.wait_ge(sb_ready, s.m(b - 1))
                        retrieval_layer(1, q1_t, zb_filled)
                    b = s.tile(3)
                    if b is not None:
                        pe.wait_ge(q1l_ready, s.m(b))
                        if b + 2 < B:
                            pe.wait_ge(qt_ready, s.m(b + 2))
                        else:
                            pe.wait_ge(xt_ready, s.m(b - 3))
                        transposes(q1s).then_inc(q1t_filled, 1)
                    if s.has(0):
                        g = s.group(0)
                        if s.i % E == 0:
                            pe.wait_ge(copied[g], s.J * 16)
                        if s.has(1):
                            pe.wait_ge(h1h_ready, s.n(1, 2))
                        at = slice(GRP * g, GRP * g + GRP)
                        layer(s, 0, p_1, ffn_w[0],
                              lambda h, k: xt_use[:, h, k, at, :].rearrange("p b t -> p (b t)"), l1_filled)
                    b = s.tile(5)
                    if b is not None:
                        pe.wait_ge(xnl_ready, s.m(b))
                        if b + 2 < B:
                            pe.wait_ge(q1t_ready, s.m(b + 2))
                        else:
                            pe.wait_ge(xt_ready, s.m(b - 1))
                        transposes(xn2s[:, :, :]).then_inc(xt_filled, 1)
                    if retrieves(s) and s.i == 13:
                        pe.wait_ge(xt_ready, s.m(B - 1))
                        pe.wait_ge(sb_ready, s.m(B - 1))
                        pe.wait_ge(const_v, 2)
                        for b in range(B):
                            last = product(p_z[0:TOK, 0:E], lambda h, k: xt_new[:, h, k, b, :],
                                           lambda h, k: w_r[:, h, k, :], start=(b == 0), stop=(b == B - 1))
                        last.then_inc(logits_filled, 1)
                    if retrieves(s) and s.i == 15:
                        pe.wait_ge(soft_v, (s.J + 1) * SOFT)
                        nc.tensor.transpose(p_z[0:E, 0:TOK], gate_new[:, :],
                                            eye[0:TOK, 0:TOK]).then_inc(gate_t_filled, 1)
                        pe.wait_ge(const_v, s.J + 3)
                        mm(p_z[0:TOK, 0:D], gate_t[:, :], bo_s[:, :], start=True,
                           stop=True).then_inc(yb_filled, 1)

                macros(pe, step)


_INS = ['x', 'L0_tok_blur_kernel', 'L0_attn_Wk', 'L0_attn_Wq', 'L0_attn_Wv', 'L0_attn_Wlr', 'L0_attn_blr',
        'L0_attn_Ws', 'L0_attn_bs', 'L0_ffn_Wr', 'L0_ffn_br', 'L0_ffn_W1', 'L0_ffn_b1', 'L0_ffn_g1',
        'L0_ffn_be1', 'L0_ffn_m1', 'L0_ffn_v1', 'L0_ffn_W2', 'L0_ffn_b2', 'L0_ffn_g2', 'L0_ffn_be2',
        'L0_ffn_m2', 'L0_ffn_v2', 'L0_ffn_Wo', 'L0_ffn_bo']
_OUTS = [((B, TOKENS, D), 'float32')]


def kernel(**inputs):
    import numpy as _np
    import concourse.bacc as _bacc
    from concourse import mybir as _mybir
    from concourse.bass_utils import run_bass_kernel_spmd as _run

    nc = _bacc.Bacc("TRN2", target_bir_lowering=False, num_devices=1)
    arrays, args = {}, []
    for name in _INS:
        a = _np.ascontiguousarray(inputs[name])
        arrays[f"in_{name}_dram"] = a
        args.append(nc.dram_tensor(f"in_{name}_dram", a.shape, _mybir.dt.from_np(a.dtype), kind="ExternalInput").ap())
    for i, (shape, dtype) in enumerate(_OUTS):
        dt = _mybir.dt.from_np(_np.dtype(dtype))
        args.append(nc.dram_tensor(f"out_{i}_dram", shape, dt, kind="ExternalOutput").ap())
    audio_tower(nc, *args)
    r = _run(nc, [arrays], core_ids=[0])
    got = tuple(r.results[0][f"out_{i}_dram"] for i in range(len(_OUTS)))
    return got[0]
```

```python
from contextlib import ExitStack

import concourse.bass as bass
from concourse import mybir

F32 = mybir.dt.float32
F32R = mybir.dt.float32r
ALU = mybir.AluOpType
ACT = mybir.ActivationFunctionType
AX_X = mybir.AxisListType.X

B = 8
D = 256
KT = D // 128
TOK = 125
NJ = 12
TILES = B * NJ
TOKENS = NJ * TOK
CH = 4
CHUNKS = NJ // CH
E = 8
GRP = 4
NTOK = GRP * TOK
TP = TOK + 1
HI, LO = 0, 1

LR, WD, ADAM_EPS, MAX_ALR = 0.001, 0.01, 1e-8, 0.1
LN_EPS, BN_EPS = 1e-5, 1e-3
GRAD_SCALE = MAX_ALR * 2.0 / D

POOL, STATS, RSTD, NORM, X_T, LAYER0, LAYER1, BACK1, GRAD0 = -1, 1, 2, 3, 4, 5, 6, 7, 8


class Step:

    def __init__(self, b, t):
        self.b, self.t = b, t

    def has(self, lag):
        return not isinstance(self.b, int) or 0 <= NJ * self.b + self.t - lag < TILES

    def n(self, lag):
        return self.b * NJ + (self.t - lag + 1)

    def slot(self, lag, ring):
        return (self.t - lag) % ring

    def chunk(self, lag):
        return (self.t - lag) // CH

    def part(self, lag):
        return (self.t - lag) % CH


class Pace:

    def __init__(self, J, n):
        self.J, self.i = J, n

    def has(self, lag=0):
        return not isinstance(self.J, int) or 0 <= 16 * (self.J - 1) + self.i - lag < 16 * NJ

    def n(self, lag=0, per=1):
        return self.J * (16 * per) + per * (self.i - lag + 1 - 16)

    def expert(self, lag=0):
        return (self.i - lag) % E

    def group(self, lag=0):
        return (self.i - lag) // E % 2

    def tile(self, lag):
        b = self.i - lag
        return b if 0 <= b < B and not (isinstance(self.J, int) and self.J >= NJ) else None

    def m(self, b, per=1):
        return self.J * (B * per) + (b + 1) * per

    def has_m(self, b):
        return not isinstance(self.J, int) or self.J * B + b >= 0


def audio_tower(nc, x, blur, wk, wq, wv, wlr, blr, ws, bs, wr, br, w1, b1, g1, be1, m1, v1,
                w2, b2, g2, be2, m2, v2, wo, bo, out):
    h_dram = nc.dram_tensor("h_dram", (B, TOKENS, D), F32, kind="Internal").ap()
    q_dram = nc.dram_tensor("q_dram", (B, TOKENS, D), F32, kind="Internal").ap()
    s_dram = nc.dram_tensor("s_dram", (2, E * D), F32, kind="Internal").ap()

    with ExitStack() as keep:
        def sb_keep(name, shape, dt=F32):
            return keep.enter_context(nc.sbuf_tensor(name, shape, dt))

        eye = sb_keep("eye", [128, 128])
        eye_r = sb_keep("eye_r", [128, TP], F32R)
        bias_on = sb_keep("bias_on", [128, TOK], F32R)
        new_w = sb_keep("new_w", [128, 2, 2, KT, D], F32R)
        new_bias = sb_keep("new_bias", [128, 2, D], F32R)
        minus_half = sb_keep("minus_half", [128, 128])
        ln_eps = sb_keep("ln_eps", [128, 1])

        gradient_sweep(nc, x, blur, wk, wq, wv, wlr, blr, ws, bs, h_dram, q_dram,
                       eye, eye_r, bias_on, new_w, new_bias, minus_half, ln_eps)
        with ExitStack() as ex:
            def sb_ex(name, shape, dt=F32):
                return ex.enter_context(nc.sbuf_tensor(name, shape, dt))
            ffn_w = [sb_ex(f"ffn_w{i}", [128, E, 2, KT, D], F32R) for i in range(3)]
            ffn_bias = sb_ex("ffn_bias", [128, 2, KT * E])
            expert_weights(nc, w1, b1, g1, be1, m1, v1, w2, b2, g2, be2, m2, v2, wo, s_dram,
                           ffn_w, ffn_bias, eye, minus_half)
            block_sweep(nc, wr, br, bo, h_dram, q_dram, out, ffn_w, ffn_bias,
                        eye, eye_r, bias_on, new_w, new_bias, minus_half, ln_eps)


def gradient_sweep(nc, x, blur, wk, wq, wv, wlr, blr, ws, bs, h_dram, q_dram,
                   eye, eye_r, bias_on, new_w, new_bias, minus_half, ln_eps):
    x_rows = x.rearrange("b (p r) d -> b p (r d)", r=2 * NJ)
    h_tok = h_dram.rearrange("b (p j) d -> b p (j d)", j=NJ)
    q_tok = q_dram.rearrange("b (p j) d -> b p (j d)", j=NJ)

    with ExitStack() as ctx:
        def sb(name, shape, dt=F32):
            return ctx.enter_context(nc.sbuf_tensor(name, shape, dt))

        def psum(name, shape):
            return ctx.enter_context(nc.psum_tensor(name, shape, F32))

        def sem(name):
            return ctx.enter_context(nc.semaphore(name))

        raw_k = sb("raw_k", [128, KT, D])
        raw_w = sb("raw_w", [128, 2, KT, D])
        raw_lr = sb("raw_lr", [128, KT, 2])
        raw_b = sb("raw_b", [33, 2, D])
        raw_q = sb("raw_q", [128, KT, D])
        raw_v = sb("raw_v", [128, KT, D])
        wk_t = sb("wk_t", [128, KT, D])
        w_kz = sb("w_kz", [128, 2, KT, 2 * D], F32R)
        w_v = sb("w_v", [128, 2, KT, D + 2], F32R)
        w_q = sb("w_q", [128, 2, KT, D], F32R)
        w_1 = sb("w_1", [128, 2, KT, D], F32R)
        w_1t = sb("w_1t", [128, 2, KT, D], F32R)
        bias_h = sb("bias_h", [33, 2, D], F32R)
        bias_l = sb("bias_l", [33, 2, D], F32R)
        bias = sb("bias", [128, 2, D], F32R)
        rate_bias = sb("rate_bias", [TOK, 1])
        ones = sb("ones", [TOK, 128], F32R)
        blur_w = sb("blur_w", [TOK, 3, D])
        blur_end = sb("blur_end", [TOK, D])

        rows = sb("rows", [TOK, 2 * NJ + 2, D])
        pool = sb("pool", [TOK, 9, D])
        tap1 = sb("tap1", [TOK, D])
        tap2 = sb("tap2", [TOK, D])
        hbuf = sb("hbuf", [TOK, CHUNKS, CH, D])
        qbuf = sb("qbuf", [TOK, 3, D])
        stats = sb("stats", [TOK, 2, 6])
        mv = sb("mv", [TOK, 2, 2])
        var_eps = sb("var_eps", [TOK, 2, 1])
        rstd = sb("rstd", [TOK, 2, 1])
        xn = sb("xn", [TOK, 2, D])
        xs = sb("xs", [TOK, 6, 2, D], F32R)
        x_t = sb("x_t", [128, 3, 2, KT, TP], F32R)
        sg0 = sb("sg0", [TOK, 2, D])
        s0 = sb("s0", [TOK, 2, D])
        m0 = sb("m0", [TOK, 2, D])
        f0 = sb("f0", [TOK, 4, D])
        x1 = sb("x1", [TOK, 2, D])
        x1s = sb("x1s", [TOK, 3, 2, D], F32R)
        x1_t = sb("x1_t", [128, 2, 2, KT, TP], F32R)
        u = sb("u", [TOK, 2, D])
        sg1 = sb("sg1", [TOK, 2, D])
        rate = sb("rate", [TOK, 4, 1])
        s1 = sb("s1", [TOK, 2, D])
        m1 = sb("m1", [TOK, 2, D])
        f1 = sb("f1", [TOK, 2, D])
        diff = sb("diff", [TOK, 2, D])
        dz1 = sb("dz1", [TOK, 2, D])
        dz1s = sb("dz1s", [TOK, 2, 2, D], F32R)
        dz1_t = sb("dz1_t", [128, 2, 2, KT, TP], F32R)
        back = sb("back", [TOK, 2, D])
        dz0 = sb("dz0", [TOK, 2, D])
        dz0s = sb("dz0s", [TOK, 2, 2, D], F32R)
        g0_raw = sb("g0_raw", [128, KT, D])
        mag, ratio, stepped = (t[:, :, :].rearrange("p k n -> p (k n)") for t in (raw_q, raw_v, wk_t))

        p_t = psum("p_t", [128, 512])
        p_kz = psum("p_kz", [128, 512])
        p_v = psum("p_v", [128, 512])
        p_z1 = psum("p_z1", [128, 512])
        p_dx = psum("p_dx", [128, 512])
        p_g0 = psum("p_g0", [128, 512])
        p_g1 = psum("p_g1", [128, 512])
        p_gb = psum("p_gb", [128, 512])

        loaded = sem("loaded")
        consts = sem("consts")
        eye_zero = sem("eye_zero")
        setup_t = sem("setup_t")
        setup_v = sem("setup_v")
        wk_t_done = sem("wk_t_done")
        kw0_filled = sem("kw0_filled")
        chain = sem("chain")
        taps_loaded = sem("taps_loaded")
        x_loaded = [sem(f"x_loaded{c}") for c in range(CHUNKS)]
        pooled = sem("pooled")
        tok_ops = sem("tok_ops")
        h_stored = [sem(f"h_stored{c}") for c in range(CHUNKS)]
        q_stored = [sem(f"q_stored{r}") for r in range(3)]
        stats_ready = sem("stats_ready")
        mv_ready = sem("mv_ready")
        eps_added = sem("eps_added")
        rstd_ready = sem("rstd_ready")
        xn_ready = sem("xn_ready")
        xh_ready = sem("xh_ready")
        xl_ready = sem("xl_ready")
        xt_filled = sem("xt_filled")
        xt_ready = sem("xt_ready")
        kz_filled = sem("kz_filled")
        v_filled = sem("v_filled")
        q_filled = sem("q_filled")
        rate_ready = sem("rate_ready")
        sg0_ready = sem("sg0_ready")
        s0_ready = sem("s0_ready")
        x1_ready = sem("x1_ready")
        m0_ready = sem("m0_ready")
        f0_ready = sem("f0_ready")
        q_copied = sem("q_copied")
        u_ready = sem("u_ready")
        x1h_ready = sem("x1h_ready")
        x1l_ready = sem("x1l_ready")
        x1t_filled = sem("x1t_filled")
        x1t_ready = sem("x1t_ready")
        z1_filled = sem("z1_filled")
        sg1_ready = sem("sg1_ready")
        s1_ready = sem("s1_ready")
        m1_ready = sem("m1_ready")
        f1_ready = sem("f1_ready")
        diff_ready = sem("diff_ready")
        dz1_ready = sem("dz1_ready")
        dz1h_ready = sem("dz1h_ready")
        dz1l_ready = sem("dz1l_ready")
        dz1t_filled = sem("dz1t_filled")
        dz1t_ready = sem("dz1t_ready")
        dx_filled = sem("dx_filled")
        g1_added = sem("g1_added")
        back_ready = sem("back_ready")
        dz0_ready = sem("dz0_ready")
        dz0h_ready = sem("dz0h_ready")
        dz0l_ready = sem("dz0l_ready")
        g0_added = sem("g0_added")
        adam_v = sem("adam_v")
        adam_t = sem("adam_t")

        LOADS = 12
        TOK_OPS = 5

        def pool_slot(r):
            return 0 if r == 0 else 1 + (r - 1) % 8

        def gradient_steps(engine, step):
            for t in range(NJ):
                step(Step(0, t))
            with engine.Fori(1, B - 1) as b:
                for t in range(NJ):
                    step(Step(b, t))
            for t in range(NJ):
                step(Step(B - 1, t))
            for t in range(GRAD0):
                step(Step(B, t))

        with nc.Block() as block:

            @block.sync
            def _(sp):
                def load_rows(b, c):
                    one = slice(b, b + 1) if isinstance(b, int) else bass.ds(b, 1)
                    src = x_rows[one].rearrange("a p n -> p (a n)")
                    first, last = (8 * c + 2 if c else 0), min(8 * c + 10, 2 * NJ)
                    sp.dma_start(rows[:, first:last, :].rearrange("p r d -> p (r d)"),
                                 src[:, first * D:last * D]).then_inc(x_loaded[c], 16)
                    if c == CHUNKS - 1:
                        sp.dma_start(rows[0:TOK - 1, 2 * NJ:, :].rearrange("p r d -> p (r d)"),
                                     src[1:TOK, 0:2 * D]).then_inc(x_loaded[c], 16)
                        for r in (2 * NJ, 2 * NJ + 1):
                            sp.dma_start(rows[TOK - 1:TOK, r, :],
                                         src[TOK - 1:TOK, (2 * NJ - 1) * D:]).then_inc(x_loaded[c], 16)

                load_rows(0, 0)
                for c in range(3):
                    sp.dma_start(blur_w[:, c, :], blur[c].broadcast_to([TOK, D])).then_inc(taps_loaded, 16)
                sp.wait_ge(consts, 1)
                sp.dma_start(blur_end[0:TOK - 1, :], blur[2].broadcast_to([TOK - 1, D])).then_inc(taps_loaded, 16)
                for dst, src in ((raw_k, wk), (raw_q, wq), (raw_v, wv)):
                    sp.dma_start(dst[:, :, :], src.rearrange("(k p) n -> p k n", p=128)).then_inc(loaded, 16)
                for l in range(2):
                    sp.dma_start(raw_w[:, l], ws[l].rearrange("(k p) n -> p k n", p=128)).then_inc(loaded, 16)
                for c in range(2):
                    sp.dma_start(raw_lr[:, :, c:c + 1], wlr.rearrange("(k p) n -> p k n", p=128),
                                 allow_slow_non_contiguous=True).then_inc(loaded, 16)
                for p in (0, 32):
                    for l in range(2):
                        sp.dma_start(raw_b[p:p + 1, l, :], bs[l:l + 1, :]).then_inc(loaded, 16)
                sp.dma_start(rate_bias[:, :], blr.rearrange("(a n) -> a n", a=1).broadcast_to([TOK, 1])
                             ).then_inc(loaded, 16)
                for c in range(1, CHUNKS):
                    load_rows(0, c)

                def step(s):
                    b, t = s.b, s.t
                    if not isinstance(b, int) or b < B:
                        if not isinstance(b, int) or b < B - 1:
                            if t in (5, 9):
                                sp.wait_ge(pooled, s.n(0))
                                load_rows(b + 1, (t - 5) // CH)
                    if t == 0 and isinstance(b, int) and b == 0:
                        return
                    if t == 0 and (not isinstance(b, int) or b < B):
                        sp.wait_ge(pooled, s.n(1))
                        load_rows(b, CHUNKS - 1)
                    if s.has(STATS) and s.part(STATS) == CH - 1:
                        c = s.chunk(STATS)
                        sp.wait_ge(tok_ops, s.n(STATS) * TOK_OPS)
                        bb = b if c >= 0 else b - 1
                        one = slice(bb, bb + 1) if isinstance(bb, int) else bass.ds(bb, 1)
                        c = c % CHUNKS
                        sp.dma_start(h_tok[one].rearrange("a p n -> p (a n)")[:, c * CH * D:(c + 1) * CH * D],
                                     hbuf[:, c, :, :].rearrange("p u d -> p (u d)")).then_inc(h_stored[c], 16)
                    if s.has(LAYER0):
                        j = t - LAYER0
                        bb = b if j >= 0 else b - 1
                        one = slice(bb, bb + 1) if isinstance(bb, int) else bass.ds(bb, 1)
                        j = j % NJ
                        sp.wait_ge(q_copied, s.n(LAYER0))
                        sp.dma_start(q_tok[one].rearrange("a p n -> p (a n)")[:, j * D:(j + 1) * D],
                                     qbuf[:, j % 3, :]).then_inc(q_stored[j % 3], 16)

                gradient_steps(sp, step)
                for c in range(CHUNKS):
                    sp.wait_ge(h_stored[c], 16 * B)
                for r in range(3):
                    sp.wait_ge(q_stored[r], 16 * TILES // 3)

            @block.gpsimd
            def _(po):
                po.memset(raw_b[:, :, :], 0.0)
                po.memset(blur_end[:, :], 0.0).then_inc(consts, 1)
                po.memset(eye[:, :], 0.0).then_inc(eye_zero, 1)
                po.memset(bias_on[:, :].bitcast(F32), 0.0)
                po.memset(bias[:, :, :].bitcast(F32), 0.0)
                po.memset(new_bias[:, :, :].bitcast(F32), 0.0)
                po.memset(ones[:, :].bitcast(F32), 1.0)
                po.memset(minus_half[:, :], -0.5)
                po.memset(ln_eps[:, :], LN_EPS).then_inc(eye_zero, 1)
                po.wait_ge(eye_zero, 2)
                po.affine_select(out=eye[:, :], in_=eye[:, :], compare_op=ALU.not_equal, fill=1.0, base=0,
                                 pattern=[[-1, 128]], channel_multiplier=1).then_inc(consts, 1)
                po.wait_ge(consts, 2)
                po.wait_ge(taps_loaded, 64)

                def tokenize(s):
                    h = hbuf[:, s.t // CH, s.t % CH, :]
                    last = blur_end[:, :] if s.t == NJ - 1 else blur_w[:, 2, :]
                    po.wait_ge(pooled, s.n(0))
                    if s.has(NJ):
                        po.wait_ge(xn_ready, s.n(NJ))
                        po.wait_ge(h_stored[s.t // CH], s.b * 16)
                    po.tensor_tensor(h, pool[:, pool_slot(2 * s.t), :], blur_w[:, 0, :],
                                     ALU.mult).then_inc(tok_ops, 1)
                    if s.has(1):
                        po.wait_ge(tok_ops, s.n(1) * TOK_OPS)
                    po.tensor_tensor(tap1[:, :], pool[:, pool_slot(2 * s.t + 1), :], blur_w[:, 1, :],
                                     ALU.mult).then_inc(tok_ops, 1)
                    po.tensor_tensor(tap2[:, :], pool[:, pool_slot(2 * s.t + 2), :], last,
                                     ALU.mult).then_inc(tok_ops, 1)
                    po.wait_ge(tok_ops, s.n(0) * TOK_OPS - 3)
                    po.tensor_tensor(h, h, tap1[:, :], ALU.add).then_inc(tok_ops, 1)
                    po.wait_ge(tok_ops, s.n(0) * TOK_OPS - 1)
                    po.tensor_tensor(h, h, tap2[:, :], ALU.add).then_inc(tok_ops, 1)

                def step(s):
                    if s.has(RSTD):
                        k = s.slot(RSTD, 2)
                        po.wait_ge(mv_ready, s.n(RSTD))
                        po.tensor_tensor(var_eps[:, k, :], mv[:, k, 1:2], ln_eps[0:TOK, :],
                                         ALU.add).then_inc(eps_added, 1)
                        po.wait_ge(eps_added, s.n(RSTD))
                        if s.has(RSTD + 2):
                            po.wait_ge(xn_ready, s.n(RSTD + 2))
                        po.tensor_tensor(rstd[:, k, :], var_eps[:, k, :], minus_half[0:TOK, 0:1],
                                         ALU.pow).then_inc(rstd_ready, 1)
                    if s.has(GRAD0):
                        k = s.slot(GRAD0, 2)
                        po.wait_ge(dz0h_ready, s.n(GRAD0))
                        if s.has(GRAD0 + 2):
                            po.wait_ge(g0_added, s.n(GRAD0 + 2))
                        po.tensor_tensor(dz0s[:, k, LO, :], dz0[:, k, :], dz0s[:, k, HI, :],
                                         ALU.subtract).then_inc(dz0l_ready, 1)
                    if s.has(NORM):
                        k, r = s.slot(NORM, 2), s.slot(NORM, 6)
                        po.wait_ge(xh_ready, s.n(NORM))
                        po.tensor_tensor(xs[:, r, LO, :], xn[:, k, :], xs[:, r, HI, :],
                                         ALU.subtract).then_inc(xl_ready, 1)
                    if s.has(0):
                        tokenize(s)
                    if s.has(LAYER0):
                        k = s.slot(LAYER0, 2)
                        po.wait_ge(m0_ready, s.n(LAYER0))
                        if s.has(LAYER0 + 4):
                            po.wait_ge(dz0_ready, s.n(LAYER0 + 4))
                        po.tensor_tensor(f0[:, s.slot(LAYER0, 4), :], sg0[:, k, :], m0[:, k, :],
                                         ALU.subtract).then_inc(f0_ready, 1)

                gradient_steps(po, step)

            @block.scalar
            def _(act):
                def step(s):
                    if s.has(LAYER1):
                        k = s.slot(LAYER1, 2)
                        act.wait_ge(z1_filled, s.n(LAYER1))
                        if s.has(LAYER1 + 2):
                            act.wait_ge(f1_ready, s.n(LAYER1 + 2))
                        nc.scalar.activation(sg1[:, k, :], p_z1[0:TOK, 0:D],
                                             ACT.Sigmoid).then_inc(sg1_ready, 1)
                    if s.has(X_T):
                        act.wait_ge(xt_filled, s.n(X_T))
                        if s.has(X_T + 3):
                            act.wait_ge(q_filled, s.n(X_T + 3))
                        nc.scalar.copy(x_t[:, s.slot(X_T, 3)].rearrange("p h k t -> p (h k t)"),
                                       p_t[:, 0:4 * TP]).then_inc(xt_ready, 1)
                    if s.has(LAYER0):
                        act.wait_ge(kz_filled, s.n(LAYER0))
                        if s.has(LAYER0 + 2):
                            act.wait_ge(f0_ready, s.n(LAYER0 + 2))
                        nc.scalar.activation(sg0[:, s.slot(LAYER0, 2), :], p_kz[0:TOK, D:2 * D],
                                             ACT.Sigmoid).then_inc(sg0_ready, 1)
                    if s.has(NORM):
                        act.wait_ge(xn_ready, s.n(NORM))
                        if s.has(NORM + 6):
                            act.wait_ge(g0_added, s.n(NORM + 6))
                        nc.scalar.copy(xs[:, s.slot(NORM, 6), HI, :],
                                       xn[:, s.slot(NORM, 2), :]).then_inc(xh_ready, 1)
                    if s.has(LAYER0):
                        act.wait_ge(v_filled, s.n(LAYER0))
                        if s.has(LAYER0 + 4):
                            act.wait_ge(back_ready, s.n(LAYER0 + 4))
                        nc.scalar.activation(rate[:, s.slot(LAYER0, 4), :], p_v[0:TOK, D:D + 1], ACT.Sigmoid,
                                             bias=rate_bias[:, :]).then_inc(rate_ready, 1)
                    if s.has(LAYER1):
                        k = s.slot(LAYER1, 2)
                        act.wait_ge(dz1_ready, s.n(LAYER1))
                        if s.has(LAYER1 + 2):
                            act.wait_ge(g1_added, s.n(LAYER1 + 2))
                        nc.scalar.copy(dz1s[:, k, HI, :], dz1[:, k, :]).then_inc(dz1h_ready, 1)
                    if s.has(LAYER0):
                        k, r = s.slot(LAYER0, 2), s.slot(LAYER0, 3)
                        act.wait_ge(x1_ready, s.n(LAYER0))
                        if s.has(LAYER0 + 3):
                            act.wait_ge(g1_added, s.n(LAYER0 + 3))
                        nc.scalar.copy(x1s[:, r, HI, :], x1[:, k, :]).then_inc(x1h_ready, 1)
                    if s.has(LAYER0):
                        act.wait_ge(q_filled, s.n(LAYER0))
                        if s.has(LAYER0 + 3):
                            i3 = (s.t - LAYER0) // 3
                            act.wait_ge(q_stored[s.slot(LAYER0, 3)], s.b * 64 + 16 * i3)
                        nc.scalar.copy(qbuf[:, s.slot(LAYER0, 3), :], p_z1[0:TOK, D:2 * D]).then_inc(q_copied, 1)
                    if s.has(LAYER1):
                        act.wait_ge(dz1t_filled, s.n(LAYER1))
                        if s.has(LAYER1 + 2):
                            act.wait_ge(dx_filled, s.n(LAYER1 + 2))
                        nc.scalar.copy(dz1_t[:, s.slot(LAYER1, 2)].rearrange("p h k t -> p (h k t)"),
                                       p_t[:, 0:4 * TP]).then_inc(dz1t_ready, 1)
                    if s.has(LAYER0):
                        act.wait_ge(x1t_filled, s.n(LAYER0))
                        if s.has(LAYER0 + 2):
                            act.wait_ge(z1_filled, s.n(LAYER0 + 2))
                        nc.scalar.copy(x1_t[:, s.slot(LAYER0, 2)].rearrange("p h k t -> p (h k t)"),
                                       p_t[:, 0:4 * TP]).then_inc(x1t_ready, 1)
                    if s.has(BACK1):
                        k = s.slot(BACK1, 2)
                        act.wait_ge(dz0_ready, s.n(BACK1))
                        if s.has(BACK1 + 2):
                            act.wait_ge(g0_added, s.n(BACK1 + 2))
                        nc.scalar.copy(dz0s[:, k, HI, :], dz0[:, k, :]).then_inc(dz0h_ready, 1)

                gradient_steps(act, step)

            @block.vector
            def _(dve):
                count = [0]

                def link(ins, s=chain):
                    count[0] += 1
                    ins.then_inc(s, 1)
                    dve.wait_ge(s, count[0])

                def split(high, low, src):
                    link(nc.vector.tensor_copy(high, src))
                    link(nc.vector.tensor_tensor(low, src, high, ALU.subtract))

                def pool_rows(s):
                    t = s.slot(POOL, NJ)
                    c = t // CH
                    b = s.b if s.t - POOL < NJ else s.b + 1
                    dve.wait_ge(x_loaded[c], (b + 1) * (64 if c == CHUNKS - 1 else 16))
                    if s.has(POOL + 3):
                        dve.wait_ge(tok_ops, s.n(POOL + 3) * TOK_OPS)
                    first, last = (2 * t + 1 if t else 0), 2 * t + 3
                    at = pool_slot(first)
                    nc.vector.tensor_tensor(pool[:, at:at + last - first, :], rows[:, first:last, :],
                                            rows[:, first + 1:last + 1, :], ALU.max).then_inc(pooled, 1)

                pool_rows(Step(0, POOL))
                dve.wait_ge(loaded, 16 * LOADS)
                dve.wait_ge(consts, 2)
                link(nc.vector.tensor_copy(eye_r[:, :], eye[:, 0:TP]))
                for p in (0, 32):
                    link(nc.vector.memset(bias_on[p:p + 1, :].bitcast(F32), 1.0))
                dve.wait_ge(setup_t, 1)
                link(nc.vector.tensor_copy(wk_t[:, :, :].rearrange("p k n -> p (k n)"), p_kz[:, :]))
                dve.sem_inc(wk_t_done, 1)
                split(w_v[:, HI, :, 0:D], w_v[:, LO, :, 0:D], raw_v[:, :, :])
                split(w_v[:, HI, :, D:], w_v[:, LO, :, D:], raw_lr[:, :, :])
                split(w_kz[:, HI, :, 0:D], w_kz[:, LO, :, 0:D], raw_k[:, :, :])
                dve.wait_ge(kw0_filled, 1)
                split(w_kz[:, HI, :, D:], w_kz[:, LO, :, D:], p_z1[:, :].rearrange("p (k n) -> p k n", k=KT))
                split(w_q[:, HI], w_q[:, LO], raw_q[:, :, :])
                split(w_1[:, HI], w_1[:, LO], raw_w[:, 1])
                split(bias_h[:, :, :], bias_l[:, :, :], raw_b[:, :, :])
                link(nc.vector.tensor_copy(bias[0:1], bias_h[0:1]))
                link(nc.vector.tensor_copy(bias[32:33], bias_l[32:33]))
                split(w_1t[:, HI].rearrange("p k n -> p (k n)"), w_1t[:, LO].rearrange("p k n -> p (k n)"),
                      p_dx[:, :])
                dve.sem_inc(setup_v, 1)

                def step(s):
                    if s.has(LAYER1):
                        k = s.slot(LAYER1, 2)
                        dve.wait_ge(sg1_ready, s.n(LAYER1))
                        nc.vector.tensor_tensor(s1[:, k, :], p_z1[0:TOK, 0:D], sg1[:, k, :],
                                                ALU.mult).then_inc(s1_ready, 1)
                    if s.has(NORM):
                        k = s.slot(NORM, 2)
                        h = hbuf[:, s.chunk(NORM) % CHUNKS, s.part(NORM), :]
                        dve.wait_ge(rstd_ready, s.n(NORM))
                        if s.has(NORM + 2):
                            dve.wait_ge(xl_ready, s.n(NORM + 2))
                        nc.vector.tensor_scalar(xn[:, k, :], h, mv[:, k, 0:1], rstd[:, k, :],
                                                ALU.subtract, ALU.mult).then_inc(xn_ready, 1)
                    if s.has(LAYER1):
                        k = s.slot(LAYER1, 2)
                        dve.wait_ge(s1_ready, s.n(LAYER1))
                        nc.vector.scalar_tensor_tensor(out=m1[:, k, :], in0=sg1[:, k, :], scalar=1.0,
                                                       in1=s1[:, k, :], op0=ALU.subtract,
                                                       op1=ALU.mult).then_inc(m1_ready, 1)
                        nc.vector.tensor_tensor(diff[:, k, :], u[:, k, :], s1[:, k, :],
                                                ALU.add).then_inc(diff_ready, 1)
                        dve.wait_ge(m1_ready, s.n(LAYER1))
                        nc.vector.tensor_tensor(f1[:, k, :], sg1[:, k, :], m1[:, k, :],
                                                ALU.subtract).then_inc(f1_ready, 1)
                    if s.has(LAYER1):
                        k = s.slot(LAYER1, 2)
                        dve.wait_ge(f1_ready, s.n(LAYER1))
                        if s.has(LAYER1 + 2):
                            dve.wait_ge(dz1l_ready, s.n(LAYER1 + 2))
                        nc.vector.scalar_tensor_tensor(out=dz1[:, k, :], in0=diff[:, k, :],
                                                       scalar=rate[:, s.slot(LAYER1, 4), :],
                                                       in1=f1[:, k, :], op0=ALU.mult,
                                                       op1=ALU.mult).then_inc(dz1_ready, 1)
                    if s.has(LAYER0):
                        k = s.slot(LAYER0, 2)
                        dve.wait_ge(sg0_ready, s.n(LAYER0))
                        nc.vector.tensor_tensor(s0[:, k, :], p_kz[0:TOK, D:2 * D], sg0[:, k, :],
                                                ALU.mult).then_inc(s0_ready, 1)
                    if s.has(LAYER1):
                        k = s.slot(LAYER1, 2)
                        dve.wait_ge(dz1h_ready, s.n(LAYER1))
                        nc.vector.tensor_tensor(dz1s[:, k, LO, :], dz1[:, k, :], dz1s[:, k, HI, :],
                                                ALU.subtract).then_inc(dz1l_ready, 1)
                    if s.has(LAYER0):
                        k = s.slot(LAYER0, 2)
                        dve.wait_ge(s0_ready, s.n(LAYER0))
                        if s.has(LAYER0 + 2):
                            dve.wait_ge(x1h_ready, s.n(LAYER0 + 2))
                        nc.vector.tensor_tensor(x1[:, k, :], p_kz[0:TOK, 0:D], s0[:, k, :],
                                                ALU.add).then_inc(x1_ready, 1)
                        nc.vector.scalar_tensor_tensor(out=m0[:, k, :], in0=sg0[:, k, :], scalar=1.0,
                                                       in1=s0[:, k, :], op0=ALU.subtract,
                                                       op1=ALU.mult).then_inc(m0_ready, 1)
                    if s.has(STATS):
                        h = hbuf[:, s.chunk(STATS) % CHUNKS, s.part(STATS), :]
                        dve.wait_ge(tok_ops, s.n(STATS) * TOK_OPS)
                        nc.vector.bn_stats(stats[:, s.slot(STATS, 2), :], h).then_inc(stats_ready, 1)
                    if s.has(LAYER0):
                        k = s.slot(LAYER0, 2)
                        dve.wait_ge(x1h_ready, s.n(LAYER0))
                        r = s.slot(LAYER0, 3)
                        nc.vector.tensor_tensor(x1s[:, r, LO, :], x1[:, k, :], x1s[:, r, HI, :],
                                                ALU.subtract).then_inc(x1l_ready, 1)
                    if s.has(STATS):
                        dve.wait_ge(stats_ready, s.n(STATS))
                    if s.has(POOL):
                        pool_rows(s)
                    if s.has(STATS):
                        k = s.slot(STATS, 2)
                        nc.vector.bn_aggr(mv[:, k, :], stats[:, k, :]).then_inc(mv_ready, 1)
                    if s.has(BACK1):
                        k = s.slot(BACK1, 2)
                        dve.wait_ge(dx_filled, s.n(BACK1))
                        nc.vector.scalar_tensor_tensor(out=back[:, k, :], in0=diff[:, k, :],
                                                       scalar=rate[:, s.slot(BACK1, 4), :],
                                                       in1=p_dx[0:TOK, 0:D],
                                                       op0=ALU.mult, op1=ALU.add).then_inc(back_ready, 1)
                    if s.has(LAYER0):
                        k = s.slot(LAYER0, 2)
                        dve.wait_ge(rate_ready, s.n(LAYER0))
                        nc.vector.tensor_tensor(u[:, k, :], x1[:, k, :], p_v[0:TOK, 0:D],
                                                ALU.subtract).then_inc(u_ready, 1)
                    if s.has(BACK1):
                        k = s.slot(BACK1, 2)
                        dve.wait_ge(back_ready, s.n(BACK1))
                        dve.wait_ge(f0_ready, s.n(BACK1))
                        if s.has(BACK1 + 2):
                            dve.wait_ge(dz0l_ready, s.n(BACK1 + 2))
                        nc.vector.tensor_tensor(dz0[:, k, :], back[:, k, :], f0[:, s.slot(BACK1, 4), :],
                                                ALU.mult).then_inc(dz0_ready, 1)

                gradient_steps(dve, step)

                count[0] = 0
                A = adam_v
                dve.wait_ge(g0_added, TILES)
                link(nc.vector.tensor_copy(g0_raw[:, :, :].rearrange("p k n -> p (k n)"), p_g0[:, :]), A)
                def adam(g, p, rows_=128, two=None):
                    mag_, ratio_, new = (t[0:rows_, :] if two is None else
                                         t[0:rows_, :].rearrange("p (l n) -> p l n", l=two)
                                         for t in (mag, ratio, stepped))
                    link(nc.vector.tensor_scalar(ratio_, g, GRAD_SCALE, None, ALU.mult), A)
                    link(nc.vector.scalar_tensor_tensor(out=mag_, in0=ratio_, scalar=-1.0, in1=ratio_,
                                                        op0=ALU.mult, op1=ALU.max), A)
                    link(nc.vector.tensor_scalar(mag_, mag_, ADAM_EPS, None, ALU.add), A)
                    link(nc.vector.reciprocal(mag_, mag_), A)
                    link(nc.vector.scalar_tensor_tensor(out=ratio_, in0=ratio_, scalar=LR, in1=mag_,
                                                        op0=ALU.mult, op1=ALU.mult), A)
                    link(nc.vector.scalar_tensor_tensor(out=new, in0=p, scalar=1.0 - LR * WD, in1=ratio_,
                                                        op0=ALU.mult, op1=ALU.subtract), A)
                    return new

                for l, grad in ((1, p_g1), (0, p_kz)):
                    if l == 0:
                        dve.wait_ge(adam_t, 1)
                    new = adam(grad[:, :], raw_w[:, l].rearrange("p k n -> p (k n)"))
                    src = new.rearrange("p (k n) -> p k n", k=KT)
                    link(nc.vector.tensor_copy(new_w[:, l, HI], src), A)
                    link(nc.vector.tensor_tensor(new_w[:, l, LO], src, new_w[:, l, HI], ALU.subtract), A)
                new = adam(p_gb[0:33, :].rearrange("p (l n) -> p l n", l=2), raw_b[:, :, :], 33, 2)
                nb_h, nb_l = bias_h[:, :, :], bias_l[:, :, :]
                link(nc.vector.tensor_copy(nb_h, new), A)
                link(nc.vector.tensor_tensor(nb_l, new, nb_h, ALU.subtract), A)
                link(nc.vector.tensor_copy(new_bias[0:1], nb_h[0:1]), A)
                link(nc.vector.tensor_copy(new_bias[32:33], nb_l[32:33]), A)

            @block.tensor
            def _(pe):
                mm = nc.tensor.matmul

                pe.wait_ge(loaded, 16 * LOADS)
                pe.wait_ge(consts, 2)
                for dst, src in ((p_kz, raw_k), (p_dx, raw_w[:, 1])):
                    for k in range(KT):
                        for m in range(KT):
                            last = nc.tensor.transpose(dst[:, m * D + k * 128:m * D + (k + 1) * 128],
                                                       src[:, k, m * 128:(m + 1) * 128], eye[:, :])
                last.then_inc(setup_t, 1)
                pe.wait_ge(wk_t_done, 1)
                for m in range(KT):
                    for k in range(KT):
                        last = mm(p_z1[:, m * D:(m + 1) * D], wk_t[:, k, m * 128:(m + 1) * 128],
                                  raw_w[:, 0, k, :], start=(k == 0), stop=(k == KT - 1))
                last.then_inc(kw0_filled, 1)
                pe.wait_ge(setup_v, 1)

                def product(dst, left, right, start=True, stop=True):
                    n = 0
                    for k in range(KT):
                        for h, g in ((HI, HI), (HI, LO), (LO, HI)):
                            n += 1
                            last = mm(dst, left(h, k), right(g, k), start=start and n == 1,
                                      stop=stop and n == 3 * KT, skip_group_check=True)
                    return last

                def transposes(src):
                    for h in (HI, LO):
                        for k in range(KT):
                            at = (h * KT + k) * TP
                            last = mm(p_t[:, at:at + TP], src[:, h, k * 128:(k + 1) * 128],
                                      eye_r[0:TOK, :], start=True, stop=True, skip_group_check=True)
                    return last

                def gradient(dst, left, right, l, first, first_bias):
                    for m in range(KT):
                        for h, g in ((HI, HI), (HI, LO), (LO, HI)):
                            mm(dst[:, m * D:(m + 1) * D], left[:, h, m * 128:(m + 1) * 128],
                               right[:, g, :], start=first, stop=True, skip_group_check=True)
                            first = False
                    for g in (HI, LO):
                        last = mm(p_gb[:, l * D:(l + 1) * D], ones[:, :], right[:, g, :],
                                  start=first_bias, stop=True, skip_group_check=True)
                        first_bias = False
                    return last

                def step(s):
                    known = isinstance(s.b, int)
                    if s.has(LAYER1):
                        pe.wait_ge(x1t_ready, s.n(LAYER1))
                        pe.wait_ge(q_copied, s.n(LAYER1))
                        x1t = x1_t[:, s.slot(LAYER1, 2)]
                        product(p_z1[0:TOK, 0:D], lambda h, k: x1t[:, h, k, 0:TOK],
                                lambda h, k: w_1[:, h, k, :], stop=False)
                        mm(p_z1[0:TOK, 0:D], bias_on[:, :], bias[:, 1, :], start=False, stop=True,
                           skip_group_check=True).then_inc(z1_filled, 1)
                    if s.has(X_T):
                        pe.wait_ge(xl_ready, s.n(X_T))
                        if s.has(X_T + 1):
                            pe.wait_ge(xt_ready, s.n(X_T + 1))
                        if s.has(LAYER0 + 1):
                            pe.wait_ge(x1t_ready, s.n(LAYER0 + 1))
                        transposes(xs[:, s.slot(X_T, 6)]).then_inc(xt_filled, 1)
                    if s.has(LAYER0):
                        xt = x_t[:, s.slot(LAYER0, 3)]
                        pe.wait_ge(xt_ready, s.n(LAYER0))
                        if s.has(LAYER0 + 1):
                            pe.wait_ge(x1_ready, s.n(LAYER0 + 1))
                        product(p_kz[0:TOK, :], lambda h, k: xt[:, h, k, 0:TOK],
                                lambda h, k: w_kz[:, h, k, :], stop=False)
                        mm(p_kz[0:TOK, D:2 * D], bias_on[:, :], bias[:, 0, :], start=False, stop=True,
                           skip_group_check=True).then_inc(kz_filled, 1)
                        if s.has(LAYER0 + 1):
                            pe.wait_ge(u_ready, s.n(LAYER0 + 1))
                        product(p_v[0:TOK, 0:D + 2], lambda h, k: xt[:, h, k, 0:TOK],
                                lambda h, k: w_v[:, h, k, :]).then_inc(v_filled, 1)
                        if s.has(LAYER1):
                            pe.wait_ge(s1_ready, s.n(LAYER1))
                        product(p_z1[0:TOK, D:2 * D], lambda h, k: xt[:, h, k, 0:TOK],
                                lambda h, k: w_q[:, h, k, :]).then_inc(q_filled, 1)
                    if s.has(BACK1):
                        dt = dz1_t[:, s.slot(BACK1, 2)]
                        pe.wait_ge(dz1t_ready, s.n(BACK1))
                        if s.has(BACK1 + 1):
                            pe.wait_ge(back_ready, s.n(BACK1 + 1))
                        product(p_dx[0:TOK, 0:D], lambda h, k: dt[:, h, k, 0:TOK],
                                lambda h, k: w_1t[:, h, k, :]).then_inc(dx_filled, 1)
                    if s.has(LAYER1):
                        pe.wait_ge(dz1l_ready, s.n(LAYER1))
                        if s.has(X_T):
                            pe.wait_ge(xt_ready, s.n(X_T))
                        else:
                            pe.wait_ge(x1t_ready, s.n(LAYER1))
                        transposes(dz1s[:, s.slot(LAYER1, 2)]).then_inc(dz1t_filled, 1)
                    if s.has(BACK1):
                        first = known and s.b * NJ + s.t == BACK1
                        gradient(p_g1, x1s[:, s.slot(BACK1, 3)], dz1s[:, s.slot(BACK1, 2)], 1,
                                 first, first).then_inc(g1_added, 1)
                    if s.has(LAYER0):
                        pe.wait_ge(x1l_ready, s.n(LAYER0))
                        if s.has(LAYER1):
                            pe.wait_ge(dz1t_ready, s.n(LAYER1))
                        elif s.has(X_T):
                            pe.wait_ge(xt_ready, s.n(X_T))
                        transposes(x1s[:, s.slot(LAYER0, 3)]).then_inc(x1t_filled, 1)
                    if s.has(GRAD0):
                        pe.wait_ge(dz0l_ready, s.n(GRAD0))
                        gradient(p_g0, xs[:, s.slot(GRAD0, 6)], dz0s[:, s.slot(GRAD0, 2)], 0,
                                 known and s.b * NJ + s.t == GRAD0, False).then_inc(g0_added, 1)

                gradient_steps(pe, step)

                pe.wait_ge(adam_v, 1)
                for m in range(KT):
                    for k in range(KT):
                        last = mm(p_kz[:, m * D:(m + 1) * D], raw_k[:, k, m * 128:(m + 1) * 128],
                                  g0_raw[:, k, :], start=(k == 0), stop=(k == KT - 1))
                last.then_inc(adam_t, 1)


def expert_weights(nc, w1, b1, g1, be1, m1, v1, w2, b2, g2, be2, m2, v2, wo, s_dram,
                   ffn_w, ffn_bias, eye, minus_half):
    RING = 4
    with ExitStack() as ctx:
        def sb(name, shape, dt=F32):
            return ctx.enter_context(nc.sbuf_tensor(name, shape, dt))

        def sem(name):
            return ctx.enter_context(nc.semaphore(name))

        par = sb("par", [KT * E, 2, 5, 128])
        bn_eps = sb("bn_eps", [KT * E, 128])
        scale = sb("scale", [KT * E, 2, 128])
        shift = sb("shift", [KT * E, 2, 128])
        scale_b = sb("scale_b", [128, 2, E, D])
        staged = sb("staged", [128, RING, KT, D])
        scaled = sb("scaled", [128, 2, KT, D])
        p_b = ctx.enter_context(nc.psum_tensor("p_b", [128, 2, KT * E], F32))

        par_loaded = sem("par_loaded")
        eps_set = sem("eps_set")
        pow_done = sem("pow_done")
        bn_v = sem("bn_v")
        bias_t = sem("bias_t")
        s_stored = sem("s_stored")
        s_loaded = sem("s_loaded")
        w_loaded = [sem(f"w_loaded{i}") for i in range(RING)]
        w_scaled = sem("w_scaled")
        w_high = sem("w_high")
        w_low = sem("w_low")
        jobs = [(i, e) for e in range(E) for i in range(3)]
        scales = [n for n, (i, e) in enumerate(jobs) if i < 2]

        def scaled_by(n):
            return sum(m <= n for m in scales)

        def source(n):
            return scaled[:, scales.index(n) % 2] if n in scales else staged[:, n % RING]

        with nc.Block() as block:
            @block.sync
            def _(sp):
                for l, arrays in enumerate(((g1, v1, b1, m1, be1), (g2, v2, b2, m2, be2))):
                    for i, a in enumerate(arrays):
                        sp.dma_start(par[:, l, i, :],
                                     a.rearrange("e (m p) -> (e m) p", p=128)).then_inc(par_loaded, 16)
                for n, (i, e) in enumerate(jobs):
                    if n == 1:
                        sp.wait_ge(bn_v, 4)
                        for l in range(2):
                            sp.dma_start(s_dram[l].rearrange("(r p) -> r p", p=128),
                                         scale[:, l, :]).then_inc(s_stored, 16)
                        sp.wait_ge(s_stored, 32)
                        for l in range(2):
                            sp.dma_start(scale_b[:, l].rearrange("p e n -> p (e n)"),
                                         s_dram[l:l + 1].broadcast_to([128, E * D])).then_inc(s_loaded, 16)
                    if n >= RING:
                        m = n - RING
                        if m in scales:
                            sp.wait_ge(w_scaled, scaled_by(m))
                        else:
                            sp.wait_ge(w_low, m + 1)
                    src = (w1, w2, wo)[i][e].rearrange("(k p) n -> p k n", p=128)
                    sp.dma_start(staged[:, n % RING], src).then_inc(w_loaded[n % RING], 16)

            @block.gpsimd
            def _(po):
                po.memset(bn_eps[:, :], BN_EPS).then_inc(eps_set, 1)
                for l in range(2):
                    po.wait_ge(bn_v, 2 * l + 1)
                    po.tensor_tensor(scale[:, l, :], par[:, l, 1, :], minus_half[0:KT * E, :],
                                     ALU.pow).then_inc(pow_done, 1)

            @block.vector
            def _(dve):
                count = [0]

                def link(ins):
                    count[0] += 1
                    ins.then_inc(bn_v, 1)
                    dve.wait_ge(bn_v, count[0])

                dve.wait_ge(par_loaded, 160)
                dve.wait_ge(eps_set, 1)
                for l in range(2):
                    link(nc.vector.tensor_tensor(par[:, l, 1, :], par[:, l, 1, :], bn_eps[:, :], ALU.add))
                    dve.wait_ge(pow_done, l + 1)
                    link(nc.vector.tensor_tensor(scale[:, l, :], scale[:, l, :], par[:, l, 0, :], ALU.mult))
                for l in range(2):
                    link(nc.vector.tensor_tensor(shift[:, l, :], par[:, l, 2, :], par[:, l, 3, :],
                                                 ALU.subtract))
                    link(nc.vector.tensor_tensor(shift[:, l, :], shift[:, l, :], scale[:, l, :], ALU.mult))
                    link(nc.vector.tensor_tensor(shift[:, l, :], shift[:, l, :], par[:, l, 4, :], ALU.add))
                dve.wait_ge(bias_t, 1)
                link(nc.vector.tensor_copy(ffn_bias[:, :, :], p_b[:, :, :]))
                dve.wait_ge(s_loaded, 32)

                def low(n):
                    i, e = jobs[n]
                    dve.wait_ge(w_high, n + 1)
                    nc.vector.tensor_tensor(ffn_w[i][:, e, LO], source(n), ffn_w[i][:, e, HI],
                                            ALU.subtract).then_inc(w_low, 1)

                for n, (i, e) in enumerate(jobs):
                    if i < 2:
                        s = scaled_by(n)
                        dve.wait_ge(w_loaded[n % RING], 16 * (n // RING + 1))
                        if s > 2:
                            dve.wait_ge(w_low, scales[s - 3] + 1)
                        nc.vector.tensor_tensor(scaled[:, (s - 1) % 2], staged[:, n % RING],
                                                scale_b[:, i, e, :].unsqueeze(1).broadcast_to([128, KT, D]),
                                                ALU.mult).then_inc(w_scaled, 1)
                    if n >= 1:
                        low(n - 1)
                low(len(jobs) - 1)

            @block.scalar
            def _(act):
                for n, (i, e) in enumerate(jobs):
                    if i < 2:
                        act.wait_ge(w_scaled, scaled_by(n))
                    else:
                        act.wait_ge(w_loaded[n % RING], 16 * (n // RING + 1))
                    nc.scalar.copy(ffn_w[i][:, e, HI], source(n)).then_inc(w_high, 1)

            @block.tensor
            def _(pe):
                pe.wait_ge(bn_v, 10)
                for l in range(2):
                    last = nc.tensor.transpose(p_b[:, l, :], shift[:, l, :], eye[0:KT * E, 0:KT * E])
                last.then_inc(bias_t, 1)


def block_sweep(nc, wr, br, bo, h_dram, q_dram, out, ffn_w, ffn_bias,
                eye, eye_r, bias_on, new_w, new_bias, minus_half, ln_eps):
    h_j = h_dram.rearrange("b (p j) d -> b j p d", j=NJ)
    q_j = q_dram.rearrange("b (p j) d -> b j p d", j=NJ)
    out_j = out.rearrange("b (p j) d -> j p b d", j=NJ)

    with ExitStack() as ctx:
        def sb(name, shape, dt=F32):
            return ctx.enter_context(nc.sbuf_tensor(name, shape, dt))

        def psum(name, shape):
            return ctx.enter_context(nc.psum_tensor(name, shape, F32))

        def sem(name):
            return ctx.enter_context(nc.semaphore(name))

        xt_new = sb("xt_new", [128, 2, KT, B, TOK], F32R)
        xt_use = sb("xt_use", [128, 2, KT, B, TOK], F32R)
        h1f = sb("h1f", [128, KT, NTOK])
        h1s = sb("h1s", [128, 2, KT, NTOK], F32R)
        h2f = sb("h2f", [128, KT, NTOK])
        h2s = sb("h2s", [128, 2, KT, NTOK], F32R)
        res = sb("res", [TOK, B, D])
        acc = sb("acc", [TOK, B, D])
        yb = sb("yb", [TOK, D])
        qin = sb("qin", [TOK, 4, D])
        hin = sb("hin", [TOK, 4, D])
        qs = sb("qs", [TOK, 2, D], F32R)
        q_t = sb("q_t", [128, 2, KT, TP], F32R)
        rsg = sb("rsg", [TOK, 2, D])
        rs = sb("rs", [TOK, D])
        q1 = sb("q1", [TOK, 3, D])
        q1s = sb("q1s", [TOK, 2, D], F32R)
        q1_t = sb("q1_t", [128, 2, KT, TP], F32R)
        xn2 = sb("xn2", [TOK, D])
        xn2s = sb("xn2s", [TOK, 2, D], F32R)
        stats = sb("stats2", [TOK, 6])
        mv = sb("mv2", [TOK, 2, 2])
        var_eps = sb("var_eps2", [TOK, 1])
        rstd = sb("rstd2", [TOK, 2, 1])
        raw_r = sb("raw_r", [128, KT, E])
        w_r = sb("w_r", [128, 2, KT, E], F32R)
        br_b = sb("br_b", [TOK, E])
        bo_s = sb("bo_s", [E, D])
        logit = sb("logit", [TOK, E])
        top = sb("top", [TOK, 1])
        sig = sb("sig", [TOK, 2, E])
        total = sb("total", [TOK, 1])
        gate_new = sb("gate_new", [TOK, E])
        gate = sb("gate", [TOK, E])
        gate_t = sb("gate_t", [E, TOK])

        p_1 = [psum(f"p_1{m}", [128, 512]) for m in range(KT)]
        p_2 = [psum(f"p_2{m}", [128, 512]) for m in range(KT)]
        p_3 = [psum(f"p_3{m}", [128, 2, D]) for m in range(2)]
        p_t = psum("p_t2", [128, 512])
        p_z = psum("p_z", [128, 512])

        const_loaded = sem("const_loaded")
        const_v = sem("const_v")
        q_loaded = [sem(f"q_loaded{i}") for i in range(4)]
        h_loaded = [sem(f"h_loaded{i}") for i in range(4)]
        qh_ready = sem("qh_ready")
        ql_ready = sem("ql_ready")
        qt_filled = sem("qt_filled")
        qt_ready = sem("qt_ready")
        za_filled = sem("za_filled")
        sga_ready = sem("sga_ready")
        sa_ready = sem("sa_ready")
        q1_ready = sem("q1_ready")
        q1h_ready = sem("q1h_ready")
        q1l_ready = sem("q1l_ready")
        q1t_filled = sem("q1t_filled")
        q1t_ready = sem("q1t_ready")
        zb_filled = sem("zb_filled")
        sgb_ready = sem("sgb_ready")
        sb_ready = sem("sb_ready")
        r_ready = sem("r_ready")
        res_ready = sem("res_ready")
        stat_ready = sem("stat_ready")
        mv_ready = sem("mv2_ready")
        eps_added = sem("eps2_added")
        rstd_ready = sem("rstd2_ready")
        xn_ready = sem("xn2_ready")
        xnh_ready = sem("xn2h_ready")
        xnl_ready = sem("xn2l_ready")
        xt_filled = sem("xt2_filled")
        xt_ready = sem("xt2_ready")
        logits_filled = sem("logits_filled")
        soft_v = sem("soft_v")
        sig_ready = sem("sig_ready")
        gate_t_filled = sem("gate_t_filled")
        gate_t_ready = sem("gate_t_ready")
        yb_filled = sem("yb_filled")
        yb_ready = sem("yb_ready")
        gate_ready = sem("gate_ready")
        acc_ready = sem("acc_ready")
        copied = [sem(f"copied{g}") for g in range(2)]
        l1_filled = sem("l1_filled")
        h1h_ready = sem("h1h_ready")
        h1l_ready = sem("h1l_ready")
        l2_filled = sem("l2_filled")
        h2h_ready = sem("h2h_ready")
        h2l_ready = sem("h2l_ready")
        l3_filled = sem("l3_filled")
        mixed = sem("mixed")
        out_stored = [sem(f"out_stored{g}") for g in range(2)]

        SOFT = 8

        def macros(engine, step):
            for J in (0, 1):
                for n in range(16):
                    step(Pace(J, n))
            with engine.Fori(2, NJ) as J:
                for n in range(16):
                    step(Pace(J, n))
            for n in range(16):
                step(Pace(NJ, n))
            for n in range(2):
                step(Pace(NJ + 1, n))

        def retrieves(s):
            return not isinstance(s.J, int) or s.J < NJ

        def col(J, shift):
            j = J + shift
            return slice(j, j + 1) if isinstance(j, int) else bass.ds(j, 1)

        with nc.Block() as block:
            @block.sync
            def _(sp):
                sp.dma_start(raw_r[:, :, :], wr.rearrange("(k p) n -> p k n", p=128)).then_inc(const_loaded, 16)
                sp.dma_start(br_b[:, :], br.rearrange("(a n) -> a n", a=1).broadcast_to([TOK, E])).then_inc(const_loaded, 16)
                sp.dma_start(bo_s[:, :], bo).then_inc(const_loaded, 16)

                def load(s, b):
                    if s.has_m(b - 4):
                        sp.wait_ge(q1_ready, s.m(b - 4))
                    sp.dma_start(qin[:, b % 4, :], q_j[b, col(s.J, 0)].rearrange("a p d -> p (a d)")
                                 ).then_inc(q_loaded[b % 4], 16)
                    if s.has_m(b - 4):
                        sp.wait_ge(res_ready, s.m(b - 4))
                    sp.dma_start(hin[:, b % 4, :], h_j[b, col(s.J, 0)].rearrange("a p d -> p (a d)")
                                 ).then_inc(h_loaded[b % 4], 16)

                def hand_over(s, g):
                    sp.wait_ge(xt_ready, s.m(GRP * g + GRP - 1))
                    if s.has():
                        sp.wait_ge(l1_filled, Pace(s.J, 8 * g + 7).n(0, 2))
                    at = slice(GRP * g, GRP * g + GRP)
                    sp.dma_start(xt_use[:, :, :, at, :].rearrange("p h k b t -> p (h k) (b t)").bitcast(F32),
                                 xt_new[:, :, :, at, :].rearrange("p h k b t -> p (h k) (b t)").bitcast(F32)
                                 ).then_inc(copied[g], 16)

                def store(s, g, shift):
                    sp.wait_ge(mixed, s.n(2, 4))
                    sp.dma_start(out_j[col(s.J, shift), :, GRP * g:GRP * g + GRP, :].rearrange("a p b d -> p (a b) d"),
                                 acc[:, GRP * g:GRP * g + GRP, :]).then_inc(out_stored[g], 16)

                def step(s):
                    if retrieves(s) and s.i < B:
                        load(s, s.i)
                    if s.i == 1 and s.has(2):
                        store(s, 1, -2)
                    if s.i == 9 and s.has(2):
                        store(s, 0, -1)
                    if retrieves(s) and s.i == 10:
                        hand_over(s, 0)
                    if retrieves(s) and s.i == 15:
                        hand_over(s, 1)

                macros(sp, step)
                for g in range(2):
                    sp.wait_ge(out_stored[g], 16 * NJ)

            @block.gpsimd
            def _(po):
                def step(s):
                    if s.has() and s.i in (1, 3):
                        g = s.i // 2
                        po.wait_ge(yb_ready, s.J)
                        if s.has(16):
                            po.wait_ge(out_stored[g], s.J * 16 - 16)
                        for b in range(GRP * g, GRP * g + GRP):
                            po.tensor_tensor(acc[:, b, :], res[:, b, :], yb[:, :], ALU.add).then_inc(acc_ready, 1)
                    b = s.tile(4)
                    if b is not None:
                        po.wait_ge(mv_ready, s.m(b))
                        po.tensor_tensor(var_eps[:, :], mv[:, b % 2, 1:2], ln_eps[0:TOK, :],
                                         ALU.add).then_inc(eps_added, 1)
                        po.wait_ge(eps_added, s.m(b))
                        if s.has_m(b - 2):
                            po.wait_ge(xn_ready, s.m(b - 2))
                        po.tensor_tensor(rstd[:, b % 2, :], var_eps[:, :], minus_half[0:TOK, 0:1],
                                         ALU.pow).then_inc(rstd_ready, 1)

                macros(po, step)

            @block.scalar
            def _(act):
                def evacuate(dst, bank, filled, ready):
                    pass

                def relu(s, lag, bank, layer, full, parts, filled, reader, low, high):
                    for m in range(KT):
                        c = m + KT * s.expert(lag)
                        bias = ffn_bias[:, layer, c:c + 1]
                        act.wait_ge(filled, s.n(lag, 2) - (KT - 1 - m))
                        if s.has(lag + 1):
                            act.wait_ge(low, s.n(lag + 1, 2) - (KT - 1 - m))
                        nc.scalar.activation(full[:, m, :], bank[m][:, 0:NTOK], ACT.Relu, bias=bias)
                        if m == 0 and s.has(lag + 1):
                            act.wait_ge(*reader)
                        nc.scalar.activation(parts[:, HI, m, :], bank[m][:, 0:NTOK], ACT.Relu,
                                             bias=bias).then_inc(high, 1)

                def step(s):
                    b = s.tile(2)
                    if b is not None:
                        act.wait_ge(za_filled, s.m(b))
                        if s.has_m(b - 1):
                            act.wait_ge(sa_ready, s.m(b - 1))
                        nc.scalar.activation(rsg[:, 0, :], p_z[0:TOK, 0:D], ACT.Sigmoid).then_inc(sga_ready, 1)
                    b = s.tile(1)
                    if b is not None:
                        act.wait_ge(qt_filled, s.m(b))
                        if s.has_m(b - 1):
                            act.wait_ge(za_filled, s.m(b - 1))
                        nc.scalar.copy(q_t[:, :, :, :].rearrange("p h k t -> p (h k t)"),
                                       p_t[:, 0:4 * TP]).then_inc(qt_ready, 1)
                    b = s.tile(0)
                    if b is not None:
                        act.wait_ge(q_loaded[b % 4], s.J * 32 + 16 * (b // 4 + 1))
                        if s.has_m(b - 1):
                            act.wait_ge(qt_filled, s.m(b - 1))
                        nc.scalar.copy(qs[:, HI, :], qin[:, b % 4, :]).then_inc(qh_ready, 1)
                    b = s.tile(6)
                    if b is not None:
                        act.wait_ge(xt_filled, s.m(b))
                        if b % GRP == 0 and s.has_m(b - 8):
                            act.wait_ge(copied[b // GRP], s.J * 16)
                        if b == 0 and s.has_m(b - 8):
                            act.wait_ge(logits_filled, s.J)
                        nc.scalar.copy(xt_new[:, :, :, b, :].rearrange("p h k t -> p (h k) t"),
                                       p_t[:, 0:4 * TP].rearrange("p (c t) -> p c t", t=TP)[:, :, 0:TOK]
                                       ).then_inc(xt_ready, 1)
                    if s.has(1):
                        relu(s, 1, p_2, 1, h2f, h2s, l2_filled, (l3_filled, s.n(2, 2)), h2l_ready, h2h_ready)
                    b = s.tile(4)
                    if b is not None:
                        act.wait_ge(zb_filled, s.m(b))
                        if s.has_m(b - 1):
                            act.wait_ge(sb_ready, s.m(b - 1))
                        nc.scalar.activation(rsg[:, 1, :], p_z[0:TOK, 0:D], ACT.Sigmoid).then_inc(sgb_ready, 1)
                    b = s.tile(3)
                    if b is not None:
                        act.wait_ge(q1t_filled, s.m(b))
                        if s.has_m(b - 1):
                            act.wait_ge(zb_filled, s.m(b - 1))
                        nc.scalar.copy(q1_t[:, :, :, :].rearrange("p h k t -> p (h k t)"),
                                       p_t[:, 0:4 * TP]).then_inc(q1t_ready, 1)
                    b = s.tile(2)
                    if b is not None:
                        act.wait_ge(q1_ready, s.m(b))
                        if s.has_m(b - 1):
                            act.wait_ge(q1t_filled, s.m(b - 1))
                        nc.scalar.copy(q1s[:, HI, :], q1[:, b % 3, :]).then_inc(q1h_ready, 1)
                    if s.has(0):
                        relu(s, 0, p_1, 0, h1f, h1s, l1_filled, (l2_filled, s.n(1, 2)), h1l_ready, h1h_ready)
                    b = s.tile(5)
                    if b is not None:
                        act.wait_ge(xn_ready, s.m(b))
                        if s.has_m(b - 1):
                            act.wait_ge(xt_filled, s.m(b - 1))
                        nc.scalar.copy(xn2s[:, HI, :], xn2[:, :]).then_inc(xnh_ready, 1)
                    if retrieves(s) and s.i == 14:
                        act.wait_ge(soft_v, s.J * SOFT + 3)
                        nc.scalar.activation(sig[:, 0, :], logit[:, :], ACT.Sigmoid)
                        nc.scalar.activation(sig[:, 1, :], logit[:, :], ACT.Sigmoid,
                                             scale=-1.0).then_inc(sig_ready, 1)

                macros(act, step)

            @block.vector
            def _(dve):
                dve.wait_ge(const_loaded, 48)
                nc.vector.tensor_copy(w_r[:, HI], raw_r[:, :, :]).then_inc(const_v, 1)
                dve.wait_ge(const_v, 1)
                nc.vector.tensor_tensor(w_r[:, LO], raw_r[:, :, :], w_r[:, HI], ALU.subtract).then_inc(const_v, 1)

                def mix(s, half):
                    e, g = s.expert(2), s.group(2)
                    dve.wait_ge(l3_filled, s.n(2, 2) - (1 - half))
                    for t in range(2):
                        b = GRP * g + 2 * half + t
                        if e == 0:
                            dve.wait_ge(acc_ready, s.J * B + (b + 1 - B - (B if s.i < 2 else 0)))
                        else:
                            dve.wait_ge(mixed, s.n(3, 4) - (3 - 2 * half - t))
                        nc.vector.scalar_tensor_tensor(out=acc[:, b, :], in0=p_3[half][0:TOK, t, :],
                                                       scalar=gate[:, e:e + 1], in1=acc[:, b, :],
                                                       op0=ALU.mult, op1=ALU.add).then_inc(mixed, 1)

                def low(s, lag, full, parts, high, low_):
                    for m in range(KT):
                        dve.wait_ge(high, s.n(lag, 2) - (KT - 1 - m))
                        nc.vector.tensor_tensor(parts[:, LO, m, :], full[:, m, :], parts[:, HI, m, :],
                                                ALU.subtract).then_inc(low_, 1)

                def soft(k, s, ins):
                    ins.then_inc(soft_v, 1)
                    dve.wait_ge(soft_v, s.J * SOFT + k)

                def step(s):
                    if s.has(2) and s.i == 2:
                        dve.wait_ge(soft_v, s.J * SOFT)
                        if s.has(3):
                            dve.wait_ge(mixed, s.n(3, 4))
                        nc.vector.tensor_copy(gate[:, :], gate_new[:, :]).then_inc(gate_ready, 1)
                        dve.wait_ge(gate_ready, s.J)
                    if s.has(2):
                        mix(s, 0)
                    if s.has(0) and s.i == 0:
                        dve.wait_ge(yb_filled, s.J)
                        if s.has(16):
                            dve.wait_ge(acc_ready, s.J * B - B)
                        nc.vector.tensor_copy(yb[:, :], p_z[0:TOK, 0:D]).then_inc(yb_ready, 1)
                    b = s.tile(2)
                    if b is not None:
                        if s.has_m(max(b - 3, -1)):
                            dve.wait_ge(r_ready, s.m(max(b - 3, -1)))
                        dve.wait_ge(sga_ready, s.m(b))
                        nc.vector.tensor_tensor(rs[:, :], p_z[0:TOK, 0:D], rsg[:, 0, :],
                                                ALU.mult).then_inc(sa_ready, 1)
                        dve.wait_ge(sa_ready, s.m(b))
                        nc.vector.tensor_tensor(q1[:, b % 3, :], qin[:, b % 4, :], rs[:, :],
                                                ALU.add).then_inc(q1_ready, 1)
                    if s.has(2):
                        mix(s, 1)
                    b = s.tile(0)
                    if b is not None:
                        dve.wait_ge(qh_ready, s.m(b))
                        nc.vector.tensor_tensor(qs[:, LO, :], qin[:, b % 4, :], qs[:, HI, :],
                                                ALU.subtract).then_inc(ql_ready, 1)
                    if s.has(1):
                        low(s, 1, h2f, h2s, h2h_ready, h2l_ready)
                    b = s.tile(4)
                    if b is not None:
                        dve.wait_ge(q1_ready, s.m(min(b + 2, B - 1)))
                        dve.wait_ge(sgb_ready, s.m(b))
                        nc.vector.tensor_tensor(rs[:, :], p_z[0:TOK, 0:D], rsg[:, 1, :],
                                                ALU.mult).then_inc(sb_ready, 1)
                        dve.wait_ge(sb_ready, s.m(b))
                        if s.has_m(b - 8) and s.has():
                            dve.wait_ge(acc_ready, s.J * B + (b + 1 - B))
                        nc.vector.tensor_tensor(res[:, b, :], q1[:, b % 3, :], rs[:, :],
                                                ALU.add).then_inc(r_ready, 1)
                        dve.wait_ge(r_ready, s.m(b))
                        dve.wait_ge(h_loaded[b % 4], s.J * 32 + 16 * (b // 4 + 1))
                        nc.vector.tensor_tensor(res[:, b, :], hin[:, b % 4, :], res[:, b, :],
                                                ALU.add).then_inc(res_ready, 1)
                        dve.wait_ge(res_ready, s.m(b))
                        nc.vector.bn_stats(stats[:, :], res[:, b, :]).then_inc(stat_ready, 1)
                    b = s.tile(2)
                    if b is not None:
                        dve.wait_ge(q1h_ready, s.m(b))
                        nc.vector.tensor_tensor(q1s[:, LO, :], q1[:, b % 3, :], q1s[:, HI, :],
                                                ALU.subtract).then_inc(q1l_ready, 1)
                    b = s.tile(5)
                    if b is not None:
                        dve.wait_ge(rstd_ready, s.m(b))
                        if s.has_m(b - 1):
                            dve.wait_ge(xnl_ready, s.m(b - 1))
                        nc.vector.tensor_scalar(xn2[:, :], res[:, b, :], mv[:, b % 2, 0:1], rstd[:, b % 2, :],
                                                ALU.subtract, ALU.mult).then_inc(xn_ready, 1)
                    b4 = s.tile(4)
                    if b4 is not None:
                        dve.wait_ge(stat_ready, s.m(b4))
                    if s.has(0):
                        low(s, 0, h1f, h1s, h1h_ready, h1l_ready)
                    if b4 is not None:
                        nc.vector.bn_aggr(mv[:, b4 % 2, :], stats[:, :]).then_inc(mv_ready, 1)
                    if b is not None:
                        dve.wait_ge(xnh_ready, s.m(b))
                        nc.vector.tensor_tensor(xn2s[:, LO, :], xn2[:, :], xn2s[:, HI, :],
                                                ALU.subtract).then_inc(xnl_ready, 1)
                    if retrieves(s) and s.i == 14:
                        dve.wait_ge(logits_filled, s.J + 1)
                        soft(1, s, nc.vector.scalar_tensor_tensor(out=logit[:, :], in0=p_z[0:TOK, 0:E],
                                                                  scalar=1.0 / B, in1=br_b[:, :],
                                                                  op0=ALU.mult, op1=ALU.add))
                        soft(2, s, nc.vector.reduce_max(top[:, :], logit[:, :], AX_X))
                        soft(3, s, nc.vector.tensor_scalar(logit[:, :], logit[:, :], top[:, :], None,
                                                           ALU.subtract))
                        dve.wait_ge(sig_ready, s.J + 1)
                        soft(4, s, nc.vector.reciprocal(sig[:, 1, :], sig[:, 1, :]))
                        soft(5, s, nc.vector.tensor_tensor(logit[:, :], sig[:, 0, :], sig[:, 1, :], ALU.mult))
                        soft(6, s, nc.vector.reduce_sum(total[:, :], logit[:, :], AX_X))
                        soft(7, s, nc.vector.reciprocal(total[:, :], total[:, :]))
                        soft(8, s, nc.vector.tensor_scalar(gate_new[:, :], logit[:, :], total[:, :], None,
                                                           ALU.mult))
                    if retrieves(s) and s.i == 15:
                        dve.wait_ge(gate_t_filled, s.J + 1)
                        nc.vector.tensor_copy(gate_t[:, :], p_z[0:E, 0:TOK]).then_inc(gate_t_ready, 1)

                macros(dve, step)

            @block.tensor
            def _(pe):
                mm = nc.tensor.matmul

                def product(dst, left, right, start=True, stop=True):
                    n = 0
                    for k in range(KT):
                        for h, g in ((HI, HI), (HI, LO), (LO, HI)):
                            n += 1
                            last = mm(dst, left(h, k), right(g, k), start=start and n == 1,
                                      stop=stop and n == 3 * KT, skip_group_check=True)
                    return last

                def transposes(src):
                    for h in (HI, LO):
                        for k in range(KT):
                            at = (h * KT + k) * TP
                            last = mm(p_t[:, at:at + TP], src[:, h, k * 128:(k + 1) * 128],
                                      eye_r[0:TOK, :], start=True, stop=True, skip_group_check=True)
                    return last

                def layer(s, lag, bank, w, rhs, filled):
                    e = s.expert(lag)
                    for m in range(KT):
                        cols = slice(m * 128, (m + 1) * 128)
                        product(bank[m][:, 0:NTOK], lambda h, k: w[:, e, h, k, cols], rhs).then_inc(filled, 1)

                def layer3(s, half):
                    e = s.expert(2)
                    if s.has(3):
                        pe.wait_ge(mixed, s.n(3, 4) - 2 * (1 - half))
                    for t in range(2):
                        at = (2 * half + t) * TOK
                        last = product(p_3[half][0:TOK, t, :], lambda h, k: h2s[:, h, k, at:at + TOK],
                                       lambda h, k: ffn_w[2][:, e, h, k, :])
                    last.then_inc(l3_filled, 1)

                def retrieval_layer(l, src, filled):
                    product(p_z[0:TOK, 0:D], lambda h, k: src[:, h, k, 0:TOK],
                            lambda h, k: new_w[:, l, h, k, :], stop=False)
                    mm(p_z[0:TOK, 0:D], bias_on[:, :], new_bias[:, l, :], start=False, stop=True,
                       skip_group_check=True).then_inc(filled, 1)

                def step(s):
                    if s.has(2):
                        pe.wait_ge(h2l_ready, s.n(2, 2))
                        layer3(s, 0)
                    if s.has(0) and s.i == 0:
                        pe.wait_ge(gate_t_ready, s.J)
                        mm(p_z[0:TOK, 0:D], gate_t[:, :], bo_s[:, :], start=True,
                           stop=True).then_inc(yb_filled, 1)
                    b = s.tile(2)
                    if b is not None:
                        pe.wait_ge(qt_ready, s.m(b))
                        if b == 0:
                            if s.has_m(b - 8):
                                pe.wait_ge(yb_ready, s.J)
                        elif b < 3:
                            pe.wait_ge(sa_ready, s.m(b - 1))
                        else:
                            pe.wait_ge(sb_ready, s.m(b - 3))
                        retrieval_layer(0, q_t, za_filled)
                    b = s.tile(1)
                    if b is not None:
                        pe.wait_ge(ql_ready, s.m(b))
                        if b >= 3:
                            pe.wait_ge(q1t_ready, s.m(b - 3))
                        elif b >= 1:
                            pe.wait_ge(qt_ready, s.m(b - 1))
                        elif s.has_m(-1):
                            pe.wait_ge(xt_ready, s.m(-1))
                        transposes(qs).then_inc(qt_filled, 1)
                    if s.has(2):
                        layer3(s, 1)
                    b = s.tile(6)
                    if b is not None:
                        pe.wait_ge(xnl_ready, s.m(b))
                        if b + 5 < B:
                            pe.wait_ge(qt_ready, s.m(b + 5))
                        elif b + 2 < B:
                            pe.wait_ge(q1t_ready, s.m(b + 2))
                        else:
                            pe.wait_ge(xt_ready, s.m(b - 1))
                        transposes(xn2s[:, :, :]).then_inc(xt_filled, 1)
                    if s.has(1):
                        pe.wait_ge(h1l_ready, s.n(1, 2))
                        if s.has(2):
                            pe.wait_ge(h2h_ready, s.n(2, 2))
                        layer(s, 1, p_2, ffn_w[1], lambda h, k: h1s[:, h, k, :], l2_filled)
                    b = s.tile(4)
                    if b is not None:
                        pe.wait_ge(q1t_ready, s.m(b))
                        if b + 2 < B:
                            pe.wait_ge(sa_ready, s.m(b + 2))
                        else:
                            pe.wait_ge(sb_ready, s.m(b - 1))
                        retrieval_layer(1, q1_t, zb_filled)
                    b = s.tile(3)
                    if b is not None:
                        pe.wait_ge(q1l_ready, s.m(b))
                        if b >= 3:
                            pe.wait_ge(xt_ready, s.m(b - 3))
                        else:
                            pe.wait_ge(qt_ready, s.m(b + 2))
                        transposes(q1s).then_inc(q1t_filled, 1)
                    if s.has(0):
                        g = s.group(0)
                        if s.i % E == 0:
                            pe.wait_ge(copied[g], s.J * 16)
                        if s.has(1):
                            pe.wait_ge(h1h_ready, s.n(1, 2))
                        at = slice(GRP * g, GRP * g + GRP)
                        layer(s, 0, p_1, ffn_w[0],
                              lambda h, k: xt_use[:, h, k, at, :].rearrange("p b t -> p (b t)"), l1_filled)
                    if retrieves(s) and s.i == 13:
                        pe.wait_ge(xt_ready, s.m(B - 1))
                        pe.wait_ge(sb_ready, s.m(B - 1))
                        pe.wait_ge(const_v, 2)
                        for b in range(B):
                            last = product(p_z[0:TOK, 0:E], lambda h, k: xt_new[:, h, k, b, :],
                                           lambda h, k: w_r[:, h, k, :], start=(b == 0), stop=(b == B - 1))
                        last.then_inc(logits_filled, 1)
                    if retrieves(s) and s.i == 15:
                        pe.wait_ge(soft_v, (s.J + 1) * SOFT)
                        nc.tensor.transpose(p_z[0:E, 0:TOK], gate_new[:, :],
                                            eye[0:TOK, 0:TOK]).then_inc(gate_t_filled, 1)

                macros(pe, step)


_INS = ['x', 'L0_tok_blur_kernel', 'L0_attn_Wk', 'L0_attn_Wq', 'L0_attn_Wv', 'L0_attn_Wlr', 'L0_attn_blr',
        'L0_attn_Ws', 'L0_attn_bs', 'L0_ffn_Wr', 'L0_ffn_br', 'L0_ffn_W1', 'L0_ffn_b1', 'L0_ffn_g1',
        'L0_ffn_be1', 'L0_ffn_m1', 'L0_ffn_v1', 'L0_ffn_W2', 'L0_ffn_b2', 'L0_ffn_g2', 'L0_ffn_be2',
        'L0_ffn_m2', 'L0_ffn_v2', 'L0_ffn_Wo', 'L0_ffn_bo']
_OUTS = [((B, TOKENS, D), 'float32')]


def kernel(**inputs):
    import numpy as _np
    import concourse.bacc as _bacc
    from concourse import mybir as _mybir
    from concourse.bass_utils import run_bass_kernel_spmd as _run

    nc = _bacc.Bacc("TRN2", target_bir_lowering=False, num_devices=1)
    arrays, args = {}, []
    for name in _INS:
        a = _np.ascontiguousarray(inputs[name])
        arrays[f"in_{name}_dram"] = a
        args.append(nc.dram_tensor(f"in_{name}_dram", a.shape, _mybir.dt.from_np(a.dtype), kind="ExternalInput").ap())
    for i, (shape, dtype) in enumerate(_OUTS):
        dt = _mybir.dt.from_np(_np.dtype(dtype))
        args.append(nc.dram_tensor(f"out_{i}_dram", shape, dt, kind="ExternalOutput").ap())
    audio_tower(nc, *args)
    r = _run(nc, [arrays], core_ids=[0])
    got = tuple(r.results[0][f"out_{i}_dram"] for i in range(len(_OUTS)))
    return got[0]
```

```python
from contextlib import ExitStack

import concourse.bass as bass
from concourse import mybir

F32 = mybir.dt.float32
F32R = mybir.dt.float32r
ALU = mybir.AluOpType
ACT = mybir.ActivationFunctionType
AX_X = mybir.AxisListType.X

B = 8
D = 256
KT = D // 128
TOK = 125
NJ = 12
TILES = B * NJ
TOKENS = NJ * TOK
CH = 4
CHUNKS = NJ // CH
E = 8
GRP = 4
NTOK = GRP * TOK
TP = TOK + 1
HI, LO = 0, 1

LR, WD, ADAM_EPS, MAX_ALR = 0.001, 0.01, 1e-8, 0.1
LN_EPS, BN_EPS = 1e-5, 1e-3
GRAD_SCALE = MAX_ALR * 2.0 / D

POOL, STATS, AGGR, RSTD, NORM, X_T, LAYER0, LAYER1, BACK1, GRAD0 = -1, 1, 2, 2, 3, 4, 5, 6, 7, 8


class Step:

    def __init__(self, b, t):
        self.b, self.t = b, t

    def has(self, lag):
        return not isinstance(self.b, int) or 0 <= NJ * self.b + self.t - lag < TILES

    def n(self, lag):
        return self.b * NJ + (self.t - lag + 1)

    def slot(self, lag, ring):
        return (self.t - lag) % ring

    def chunk(self, lag):
        return (self.t - lag) // CH

    def part(self, lag):
        return (self.t - lag) % CH


class Pace:

    def __init__(self, J, n):
        self.J, self.i = J, n

    def has(self, lag=0):
        return not isinstance(self.J, int) or 0 <= 16 * (self.J - 1) + self.i - lag < 16 * NJ

    def n(self, lag=0, per=1):
        return self.J * (16 * per) + per * (self.i - lag + 1 - 16)

    def expert(self, lag=0):
        return (self.i - lag) % E

    def group(self, lag=0):
        return (self.i - lag) // E % 2

    def tile(self, lag):
        b = self.i - lag
        return b if 0 <= b < B and not (isinstance(self.J, int) and self.J >= NJ) else None

    def m(self, b, per=1):
        return self.J * (B * per) + (b + 1) * per

    def has_m(self, b):
        return not isinstance(self.J, int) or self.J * B + b >= 0


def audio_tower(nc, x, blur, wk, wq, wv, wlr, blr, ws, bs, wr, br, w1, b1, g1, be1, m1, v1,
                w2, b2, g2, be2, m2, v2, wo, bo, out):
    h_dram = nc.dram_tensor("h_dram", (B, TOKENS, D), F32, kind="Internal").ap()
    q_dram = nc.dram_tensor("q_dram", (B, TOKENS, D), F32, kind="Internal").ap()

    with ExitStack() as keep:
        def sb_keep(name, shape, dt=F32):
            return keep.enter_context(nc.sbuf_tensor(name, shape, dt))

        eye = sb_keep("eye", [128, 128])
        eye_r = sb_keep("eye_r", [128, TP], F32R)
        bias_on = sb_keep("bias_on", [128, TOK], F32R)
        new_w = sb_keep("new_w", [128, 2, 2, KT, D], F32R)
        new_bias = sb_keep("new_bias", [128, 2, D], F32R)
        minus_half = sb_keep("minus_half", [128, 128])
        ln_eps = sb_keep("ln_eps", [128, 1])

        bn_scale = sb_keep("bn_scale", [128, 2, KT * E])
        bn_shift = sb_keep("bn_shift", [128, 2, KT * E])

        gradient_sweep(nc, x, blur, wk, wq, wv, wlr, blr, ws, bs,
                       (g1, v1, b1, m1, be1), (g2, v2, b2, m2, be2), h_dram, q_dram,
                       eye, eye_r, bias_on, new_w, new_bias, minus_half, ln_eps, bn_scale, bn_shift)
        with ExitStack() as ex:
            def sb_ex(name, shape, dt=F32):
                return ex.enter_context(nc.sbuf_tensor(name, shape, dt))
            ffn_w = [sb_ex(f"ffn_w{i}", [128, E, 2, KT, D], F32R) for i in range(3)]
            block_sweep(nc, wr, br, (w1, w2, wo), bo, h_dram, q_dram, out, ffn_w, bn_scale, bn_shift,
                        eye, eye_r, bias_on, new_w, new_bias, minus_half, ln_eps)


def gradient_sweep(nc, x, blur, wk, wq, wv, wlr, blr, ws, bs, norm1, norm2, h_dram, q_dram,
                   eye, eye_r, bias_on, new_w, new_bias, minus_half, ln_eps, bn_scale, bn_shift):
    x_rows = x.rearrange("b (p r) d -> b p (r d)", r=2 * NJ)
    h_tok = h_dram.rearrange("b (p j) d -> b p (j d)", j=NJ)
    q_tok = q_dram.rearrange("b (p j) d -> b p (j d)", j=NJ)

    with ExitStack() as ctx:
        def sb(name, shape, dt=F32):
            return ctx.enter_context(nc.sbuf_tensor(name, shape, dt))

        def psum(name, shape):
            return ctx.enter_context(nc.psum_tensor(name, shape, F32))

        def sem(name):
            return ctx.enter_context(nc.semaphore(name))

        raw_k = sb("raw_k", [128, KT, D])
        raw_w = sb("raw_w", [128, 2, KT, D])
        raw_lr = sb("raw_lr", [128, KT, 2])
        raw_b = sb("raw_b", [33, 2, D])
        raw_q = sb("raw_q", [128, KT, D])
        raw_v = sb("raw_v", [128, KT, D])
        wk_t = sb("wk_t", [128, KT, D])
        w_kz = sb("w_kz", [128, 2, KT, 2 * D], F32R)
        w_v = sb("w_v", [128, 2, KT, D + 2], F32R)
        w_q = sb("w_q", [128, 2, KT, D], F32R)
        w_1 = sb("w_1", [128, 2, KT, D], F32R)
        w_1t = sb("w_1t", [128, 2, KT, D], F32R)
        bias_h = sb("bias_h", [33, 2, D], F32R)
        bias_l = sb("bias_l", [33, 2, D], F32R)
        bias = sb("bias", [128, 2, D], F32R)
        rate_bias = sb("rate_bias", [TOK, 1])
        table_in = sb("table_in", [TOK, 1])
        ones = sb("ones", [TOK, 128], F32R)
        blur_w = sb("blur_w", [TOK, 3, D])
        blur_end = sb("blur_end", [TOK, D])

        rows = sb("rows", [TOK, 2 * NJ + 2, D])
        pool = sb("pool", [TOK, 9, D])
        tap1 = sb("tap1", [TOK, D])
        tap2 = sb("tap2", [TOK, D])
        hbuf = sb("hbuf", [TOK, CHUNKS, CH, D])
        qbuf = sb("qbuf", [TOK, 3, D])
        stats = sb("stats", [TOK, 2, 6])
        mv = sb("mv", [TOK, 2, 2])
        var_eps = sb("var_eps", [TOK, 2, 1])
        rstd = sb("rstd", [TOK, 2, 1])
        shift = sb("shift", [TOK, 2, 1])
        xn = sb("xn", [TOK, 2, D])
        xs = sb("xs", [TOK, 6, 2, D], F32R)
        x_t = sb("x_t", [128, 3, 2, KT, TP], F32R)
        sg0 = sb("sg0", [TOK, 2, D])
        s0 = sb("s0", [TOK, 2, D])
        m0 = sb("m0", [TOK, 2, D])
        f0 = sb("f0", [TOK, 4, D])
        x1 = sb("x1", [TOK, 2, D])
        x1s = sb("x1s", [TOK, 3, 2, D], F32R)
        x1_t = sb("x1_t", [128, 2, 2, KT, TP], F32R)
        u = sb("u", [TOK, 2, D])
        sg1 = sb("sg1", [TOK, 2, D])
        rate = sb("rate", [TOK, 4, 1])
        s1 = sb("s1", [TOK, 2, D])
        m1 = sb("m1", [TOK, 2, D])
        f1 = sb("f1", [TOK, 2, D])
        diff = sb("diff", [TOK, 2, D])
        dz1 = sb("dz1", [TOK, 2, D])
        dz1s = sb("dz1s", [TOK, 2, 2, D], F32R)
        dz1_t = sb("dz1_t", [128, 2, 2, KT, TP], F32R)
        back = sb("back", [TOK, 2, D])
        dz0 = sb("dz0", [TOK, 2, D])
        dz0s = sb("dz0s", [TOK, 2, 2, D], F32R)
        dz_sum = sb("dz_sum", [TOK, 2, D])
        dz_sums = sb("dz_sums", [TOK, 2, 2, D], F32R)
        g0_raw = sb("g0_raw", [128, KT, D])
        par = rows[0:KT * E, 0:5, :].rearrange("p a (b n) -> p (a b) n", n=128)
        par_t = sb("par_t", [128, 10, KT * E])
        bn_eps = sb("bn_eps", [128, 2, KT * E])

        p_t = psum("p_t", [128, 512])
        p_kz = psum("p_kz", [128, 512])
        p_v = psum("p_v", [128, 512])
        p_z1 = psum("p_z1", [128, 512])
        p_dx = psum("p_dx", [128, 512])
        p_g0 = psum("p_g0", [128, 512])
        p_g1 = psum("p_g1", [128, 512])
        p_tz = psum("p_tz", [128, 512])

        loaded = sem("loaded")
        kw_loaded = sem("kw_loaded")
        w_high = sem("w_high")
        w_low = sem("w_low")
        consts = sem("consts")
        eye_zero = sem("eye_zero")
        setup_t = sem("setup_t")
        setup_v = sem("setup_v")
        wk_t_done = sem("wk_t_done")
        kw0_filled = sem("kw0_filled")
        taps_loaded = sem("taps_loaded")
        x_loaded = [sem(f"x_loaded{c}") for c in range(CHUNKS)]
        pooled = sem("pooled")
        tok_ops = sem("tok_ops")
        h_stored = [sem(f"h_stored{c}") for c in range(CHUNKS)]
        q_stored = [sem(f"q_stored{r}") for r in range(3)]
        stats_ready = sem("stats_ready")
        mv_ready = sem("mv_ready")
        eps_added = sem("eps_added")
        rstd_ready = sem("rstd_ready")
        shift_ready = sem("shift_ready")
        xn_ready = sem("xn_ready")
        xl_ready = sem("xl_ready")
        xt_filled = sem("xt_filled")
        xt_ready = sem("xt_ready")
        kz_filled = sem("kz_filled")
        v_filled = sem("v_filled")
        q_filled = sem("q_filled")
        rate_ready = sem("rate_ready")
        sg0_ready = sem("sg0_ready")
        s0_ready = sem("s0_ready")
        x1_ready = sem("x1_ready")
        m0_ready = sem("m0_ready")
        f0_ready = sem("f0_ready")
        q_copied = sem("q_copied")
        u_ready = sem("u_ready")
        x1h_ready = sem("x1h_ready")
        x1l_ready = sem("x1l_ready")
        x1t_filled = sem("x1t_filled")
        x1t_ready = sem("x1t_ready")
        z1_filled = sem("z1_filled")
        sg1_ready = sem("sg1_ready")
        s1_ready = sem("s1_ready")
        m1_ready = sem("m1_ready")
        f1_ready = sem("f1_ready")
        diff_ready = sem("diff_ready")
        dz1_ready = sem("dz1_ready")
        dz1h_ready = sem("dz1h_ready")
        dz1l_ready = sem("dz1l_ready")
        dz1t_filled = sem("dz1t_filled")
        dz1t_ready = sem("dz1t_ready")
        dx_filled = sem("dx_filled")
        g1_added = sem("g1_added")
        back_ready = sem("back_ready")
        dz0_ready = sem("dz0_ready")
        dz0h_ready = sem("dz0h_ready")
        dz0l_ready = sem("dz0l_ready")
        g0_added = sem("g0_added")
        summed1 = sem("summed1")
        summed0 = sem("summed0")
        sumh_ready = sem("sumh_ready")
        suml_ready = sem("suml_ready")
        gb_filled = sem("gb_filled")
        par_loaded = sem("par_loaded")
        par_filled = sem("par_filled")
        par_ready = sem("par_ready")
        bn_done = sem("bn_done")
        g0_copied = sem("g0_copied")
        grad_scaled = sem("grad_scaled")
        new_ready = sem("new_ready")
        newh_ready = sem("newh_ready")
        adam_v = sem("adam_v")
        adam_t = sem("adam_t")

        LOADS = 9
        TOK_OPS = 5

        def two(psum_bank):
            return psum_bank[:, :].rearrange("p (k n) -> p k n", k=KT)

        weight_parts = [(w[:, HI, :, lo:hi], w[:, LO, :, lo:hi], src) for w, lo, hi, src in (
            (w_kz, 0, D, raw_k[:, :, :]), (w_1, 0, D, raw_w[:, 1]), (w_v, 0, D, raw_v[:, :, :]),
            (w_q, 0, D, raw_q[:, :, :]), (w_v, D, D + 2, raw_lr[:, :, :]))]
        weight_parts.append((bias_h[:, :, :], bias_l[:, :, :], raw_b[:, :, :]))
        weight_parts += [(w[:, HI, :, lo:hi], w[:, LO, :, lo:hi], two(bank)) for w, lo, hi, bank in (
            (w_1t, 0, D, p_dx), (w_kz, D, 2 * D, p_z1))]

        def flat(t):
            return t.rearrange("p k n -> p (k n)")

        adam_parts = (
            (flat(raw_v[:, :, :]), flat(raw_w[:, 1]), flat(raw_q[:, :, :]), flat(wk_t[:, :, :])),
            (flat(g0_raw[:, :, :]), flat(raw_w[:, 0]), flat(raw_q[:, :, :]), flat(raw_k[:, :, :])),
            (raw_v[0:33], raw_b[:, :, :], raw_q[0:33], wk_t[0:33]))

        def pool_slot(r):
            return 0 if r == 0 else 1 + (r - 1) % 8

        def gradient_steps(engine, step):
            for t in range(NJ):
                step(Step(0, t))
            with engine.Fori(1, B - 1) as b:
                for t in range(NJ):
                    step(Step(b, t))
            for t in range(NJ):
                step(Step(B - 1, t))
            for t in range(GRAD0):
                step(Step(B, t))

        with nc.Block() as block:

            @block.sync
            def _(sp):
                def load_rows(b, c):
                    one = slice(b, b + 1) if isinstance(b, int) else bass.ds(b, 1)
                    src = x_rows[one].rearrange("a p n -> p (a n)")
                    first, last = (8 * c + 2 if c else 0), min(8 * c + 10, 2 * NJ)
                    sp.dma_start(rows[:, first:last, :].rearrange("p r d -> p (r d)"),
                                 src[:, first * D:last * D]).then_inc(x_loaded[c], 16)
                    if c == CHUNKS - 1:
                        sp.dma_start(rows[0:TOK - 1, 2 * NJ:, :].rearrange("p r d -> p (r d)"),
                                     src[1:TOK, 0:2 * D]).then_inc(x_loaded[c], 16)
                        for r in (2 * NJ, 2 * NJ + 1):
                            sp.dma_start(rows[TOK - 1:TOK, r, :],
                                         src[TOK - 1:TOK, (2 * NJ - 1) * D:]).then_inc(x_loaded[c], 16)

                load_rows(0, 0)
                sp.dma_start(raw_k[:, :, :], wk.rearrange("(k p) n -> p k n", p=128)).then_inc(kw_loaded, 16)
                for l in range(2):
                    sp.dma_start(raw_w[:, l], ws[l].rearrange("(k p) n -> p k n", p=128)).then_inc(kw_loaded, 16)
                for c in range(3):
                    sp.dma_start(blur_w[:, c, :], blur[c].broadcast_to([TOK, D])).then_inc(taps_loaded, 16)
                sp.wait_ge(consts, 1)
                sp.dma_start(blur_end[0:TOK - 1, :], blur[2].broadcast_to([TOK - 1, D])).then_inc(taps_loaded, 16)
                for dst, src in ((raw_v, wv), (raw_q, wq)):
                    sp.dma_start(dst[:, :, :], src.rearrange("(k p) n -> p k n", p=128)).then_inc(loaded, 16)
                for c in range(2):
                    sp.dma_start(raw_lr[:, :, c:c + 1], wlr.rearrange("(k p) n -> p k n", p=128),
                                 allow_slow_non_contiguous=True).then_inc(loaded, 16)
                for p in (0, 32):
                    for l in range(2):
                        sp.dma_start(raw_b[p:p + 1, l, :], bs[l:l + 1, :]).then_inc(loaded, 16)
                sp.dma_start(rate_bias[:, :], blr.rearrange("(a n) -> a n", a=1).broadcast_to([TOK, 1])
                             ).then_inc(loaded, 16)
                for c in range(1, CHUNKS):
                    load_rows(0, c)

                def step(s):
                    b, t = s.b, s.t
                    if not isinstance(b, int) or b < B:
                        if not isinstance(b, int) or b < B - 1:
                            if t in (5, 9):
                                sp.wait_ge(pooled, s.n(0))
                                load_rows(b + 1, (t - 5) // CH)
                    if t == 0 and isinstance(b, int) and b == 0:
                        return
                    if t == 0 and (not isinstance(b, int) or b < B):
                        sp.wait_ge(pooled, s.n(1))
                        load_rows(b, CHUNKS - 1)
                    if s.has(STATS) and s.part(STATS) == CH - 1:
                        c = s.chunk(STATS)
                        sp.wait_ge(tok_ops, s.n(STATS) * TOK_OPS)
                        bb = b if c >= 0 else b - 1
                        one = slice(bb, bb + 1) if isinstance(bb, int) else bass.ds(bb, 1)
                        c = c % CHUNKS
                        sp.dma_start(h_tok[one].rearrange("a p n -> p (a n)")[:, c * CH * D:(c + 1) * CH * D],
                                     hbuf[:, c, :, :].rearrange("p u d -> p (u d)")).then_inc(h_stored[c], 16)
                    if s.has(LAYER0):
                        j = t - LAYER0
                        bb = b if j >= 0 else b - 1
                        one = slice(bb, bb + 1) if isinstance(bb, int) else bass.ds(bb, 1)
                        j = j % NJ
                        sp.wait_ge(q_copied, s.n(LAYER0))
                        sp.dma_start(q_tok[one].rearrange("a p n -> p (a n)")[:, j * D:(j + 1) * D],
                                     qbuf[:, j % 3, :]).then_inc(q_stored[j % 3], 16)

                gradient_steps(sp, step)
                sp.wait_ge(pooled, TILES)
                for l, arrays in enumerate((norm1, norm2)):
                    for i, a in enumerate(arrays):
                        sp.dma_start(par[:, 5 * l + i, :],
                                     a.rearrange("e (m p) -> (e m) p", p=128)).then_inc(par_loaded, 16)
                for c in range(CHUNKS):
                    sp.wait_ge(h_stored[c], 16 * B)
                for r in range(3):
                    sp.wait_ge(q_stored[r], 16 * TILES // 3)

            @block.gpsimd
            def _(po):
                po.memset(raw_b[:, :, :], 0.0)
                po.memset(blur_end[:, :], 0.0).then_inc(consts, 1)
                po.memset(eye[:, :], 0.0).then_inc(eye_zero, 1)
                po.memset(bias_on[:, :].bitcast(F32), 0.0)
                po.memset(bias[:, :, :].bitcast(F32), 0.0)
                po.memset(new_bias[:, :, :].bitcast(F32), 0.0)
                po.memset(ones[:, :].bitcast(F32), 1.0)
                po.memset(minus_half[:, :], -0.5)
                po.memset(bn_eps[:, :, :], BN_EPS)
                po.memset(dz_sum[:, :, :], 0.0)
                po.memset(ln_eps[:, :], LN_EPS).then_inc(eye_zero, 1)
                po.wait_ge(eye_zero, 2)
                po.affine_select(out=eye[:, :], in_=eye[:, :], compare_op=ALU.not_equal, fill=1.0, base=0,
                                 pattern=[[-1, 128]], channel_multiplier=1).then_inc(consts, 1)
                po.wait_ge(consts, 2)
                po.wait_ge(taps_loaded, 64)

                def tokenize(s):
                    h = hbuf[:, s.t // CH, s.t % CH, :]
                    last = blur_end[:, :] if s.t == NJ - 1 else blur_w[:, 2, :]
                    po.wait_ge(pooled, s.n(0))
                    if s.has(NJ):
                        po.wait_ge(xn_ready, s.n(NJ))
                        po.wait_ge(h_stored[s.t // CH], s.b * 16)
                    po.tensor_tensor(h, pool[:, pool_slot(2 * s.t), :], blur_w[:, 0, :],
                                     ALU.mult).then_inc(tok_ops, 1)
                    if s.has(1):
                        po.wait_ge(tok_ops, s.n(1) * TOK_OPS)
                    po.tensor_tensor(tap1[:, :], pool[:, pool_slot(2 * s.t + 1), :], blur_w[:, 1, :],
                                     ALU.mult).then_inc(tok_ops, 1)
                    po.tensor_tensor(tap2[:, :], pool[:, pool_slot(2 * s.t + 2), :], last,
                                     ALU.mult).then_inc(tok_ops, 1)
                    po.wait_ge(tok_ops, s.n(0) * TOK_OPS - 3)
                    po.tensor_tensor(h, h, tap1[:, :], ALU.add).then_inc(tok_ops, 1)
                    po.wait_ge(tok_ops, s.n(0) * TOK_OPS - 1)
                    po.tensor_tensor(h, h, tap2[:, :], ALU.add).then_inc(tok_ops, 1)

                def step(s):
                    if s.has(RSTD):
                        k = s.slot(RSTD, 2)
                        po.wait_ge(mv_ready, s.n(RSTD))
                        po.tensor_tensor(var_eps[:, k, :], mv[:, k, 1:2], ln_eps[0:TOK, :],
                                         ALU.add).then_inc(eps_added, 1)
                        po.wait_ge(eps_added, s.n(RSTD))
                        if s.has(RSTD + 2):
                            po.wait_ge(xn_ready, s.n(RSTD + 2))
                        po.tensor_tensor(rstd[:, k, :], var_eps[:, k, :], minus_half[0:TOK, 0:1],
                                         ALU.pow).then_inc(rstd_ready, 1)
                    if s.has(GRAD0):
                        k = s.slot(GRAD0, 2)
                        po.wait_ge(dz0h_ready, s.n(GRAD0))
                        if s.has(GRAD0 + 2):
                            po.wait_ge(g0_added, s.n(GRAD0 + 2))
                        po.tensor_tensor(dz0s[:, k, LO, :], dz0[:, k, :], dz0s[:, k, HI, :],
                                         ALU.subtract).then_inc(dz0l_ready, 1)
                    if s.has(NORM):
                        k, r = s.slot(NORM, 2), s.slot(NORM, 6)
                        po.wait_ge(xn_ready, s.n(NORM))
                        po.tensor_tensor(xs[:, r, LO, :], xn[:, k, :], xs[:, r, HI, :],
                                         ALU.subtract).then_inc(xl_ready, 1)
                    if s.has(0):
                        tokenize(s)
                    if s.has(LAYER0):
                        k = s.slot(LAYER0, 2)
                        po.wait_ge(m0_ready, s.n(LAYER0))
                        if s.has(LAYER0 + 4):
                            po.wait_ge(dz0_ready, s.n(LAYER0 + 4))
                        po.tensor_tensor(f0[:, s.slot(LAYER0, 4), :], sg0[:, k, :], m0[:, k, :],
                                         ALU.subtract).then_inc(f0_ready, 1)

                gradient_steps(po, step)

                count = [0]

                def link(ins):
                    count[0] += 1
                    ins.then_inc(bn_done, 1)
                    po.wait_ge(bn_done, count[0])

                gain, var, bias_in, mean, beta = (
                    par_t[:, :, :].rearrange("p (l i) c -> p l i c", l=2)[:, :, i, :] for i in range(5))
                power = minus_half[:, 0:2 * KT * E].rearrange("p (l c) -> p l c", l=2)
                po.wait_ge(par_ready, 1)
                link(po.tensor_tensor(var, var, bn_eps[:, :, :], ALU.add))
                link(po.tensor_tensor(bn_scale[:, :, :], var, power, ALU.pow))
                link(po.tensor_tensor(bn_scale[:, :, :], bn_scale[:, :, :], gain, ALU.mult))
                link(po.tensor_tensor(bn_shift[:, :, :], bias_in, mean, ALU.subtract))
                link(po.tensor_tensor(bn_shift[:, :, :], bn_shift[:, :, :], bn_scale[:, :, :], ALU.mult))
                link(po.tensor_tensor(bn_shift[:, :, :], bn_shift[:, :, :], beta, ALU.add))

            @block.scalar
            def _(act):
                act.wait_ge(eye_zero, 2)
                nc.scalar.activation(table_in[:, :], ln_eps[0:TOK, :], ACT.Sigmoid)
                act.wait_ge(kw_loaded, 48)
                for n, (high, low, src) in enumerate(weight_parts):
                    if n == 2:
                        act.wait_ge(loaded, 16 * LOADS)
                    if n == len(weight_parts) - 2:
                        act.wait_ge(setup_t, 1)
                    if n == len(weight_parts) - 1:
                        act.wait_ge(kw0_filled, 1)
                    nc.scalar.copy(high, src).then_inc(w_high, 1)

                def step(s):
                    if s.has(LAYER1):
                        k = s.slot(LAYER1, 2)
                        act.wait_ge(z1_filled, s.n(LAYER1))
                        if s.has(LAYER1 + 2):
                            act.wait_ge(f1_ready, s.n(LAYER1 + 2))
                        nc.scalar.activation(sg1[:, k, :], p_z1[0:TOK, 0:D],
                                             ACT.Sigmoid).then_inc(sg1_ready, 1)
                    if s.has(X_T):
                        act.wait_ge(xt_filled, s.n(X_T))
                        if s.has(X_T + 3):
                            act.wait_ge(q_filled, s.n(X_T + 3))
                        nc.scalar.copy(x_t[:, s.slot(X_T, 3)].rearrange("p h k t -> p (h k t)"),
                                       p_t[:, 0:4 * TP]).then_inc(xt_ready, 1)
                    if s.has(NORM):
                        k = s.slot(NORM, 2)
                        h = hbuf[:, s.chunk(NORM) % CHUNKS, s.part(NORM), :]
                        act.wait_ge(shift_ready, s.n(NORM))
                        if s.has(NORM + 2):
                            act.wait_ge(xl_ready, s.n(NORM + 2))
                        nc.scalar.activation(xn[:, k, :], h, ACT.Identity, scale=rstd[:, k, :],
                                             bias=shift[:, k, :])
                        if s.has(NORM + 6):
                            act.wait_ge(g0_added, s.n(NORM + 6))
                        nc.scalar.activation(xs[:, s.slot(NORM, 6), HI, :], h, ACT.Identity,
                                             scale=rstd[:, k, :], bias=shift[:, k, :]).then_inc(xn_ready, 1)
                    if s.has(LAYER0):
                        act.wait_ge(kz_filled, s.n(LAYER0))
                        if s.has(LAYER0 + 2):
                            act.wait_ge(f0_ready, s.n(LAYER0 + 2))
                        nc.scalar.activation(sg0[:, s.slot(LAYER0, 2), :], p_kz[0:TOK, D:2 * D],
                                             ACT.Sigmoid).then_inc(sg0_ready, 1)
                    if s.has(LAYER1):
                        k = s.slot(LAYER1, 2)
                        act.wait_ge(dz1_ready, s.n(LAYER1))
                        if s.has(LAYER1 + 2):
                            act.wait_ge(g1_added, s.n(LAYER1 + 2))
                        nc.scalar.copy(dz1s[:, k, HI, :], dz1[:, k, :]).then_inc(dz1h_ready, 1)
                    if s.has(LAYER0):
                        k, r = s.slot(LAYER0, 2), s.slot(LAYER0, 3)
                        act.wait_ge(x1_ready, s.n(LAYER0))
                        if s.has(LAYER0 + 3):
                            act.wait_ge(g1_added, s.n(LAYER0 + 3))
                        nc.scalar.copy(x1s[:, r, HI, :], x1[:, k, :]).then_inc(x1h_ready, 1)
                    if s.has(LAYER0):
                        act.wait_ge(v_filled, s.n(LAYER0))
                        if s.has(LAYER0 + 4):
                            act.wait_ge(back_ready, s.n(LAYER0 + 4))
                        nc.scalar.activation(rate[:, s.slot(LAYER0, 4), :], p_v[0:TOK, D:D + 1], ACT.Sigmoid,
                                             bias=rate_bias[:, :]).then_inc(rate_ready, 1)
                    if s.has(LAYER0):
                        act.wait_ge(q_filled, s.n(LAYER0))
                        if s.has(LAYER0 + 3):
                            i3 = (s.t - LAYER0) // 3
                            act.wait_ge(q_stored[s.slot(LAYER0, 3)], s.b * 64 + 16 * i3)
                        nc.scalar.copy(qbuf[:, s.slot(LAYER0, 3), :], p_z1[0:TOK, D:2 * D]).then_inc(q_copied, 1)
                    if s.has(LAYER1):
                        act.wait_ge(dz1t_filled, s.n(LAYER1))
                        if s.has(LAYER1 + 2):
                            act.wait_ge(dx_filled, s.n(LAYER1 + 2))
                        nc.scalar.copy(dz1_t[:, s.slot(LAYER1, 2)].rearrange("p h k t -> p (h k t)"),
                                       p_tz[:, 0:4 * TP]).then_inc(dz1t_ready, 1)
                    if s.has(LAYER0):
                        act.wait_ge(x1t_filled, s.n(LAYER0))
                        if s.has(LAYER0 + 2):
                            act.wait_ge(z1_filled, s.n(LAYER0 + 2))
                        nc.scalar.copy(x1_t[:, s.slot(LAYER0, 2)].rearrange("p h k t -> p (h k t)"),
                                       p_t[:, 0:4 * TP]).then_inc(x1t_ready, 1)
                    if s.has(BACK1):
                        k = s.slot(BACK1, 2)
                        act.wait_ge(dz0_ready, s.n(BACK1))
                        if s.has(BACK1 + 2):
                            act.wait_ge(g0_added, s.n(BACK1 + 2))
                        nc.scalar.copy(dz0s[:, k, HI, :], dz0[:, k, :]).then_inc(dz0h_ready, 1)

                gradient_steps(act, step)

                def scaled(n, bank):
                    grad = adam_parts[n][0]
                    nc.scalar.activation(grad, bank, ACT.Copy, scale=GRAD_SCALE).then_inc(grad_scaled, 1)

                act.wait_ge(g1_added, TILES)
                scaled(0, p_g1[:, :])
                act.wait_ge(summed0, TILES)
                act.wait_ge(summed1, TILES)
                nc.scalar.copy(dz_sums[:, HI], dz_sum[:, :, :]).then_inc(sumh_ready, 1)
                act.wait_ge(g0_added, TILES)
                nc.scalar.copy(flat(g0_raw[:, :, :]), p_g0[:, :]).then_inc(g0_copied, 1)
                act.wait_ge(par_filled, 1)
                nc.scalar.copy(par_t[:, :, :].rearrange("p i c -> p (i c)"),
                               p_v[:, 0:10 * KT * E]).then_inc(par_ready, 1)
                act.wait_ge(adam_t, 1)
                scaled(1, p_kz[:, :])
                act.wait_ge(new_ready, 1)
                nc.scalar.copy(flat(new_w[:, 1, HI]), adam_parts[0][3]).then_inc(newh_ready, 1)
                act.wait_ge(gb_filled, 1)
                scaled(2, two(p_tz)[0:33])
                act.wait_ge(new_ready, 2)
                nc.scalar.copy(flat(new_w[:, 0, HI]), adam_parts[1][3]).then_inc(newh_ready, 1)
                act.wait_ge(new_ready, 3)
                nc.scalar.copy(new_bias[0:1], adam_parts[2][3][0:1])
                nc.scalar.copy(bias_h[32:33], adam_parts[2][3][32:33]).then_inc(newh_ready, 1)

            @block.vector
            def _(dve):
                def pool_rows(s):
                    t = s.slot(POOL, NJ)
                    c = t // CH
                    b = s.b if s.t - POOL < NJ else s.b + 1
                    dve.wait_ge(x_loaded[c], (b + 1) * (64 if c == CHUNKS - 1 else 16))
                    if s.has(POOL + 3):
                        dve.wait_ge(tok_ops, s.n(POOL + 3) * TOK_OPS)
                    first, last = (2 * t + 1 if t else 0), 2 * t + 3
                    at = pool_slot(first)
                    nc.vector.tensor_tensor(pool[:, at:at + last - first, :], rows[:, first:last, :],
                                            rows[:, first + 1:last + 1, :], ALU.max).then_inc(pooled, 1)

                pool_rows(Step(0, POOL))
                pool_rows(Step(0, 0))
                dve.wait_ge(consts, 2)
                nc.vector.tensor_copy(eye_r[:, :], eye[:, 0:TP])
                for p in (0, 32):
                    nc.vector.memset(bias_on[p:p + 1, :].bitcast(F32), 1.0)
                dve.wait_ge(setup_t, 1)
                nc.vector.tensor_copy(wk_t[:, :, :].rearrange("p k n -> p (k n)"),
                                      p_kz[:, :]).then_inc(wk_t_done, 1)
                for n, (high, low, src) in enumerate(weight_parts):
                    dve.wait_ge(w_high, n + 1)
                    nc.vector.tensor_tensor(low, src, high, ALU.subtract).then_inc(w_low, 1)
                dve.wait_ge(w_low, len(weight_parts))
                nc.vector.tensor_copy(bias[0:1], bias_h[0:1])
                nc.vector.tensor_copy(bias[32:33], bias_l[32:33]).then_inc(setup_v, 1)

                def step(s):
                    if s.has(AGGR):
                        dve.wait_ge(stats_ready, s.n(AGGR))
                    if s.has(POOL) and not (isinstance(s.b, int) and s.b == 0 and s.t == 0):
                        pool_rows(s)
                    if s.has(AGGR):
                        k = s.slot(AGGR, 2)
                        nc.vector.bn_aggr(mv[:, k, :], stats[:, k, :]).then_inc(mv_ready, 1)
                    if s.has(LAYER1):
                        k = s.slot(LAYER1, 2)
                        dve.wait_ge(rate_ready, s.n(LAYER1))
                        nc.vector.tensor_tensor(u[:, k, :], x1[:, k, :], p_v[0:TOK, 0:D],
                                                ALU.subtract).then_inc(u_ready, 1)
                    for lag, l, dz, ready, summed in ((BACK1, 1, dz1, dz1_ready, summed1),
                                                      (GRAD0, 0, dz0, dz0_ready, summed0)):
                        if s.has(lag):
                            dve.wait_ge(ready, s.n(lag))
                            if s.has(lag + 1):
                                dve.wait_ge(summed, s.n(lag + 1))
                            nc.vector.tensor_tensor(dz_sum[:, l, :], dz_sum[:, l, :], dz[:, s.slot(lag, 2), :],
                                                    ALU.add).then_inc(summed, 1)
                    if s.has(LAYER1):
                        k = s.slot(LAYER1, 2)
                        dve.wait_ge(sg1_ready, s.n(LAYER1))
                        nc.vector.tensor_tensor(s1[:, k, :], p_z1[0:TOK, 0:D], sg1[:, k, :],
                                                ALU.mult).then_inc(s1_ready, 1)
                    if s.has(LAYER1):
                        k = s.slot(LAYER1, 2)
                        dve.wait_ge(s1_ready, s.n(LAYER1))
                        nc.vector.scalar_tensor_tensor(out=m1[:, k, :], in0=sg1[:, k, :], scalar=1.0,
                                                       in1=s1[:, k, :], op0=ALU.subtract,
                                                       op1=ALU.mult).then_inc(m1_ready, 1)
                        dve.wait_ge(u_ready, s.n(LAYER1))
                        nc.vector.tensor_tensor(diff[:, k, :], u[:, k, :], s1[:, k, :],
                                                ALU.add).then_inc(diff_ready, 1)
                        dve.wait_ge(m1_ready, s.n(LAYER1))
                        nc.vector.tensor_tensor(f1[:, k, :], sg1[:, k, :], m1[:, k, :],
                                                ALU.subtract).then_inc(f1_ready, 1)
                    if s.has(LAYER1):
                        k = s.slot(LAYER1, 2)
                        dve.wait_ge(f1_ready, s.n(LAYER1))
                        if s.has(LAYER1 + 2):
                            dve.wait_ge(dz1l_ready, s.n(LAYER1 + 2))
                        nc.vector.scalar_tensor_tensor(out=dz1[:, k, :], in0=diff[:, k, :],
                                                       scalar=rate[:, s.slot(LAYER1, 4), :],
                                                       in1=f1[:, k, :], op0=ALU.mult,
                                                       op1=ALU.mult).then_inc(dz1_ready, 1)
                    if s.has(LAYER0):
                        k = s.slot(LAYER0, 2)
                        dve.wait_ge(sg0_ready, s.n(LAYER0))
                        nc.vector.tensor_tensor(s0[:, k, :], p_kz[0:TOK, D:2 * D], sg0[:, k, :],
                                                ALU.mult).then_inc(s0_ready, 1)
                    if s.has(LAYER0):
                        k = s.slot(LAYER0, 2)
                        dve.wait_ge(s0_ready, s.n(LAYER0))
                        if s.has(LAYER0 + 2):
                            dve.wait_ge(x1h_ready, s.n(LAYER0 + 2))
                        nc.vector.tensor_tensor(x1[:, k, :], p_kz[0:TOK, 0:D], s0[:, k, :],
                                                ALU.add).then_inc(x1_ready, 1)
                    if s.has(LAYER1):
                        k = s.slot(LAYER1, 2)
                        dve.wait_ge(dz1h_ready, s.n(LAYER1))
                        nc.vector.tensor_tensor(dz1s[:, k, LO, :], dz1[:, k, :], dz1s[:, k, HI, :],
                                                ALU.subtract).then_inc(dz1l_ready, 1)
                    if s.has(RSTD):
                        k = s.slot(RSTD, 2)
                        dve.wait_ge(rstd_ready, s.n(RSTD))
                        if s.has(RSTD + 2):
                            dve.wait_ge(xn_ready, s.n(RSTD + 2))
                        nc.vector.tensor_scalar(shift[:, k, :], mv[:, k, 0:1], rstd[:, k, :], -1.0,
                                                ALU.mult, ALU.mult).then_inc(shift_ready, 1)
                    if s.has(LAYER0):
                        k = s.slot(LAYER0, 2)
                        dve.wait_ge(x1h_ready, s.n(LAYER0))
                        r = s.slot(LAYER0, 3)
                        nc.vector.tensor_tensor(x1s[:, r, LO, :], x1[:, k, :], x1s[:, r, HI, :],
                                                ALU.subtract).then_inc(x1l_ready, 1)
                    if s.has(LAYER0):
                        k = s.slot(LAYER0, 2)
                        nc.vector.scalar_tensor_tensor(out=m0[:, k, :], in0=sg0[:, k, :], scalar=1.0,
                                                       in1=s0[:, k, :], op0=ALU.subtract,
                                                       op1=ALU.mult).then_inc(m0_ready, 1)
                    if s.has(BACK1):
                        k = s.slot(BACK1, 2)
                        dve.wait_ge(dx_filled, s.n(BACK1))
                        nc.vector.scalar_tensor_tensor(out=back[:, k, :], in0=diff[:, k, :],
                                                       scalar=rate[:, s.slot(BACK1, 4), :],
                                                       in1=p_dx[0:TOK, 0:D],
                                                       op0=ALU.mult, op1=ALU.add).then_inc(back_ready, 1)
                    if s.has(STATS):
                        h = hbuf[:, s.chunk(STATS) % CHUNKS, s.part(STATS), :]
                        dve.wait_ge(tok_ops, s.n(STATS) * TOK_OPS)
                        nc.vector.bn_stats(stats[:, s.slot(STATS, 2), :], h).then_inc(stats_ready, 1)
                    if s.has(BACK1):
                        k = s.slot(BACK1, 2)
                        dve.wait_ge(back_ready, s.n(BACK1))
                        dve.wait_ge(f0_ready, s.n(BACK1))
                        if s.has(BACK1 + 2):
                            dve.wait_ge(dz0l_ready, s.n(BACK1 + 2))
                        nc.vector.tensor_tensor(dz0[:, k, :], back[:, k, :], f0[:, s.slot(BACK1, 4), :],
                                                ALU.mult).then_inc(dz0_ready, 1)

                gradient_steps(dve, step)

                dve.wait_ge(sumh_ready, 1)
                nc.vector.tensor_tensor(dz_sums[:, LO], dz_sum[:, :, :], dz_sums[:, HI],
                                        ALU.subtract).then_inc(suml_ready, 1)

                count = [0]

                def link(ins):
                    count[0] += 1
                    ins.then_inc(adam_v, 1)
                    dve.wait_ge(adam_v, count[0])

                for n, (grad, old, mag, new) in enumerate(adam_parts):
                    dve.wait_ge(grad_scaled, n + 1)
                    link(nc.vector.scalar_tensor_tensor(out=mag, in0=grad, scalar=-1.0, in1=grad,
                                                        op0=ALU.mult, op1=ALU.max))
                    link(nc.vector.tensor_scalar(mag, mag, ADAM_EPS, None, ALU.add))
                    link(nc.vector.reciprocal(mag, mag))
                    link(nc.vector.scalar_tensor_tensor(out=grad, in0=grad, scalar=LR, in1=mag,
                                                        op0=ALU.mult, op1=ALU.mult))
                    nc.vector.scalar_tensor_tensor(out=new, in0=old, scalar=1.0 - LR * WD, in1=grad,
                                                   op0=ALU.mult, op1=ALU.subtract).then_inc(new_ready, 1)
                    if n < 2:
                        dve.wait_ge(newh_ready, n + 1)
                        nc.vector.tensor_tensor(flat(new_w[:, 1 - n, LO]), new, flat(new_w[:, 1 - n, HI]),
                                                ALU.subtract)
                dve.wait_ge(newh_ready, 3)
                nc.vector.tensor_tensor(new_bias[32:33], adam_parts[2][3][32:33], bias_h[32:33], ALU.subtract)

            @block.tensor
            def _(pe):
                mm = nc.tensor.matmul

                pe.wait_ge(kw_loaded, 48)
                pe.wait_ge(consts, 2)
                for dst, src in ((p_kz, raw_k), (p_dx, raw_w[:, 1])):
                    for k in range(KT):
                        for m in range(KT):
                            last = nc.tensor.transpose(dst[:, m * D + k * 128:m * D + (k + 1) * 128],
                                                       src[:, k, m * 128:(m + 1) * 128], eye[:, :])
                last.then_inc(setup_t, 1)
                pe.wait_ge(wk_t_done, 1)
                for m in range(KT):
                    for k in range(KT):
                        last = mm(p_z1[:, m * D:(m + 1) * D], wk_t[:, k, m * 128:(m + 1) * 128],
                                  raw_w[:, 0, k, :], start=(k == 0), stop=(k == KT - 1))
                last.then_inc(kw0_filled, 1)
                pe.wait_ge(setup_v, 1)

                def product(dst, left, right, start=True, stop=True):
                    n = 0
                    for k in range(KT):
                        for h, g in ((HI, HI), (HI, LO), (LO, HI)):
                            n += 1
                            last = mm(dst, left(h, k), right(g, k), start=start and n == 1,
                                      stop=stop and n == 3 * KT, skip_group_check=True)
                    return last

                def transposes(dst, src):
                    for h in (HI, LO):
                        for k in range(KT):
                            at = (h * KT + k) * TP
                            last = mm(dst[:, at:at + TP], src[:, h, k * 128:(k + 1) * 128],
                                      eye_r[0:TOK, :], start=True, stop=True, skip_group_check=True)
                    return last

                def gradient(dst, left, right, m, first):
                    for h, g in ((HI, HI), (HI, LO), (LO, HI)):
                        last = mm(dst[:, m * D:(m + 1) * D], left[:, h, m * 128:(m + 1) * 128],
                                  right[:, g, :], start=first, stop=True, skip_group_check=True)
                        first = False
                    return last

                def gradient1(s, m):
                    return gradient(p_g1, x1s[:, s.slot(BACK1, 3)], dz1s[:, s.slot(BACK1, 2)], m,
                                    m == 0 and isinstance(s.b, int) and s.b * NJ + s.t == BACK1)

                def step(s):
                    if s.has(LAYER1):
                        pe.wait_ge(x1t_ready, s.n(LAYER1))
                        pe.wait_ge(q_copied, s.n(LAYER1))
                        x1t = x1_t[:, s.slot(LAYER1, 2)]
                        product(p_z1[0:TOK, 0:D], lambda h, k: x1t[:, h, k, 0:TOK],
                                lambda h, k: w_1[:, h, k, :], stop=False)
                        mm(p_z1[0:TOK, 0:D], bias_on[:, :], bias[:, 1, :], start=False, stop=True,
                           skip_group_check=True).then_inc(z1_filled, 1)
                    if s.has(X_T):
                        pe.wait_ge(xl_ready, s.n(X_T))
                        if s.has(X_T + 1):
                            pe.wait_ge(xt_ready, s.n(X_T + 1))
                        if s.has(LAYER0 + 1):
                            pe.wait_ge(x1t_ready, s.n(LAYER0 + 1))
                        transposes(p_t, xs[:, s.slot(X_T, 6)]).then_inc(xt_filled, 1)
                    if s.has(LAYER0):
                        xt = x_t[:, s.slot(LAYER0, 3)]
                        pe.wait_ge(xt_ready, s.n(LAYER0))
                        if s.has(LAYER0 + 1):
                            pe.wait_ge(x1_ready, s.n(LAYER0 + 1))
                        product(p_kz[0:TOK, :], lambda h, k: xt[:, h, k, 0:TOK],
                                lambda h, k: w_kz[:, h, k, :], stop=False)
                        mm(p_kz[0:TOK, D:2 * D], bias_on[:, :], bias[:, 0, :], start=False, stop=True,
                           skip_group_check=True).then_inc(kz_filled, 1)
                        if s.has(LAYER0 + 1):
                            pe.wait_ge(u_ready, s.n(LAYER0 + 1))
                        product(p_v[0:TOK, 0:D + 2], lambda h, k: xt[:, h, k, 0:TOK],
                                lambda h, k: w_v[:, h, k, :]).then_inc(v_filled, 1)
                        if s.has(LAYER1):
                            pe.wait_ge(s1_ready, s.n(LAYER1))
                        product(p_z1[0:TOK, D:2 * D], lambda h, k: xt[:, h, k, 0:TOK],
                                lambda h, k: w_q[:, h, k, :]).then_inc(q_filled, 1)
                    if s.has(BACK1):
                        dt = dz1_t[:, s.slot(BACK1, 2)]
                        pe.wait_ge(dz1t_ready, s.n(BACK1))
                        if s.has(BACK1 + 1):
                            pe.wait_ge(back_ready, s.n(BACK1 + 1))
                        product(p_dx[0:TOK, 0:D], lambda h, k: dt[:, h, k, 0:TOK],
                                lambda h, k: w_1t[:, h, k, :]).then_inc(dx_filled, 1)
                        gradient1(s, 0)
                    if s.has(LAYER1):
                        pe.wait_ge(dz1l_ready, s.n(LAYER1))
                        if s.has(LAYER1 + 1):
                            pe.wait_ge(dz1t_ready, s.n(LAYER1 + 1))
                        transposes(p_tz, dz1s[:, s.slot(LAYER1, 2)]).then_inc(dz1t_filled, 1)
                    if s.has(LAYER0):
                        pe.wait_ge(x1l_ready, s.n(LAYER0))
                        if s.has(X_T):
                            pe.wait_ge(xt_ready, s.n(X_T))
                        transposes(p_t, x1s[:, s.slot(LAYER0, 3)]).then_inc(x1t_filled, 1)
                    if s.has(BACK1):
                        gradient1(s, 1).then_inc(g1_added, 1)
                    if s.has(GRAD0):
                        pe.wait_ge(dz0l_ready, s.n(GRAD0))
                        for m in range(KT):
                            last = gradient(p_g0, xs[:, s.slot(GRAD0, 6)], dz0s[:, s.slot(GRAD0, 2)], m,
                                            m == 0 and isinstance(s.b, int) and s.b * NJ + s.t == GRAD0)
                        last.then_inc(g0_added, 1)

                gradient_steps(pe, step)

                pe.wait_ge(par_loaded, 160)
                pe.wait_ge(u_ready, TILES)
                for i in range(10):
                    last = nc.tensor.transpose(p_v[:, i * KT * E:(i + 1) * KT * E], par[:, i, :],
                                               eye[0:KT * E, 0:KT * E])
                last.then_inc(par_filled, 1)
                pe.wait_ge(suml_ready, 1)
                for h in (HI, LO):
                    last = mm(p_tz[:, :], ones[:, :], dz_sums[:, h].rearrange("p l d -> p (l d)"),
                              start=(h == HI), stop=(h == LO))
                last.then_inc(gb_filled, 1)
                pe.wait_ge(g0_copied, 1)
                for m in range(KT):
                    for k in range(KT):
                        last = mm(p_kz[:, m * D:(m + 1) * D], raw_k[:, k, m * 128:(m + 1) * 128],
                                  g0_raw[:, k, :], start=(k == 0), stop=(k == KT - 1))
                last.then_inc(adam_t, 1)


def block_sweep(nc, wr, br, ffn_raw, bo, h_dram, q_dram, out, ffn_w, bn_scale, bn_shift,
                eye, eye_r, bias_on, new_w, new_bias, minus_half, ln_eps):
    h_j = h_dram.rearrange("b (p j) d -> b j p d", j=NJ)
    q_j = q_dram.rearrange("b (p j) d -> b j p d", j=NJ)
    out_j = out.rearrange("b (p j) d -> j p b d", j=NJ)

    with ExitStack() as ctx:
        def sb(name, shape, dt=F32):
            return ctx.enter_context(nc.sbuf_tensor(name, shape, dt))

        def psum(name, shape):
            return ctx.enter_context(nc.psum_tensor(name, shape, F32))

        def sem(name):
            return ctx.enter_context(nc.semaphore(name))

        xt_new = sb("xt_new", [128, 2, KT, B, TOK], F32R)
        xt_use = sb("xt_use", [128, 2, KT, B, TOK], F32R)
        h1f = sb("h1f", [128, KT, 512])
        h1s = sb("h1s", [128, 2, KT, NTOK], F32R)
        h2f = sb("h2f", [128, KT, 512])
        h2s = sb("h2s", [128, 2, KT, NTOK], F32R)
        res = sb("res", [TOK, B, D])
        acc_all = sb("acc", [128, B, D])
        acc = acc_all[0:TOK]
        yb = sb("yb", [TOK, D])
        qin = sb("qin", [TOK, 4, D])
        qs = sb("qs", [TOK, 2, D], F32R)
        q_t = sb("q_t", [128, 2, KT, TP], F32R)
        rsg = sb("rsg", [TOK, 2, D])
        rs = sb("rs", [TOK, D])
        q1 = sb("q1", [TOK, 3, D])
        q1s = sb("q1s", [TOK, 2, D], F32R)
        q1_t = sb("q1_t", [128, 2, KT, TP], F32R)
        xn2 = sb("xn2", [TOK, 2, D])
        feat = sb("feat", [TOK, D])
        xn2s = sb("xn2s", [TOK, 2, D], F32R)
        stats = sb("stats2", [TOK, 6])
        mv = sb("mv2", [TOK, 2, 2])
        var_eps = sb("var_eps2", [TOK, 1])
        rstd = sb("rstd2", [TOK, 2, 1])
        raw_r = sb("raw_r", [128, KT, E])
        w_r = sb("w_r", [128, 2, KT, E], F32R)
        br_b = sb("br_b", [TOK, E])
        bo_s = sb("bo_s", [E, D])
        logit = sb("logit", [TOK, E])
        top = sb("top", [TOK, 1])
        sig = sb("sig", [TOK, 2, E])
        total = sb("total", [TOK, 1])
        gate_new = sb("gate_new", [TOK, E])
        gate = sb("gate", [TOK, E])
        gate_t = sb("gate_t", [E, TOK])

        p_1 = [psum(f"p_1{m}", [128, 512]) for m in range(KT)]
        p_2 = [psum(f"p_2{m}", [128, 512]) for m in range(KT)]
        p_3 = [psum(f"p_3{m}", [128, 2, D]) for m in range(2)]
        p_t = psum("p_t2", [128, 512])
        p_z = psum("p_z", [128, 512])

        w_loaded = [sem(f"w_loaded{r}") for r in range(8)]
        w_high = sem("w_high")
        w12_low = sem("w12_low")
        w3_low = sem("w3_low")
        const_loaded = sem("const_loaded")
        const_v = sem("const_v")
        q_loaded = [sem(f"q_loaded{i}") for i in range(4)]
        h_loaded = [sem(f"h_loaded{b}") for b in range(B)]
        qh_ready = sem("qh_ready")
        ql_ready = sem("ql_ready")
        qt_filled = sem("qt_filled")
        qt_ready = sem("qt_ready")
        za_filled = sem("za_filled")
        sga_ready = sem("sga_ready")
        sa_ready = sem("sa_ready")
        q1_ready = sem("q1_ready")
        q1h_ready = sem("q1h_ready")
        q1l_ready = sem("q1l_ready")
        q1t_filled = sem("q1t_filled")
        q1t_ready = sem("q1t_ready")
        zb_filled = sem("zb_filled")
        sgb_ready = sem("sgb_ready")
        sb_ready = sem("sb_ready")
        r_ready = sem("r_ready")
        res_ready = sem("res_ready")
        stat_ready = sem("stat_ready")
        mv_ready = sem("mv2_ready")
        eps_added = sem("eps2_added")
        rstd_ready = sem("rstd2_ready")
        xn_ready = sem("xn2_ready")
        xnh_ready = sem("xn2h_ready")
        xnl_ready = sem("xn2l_ready")
        xt_filled = sem("xt2_filled")
        xt_ready = sem("xt2_ready")
        feat_added = sem("feat_added")
        feath_ready = sem("feath_ready")
        featl_ready = sem("featl_ready")
        featt_filled = sem("featt_filled")
        featt_ready = sem("featt_ready")
        logits_filled = sem("logits_filled")
        soft_v = sem("soft_v")
        sig_ready = sem("sig_ready")
        gate_t_filled = sem("gate_t_filled")
        gate_t_ready = sem("gate_t_ready")
        yb_filled = sem("yb_filled")
        yb_ready = sem("yb_ready")
        gate_ready = sem("gate_ready")
        acc_ready = sem("acc_ready")
        copied = [sem(f"copied{g}") for g in range(2)]
        l1_filled = sem("l1_filled")
        h1h_ready = sem("h1h_ready")
        h1l_ready = sem("h1l_ready")
        l2_filled = sem("l2_filled")
        h2h_ready = sem("h2h_ready")
        h2l_ready = sem("h2l_ready")
        l3_filled = sem("l3_filled")
        mixed = sem("mixed")
        out_stored = [sem(f"out_stored{g}") for g in range(2)]

        SOFT = 8
        ADDS = B - 1

        jobs = [(i, e) for e in range(E) for i in range(3)]
        places = [t[:, m, :] for t in (h1f, h2f) for m in range(KT)]
        places += [acc_all[:, b:b + 2, :].rearrange("p b d -> p (b d)") for b in range(0, B, 2)]
        RING = len(places)

        def raw(n):
            return places[n % RING].rearrange("p (k n) -> p k n", k=KT)

        def wait_low(engine, n):
            i, e = jobs[n]
            if i < 2:
                engine.wait_ge(w12_low, 2 * e + i + 1)
            else:
                engine.wait_ge(w3_low, e + 1)

        def alone(s):
            return isinstance(s.J, int) and s.J == 0

        def weight_jobs(s, first):
            n = 2 * (s.i - first)
            return range(n, n + 2) if alone(s) and 0 <= n < len(jobs) else ()

        def bank_q(s):
            return p_1[0] if alone(s) else p_t

        def bank_x(s):
            return p_1[1] if alone(s) else p_t

        def bank_za(s):
            return p_2[0] if alone(s) else p_z

        def macros(engine, step):
            for J in (0, 1):
                for n in range(16):
                    step(Pace(J, n))
            with engine.Fori(2, NJ) as J:
                for n in range(16):
                    step(Pace(J, n))
            for n in range(16):
                step(Pace(NJ, n))
            for n in range(2):
                step(Pace(NJ + 1, n))

        def retrieves(s):
            return not isinstance(s.J, int) or s.J < NJ

        def col(J, shift):
            j = J + shift
            return slice(j, j + 1) if isinstance(j, int) else bass.ds(j, 1)

        with nc.Block() as block:
            @block.sync
            def _(sp):
                sp.dma_start(raw_r[:, :, :], wr.rearrange("(k p) n -> p k n", p=128)).then_inc(const_loaded, 16)
                sp.dma_start(br_b[:, :], br.rearrange("(a n) -> a n", a=1).broadcast_to([TOK, E])).then_inc(const_loaded, 16)
                sp.dma_start(bo_s[:, :], bo).then_inc(const_loaded, 16)

                def load_queries(s, b):
                    if s.has_m(b - 4):
                        sp.wait_ge(q1_ready, s.m(b - 4))
                    sp.dma_start(qin[:, b % 4, :], q_j[b, col(s.J, 0)].rearrange("a p d -> p (a d)")
                                 ).then_inc(q_loaded[b % 4], 16)

                def load_tokens(s, b):
                    if s.has_m(b - 8) and s.has():
                        sp.wait_ge(acc_ready, s.J * B + (b + 1 - B))
                    sp.dma_start(res[:, b, :], h_j[b, col(s.J, 0)].rearrange("a p d -> p (a d)")
                                 ).then_inc(h_loaded[b], 16)

                def hand_over(s, g):
                    before = Pace(s.J, E - 1 - g * E)
                    if before.has():
                        sp.wait_ge(l1_filled, before.n(0, 2))
                    sp.wait_ge(xt_ready, s.m(GRP * g + GRP - 1 - g * B))
                    at = slice(GRP * g, GRP * g + GRP)
                    sp.dma_start(xt_use[:, :, :, at, :].rearrange("p h k b t -> p (h k) (b t)").bitcast(F32),
                                 xt_new[:, :, :, at, :].rearrange("p h k b t -> p (h k) (b t)").bitcast(F32)
                                 ).then_inc(copied[g], 16)

                def store(s, g, shift):
                    sp.wait_ge(mixed, s.n(2, 4))
                    sp.dma_start(out_j[col(s.J, shift), :, GRP * g:GRP * g + GRP, :].rearrange("a p b d -> p (a b) d"),
                                 acc[:, GRP * g:GRP * g + GRP, :]).then_inc(out_stored[g], 16)

                def step(s):
                    if retrieves(s) and s.i < B:
                        load_queries(s, s.i)
                    if s.tile(2) is not None:
                        load_tokens(s, s.tile(2))
                    for n in weight_jobs(s, 0):
                        i, e = jobs[n]
                        if n >= RING:
                            wait_low(sp, n - RING)
                        sp.dma_start(raw(n), ffn_raw[i][e].rearrange("(k p) n -> p k n", p=128)
                                     ).then_inc(w_loaded[n % RING], 16)
                    if s.i == 1 and s.has(2):
                        store(s, 1, -2)
                    if s.i == 9 and s.has(2):
                        store(s, 0, -1)
                    if retrieves(s) and s.i == 10:
                        hand_over(s, 0)
                    if s.i == 2 and s.has():
                        hand_over(s, 1)

                macros(sp, step)
                for g in range(2):
                    sp.wait_ge(out_stored[g], 16 * NJ)

            @block.gpsimd
            def _(po):
                def step(s):
                    if s.has() and s.i in (1, 3):
                        g = s.i // 3
                        po.wait_ge(yb_ready, s.J)
                        if s.has(16):
                            po.wait_ge(out_stored[g], s.J * 16 - 16)
                        for b in range(GRP * g, GRP * g + GRP):
                            po.tensor_tensor(acc[:, b, :], res[:, b, :], yb[:, :], ALU.add).then_inc(acc_ready, 1)
                    b = s.tile(4)
                    if b is not None:
                        po.wait_ge(mv_ready, s.m(b))
                        po.tensor_tensor(var_eps[:, :], mv[:, b % 2, 1:2], ln_eps[0:TOK, :],
                                         ALU.add).then_inc(eps_added, 1)
                        po.wait_ge(eps_added, s.m(b))
                        if s.has_m(b - 2):
                            po.wait_ge(xn_ready, s.m(b - 2))
                        po.tensor_tensor(rstd[:, b % 2, :], var_eps[:, :], minus_half[0:TOK, 0:1],
                                         ALU.pow).then_inc(rstd_ready, 1)
                    b = s.tile(5)
                    if b is not None and b > 0:
                        po.wait_ge(xn_ready, s.m(b))
                        if b > 1:
                            po.wait_ge(feat_added, s.J * ADDS + (b - 1))
                        elif s.has_m(-1):
                            po.wait_ge(featl_ready, s.J)
                        po.tensor_tensor(feat[:, :], xn2[:, 0, :] if b == 1 else feat[:, :], xn2[:, b % 2, :],
                                         ALU.add).then_inc(feat_added, 1)
                    for n in weight_jobs(s, 1):
                        i, e = jobs[n]
                        if i < 2:
                            po.wait_ge(w_high, n + 1)
                            po.tensor_tensor(ffn_w[i][:, e, LO], raw(n), ffn_w[i][:, e, HI],
                                             ALU.subtract).then_inc(w12_low, 1)

                macros(po, step)

            @block.scalar
            def _(act):
                def relu(s, lag, bank, layer, full, parts, filled, reader, low, high):
                    for m in range(KT):
                        c = m + KT * s.expert(lag)
                        bias, scale = bn_shift[:, layer, c:c + 1], bn_scale[:, layer, c:c + 1]
                        act.wait_ge(filled, s.n(lag, 2) - (KT - 1 - m))
                        if s.has(lag + 1):
                            act.wait_ge(low, s.n(lag + 1, 2) - (KT - 1 - m))
                        nc.scalar.activation(full[:, m, 0:NTOK], bank[m][:, 0:NTOK], ACT.Relu,
                                             bias=bias, scale=scale)
                        if m == 0 and s.has(lag + 1):
                            act.wait_ge(*reader)
                        nc.scalar.activation(parts[:, HI, m, :], bank[m][:, 0:NTOK], ACT.Relu,
                                             bias=bias, scale=scale).then_inc(high, 1)

                def normed_copies(s):
                    b = s.tile(6)
                    if b is not None:
                        act.wait_ge(xt_filled, s.m(b))
                        if b % GRP == 0 and s.has_m(b - 8):
                            act.wait_ge(copied[b // GRP], s.J * 16)
                        nc.scalar.copy(xt_new[:, :, :, b, :].rearrange("p h k t -> p (h k) t"),
                                       bank_x(s)[:, 0:4 * TP].rearrange("p (c t) -> p c t", t=TP)[:, :, 0:TOK]
                                       ).then_inc(xt_ready, 1)
                    if retrieves(s) and s.i == 14:
                        act.wait_ge(featt_filled, s.J + 1)
                        act.wait_ge(zb_filled, s.m(B - 1))
                        nc.scalar.copy(q1_t[:, :, :, :].rearrange("p h k t -> p (h k t)"),
                                       bank_x(s)[:, 0:4 * TP]).then_inc(featt_ready, 1)

                def step(s):
                    b = s.tile(2)
                    if b is not None:
                        act.wait_ge(za_filled, s.m(b))
                        if s.has_m(b - 1):
                            act.wait_ge(sa_ready, s.m(b - 1))
                        nc.scalar.activation(rsg[:, 0, :], bank_za(s)[0:TOK, 0:D],
                                             ACT.Sigmoid).then_inc(sga_ready, 1)
                    b = s.tile(1)
                    if b is not None:
                        act.wait_ge(qt_filled, s.m(b))
                        if s.has_m(b - 1):
                            act.wait_ge(za_filled, s.m(b - 1))
                        nc.scalar.copy(q_t[:, :, :, :].rearrange("p h k t -> p (h k t)"),
                                       bank_q(s)[:, 0:4 * TP]).then_inc(qt_ready, 1)
                    b = s.tile(0)
                    if b is not None:
                        act.wait_ge(q_loaded[b % 4], s.J * 32 + 16 * (b // 4 + 1))
                        if s.has_m(b - 1):
                            act.wait_ge(qt_filled, s.m(b - 1))
                        nc.scalar.copy(qs[:, HI, :], qin[:, b % 4, :]).then_inc(qh_ready, 1)
                    if not alone(s):
                        normed_copies(s)
                    if retrieves(s) and s.i == 15:
                        act.wait_ge(soft_v, s.J * SOFT + 3)
                        nc.scalar.activation(sig[:, 0, :], logit[:, :], ACT.Sigmoid)
                        nc.scalar.activation(sig[:, 1, :], logit[:, :], ACT.Sigmoid,
                                             scale=-1.0).then_inc(sig_ready, 1)
                    if s.has(1):
                        relu(s, 1, p_2, 1, h2f, h2s, l2_filled, (l3_filled, s.n(2, 2)), h2l_ready, h2h_ready)
                    b = s.tile(4)
                    if b is not None:
                        act.wait_ge(zb_filled, s.m(b))
                        if s.has_m(b - 1):
                            act.wait_ge(sb_ready, s.m(b - 1))
                        nc.scalar.activation(rsg[:, 1, :], p_z[0:TOK, 0:D], ACT.Sigmoid).then_inc(sgb_ready, 1)
                    b = s.tile(3)
                    if b is not None:
                        act.wait_ge(q1t_filled, s.m(b))
                        if b > 0:
                            act.wait_ge(zb_filled, s.m(b - 1))
                        elif s.has_m(-1):
                            act.wait_ge(logits_filled, s.J)
                        nc.scalar.copy(q1_t[:, :, :, :].rearrange("p h k t -> p (h k t)"),
                                       p_t[:, 0:4 * TP]).then_inc(q1t_ready, 1)
                    b = s.tile(2)
                    if b is not None:
                        act.wait_ge(q1_ready, s.m(b))
                        if s.has_m(b - 1):
                            act.wait_ge(q1t_filled, s.m(b - 1))
                        nc.scalar.copy(q1s[:, HI, :], q1[:, b % 3, :]).then_inc(q1h_ready, 1)
                    b = s.tile(5)
                    if b is not None:
                        act.wait_ge(xn_ready, s.m(b))
                        if b > 0:
                            act.wait_ge(xt_filled, s.m(b - 1))
                        elif s.has_m(-1):
                            act.wait_ge(featt_filled, s.J)
                        nc.scalar.copy(xn2s[:, HI, :], xn2[:, b % 2, :]).then_inc(xnh_ready, 1)
                    for n in weight_jobs(s, 1):
                        i, e = jobs[n]
                        act.wait_ge(w_loaded[n % RING], 16 * (n // RING + 1))
                        nc.scalar.copy(ffn_w[i][:, e, HI], raw(n)).then_inc(w_high, 1)
                    if isinstance(s.J, int) and s.J == 1 and s.i == 0:
                        for n in (len(jobs) - 2, len(jobs) - 1):
                            wait_low(act, n)
                    if s.has(0):
                        relu(s, 0, p_1, 0, h1f, h1s, l1_filled, (l2_filled, s.n(1, 2)), h1l_ready, h1h_ready)
                    if retrieves(s) and s.i == 13:
                        act.wait_ge(feat_added, (s.J + 1) * ADDS)
                        act.wait_ge(xt_filled, s.m(B - 1))
                        nc.scalar.copy(xn2s[:, HI, :], feat[:, :]).then_inc(feath_ready, 1)
                    if alone(s):
                        normed_copies(s)

                macros(act, step)

            @block.vector
            def _(dve):
                dve.wait_ge(const_loaded, 48)
                nc.vector.tensor_copy(w_r[:, HI], raw_r[:, :, :]).then_inc(const_v, 1)
                dve.wait_ge(const_v, 1)
                nc.vector.tensor_tensor(w_r[:, LO], raw_r[:, :, :], w_r[:, HI], ALU.subtract).then_inc(const_v, 1)

                def mix(s, half):
                    e, g = s.expert(2), s.group(2)
                    dve.wait_ge(l3_filled, s.n(2, 2) - (1 - half))
                    for t in range(2):
                        b = GRP * g + 2 * half + t
                        if e == 0:
                            dve.wait_ge(acc_ready, s.J * B + (b + 1 - B - (B if s.i < 2 else 0)))
                        else:
                            dve.wait_ge(mixed, s.n(3, 4) - (3 - 2 * half - t))
                        nc.vector.scalar_tensor_tensor(out=acc[:, b, :], in0=p_3[half][0:TOK, t, :],
                                                       scalar=gate[:, e:e + 1], in1=acc[:, b, :],
                                                       op0=ALU.mult, op1=ALU.add).then_inc(mixed, 1)

                def low(s, lag, full, parts, high, low_):
                    for m in range(KT):
                        dve.wait_ge(high, s.n(lag, 2) - (KT - 1 - m))
                        nc.vector.tensor_tensor(parts[:, LO, m, :], full[:, m, 0:NTOK], parts[:, HI, m, :],
                                                ALU.subtract).then_inc(low_, 1)

                def soft(k, s, ins):
                    ins.then_inc(soft_v, 1)
                    dve.wait_ge(soft_v, s.J * SOFT + k)

                def step(s):
                    if s.has(2) and s.i == 2:
                        dve.wait_ge(soft_v, s.J * SOFT)
                        if s.has(3):
                            dve.wait_ge(mixed, s.n(3, 4))
                        nc.vector.tensor_copy(gate[:, :], gate_new[:, :]).then_inc(gate_ready, 1)
                        dve.wait_ge(gate_ready, s.J)
                    if s.has(2):
                        mix(s, 0)
                    if s.has(0) and s.i == 0:
                        dve.wait_ge(gate_t_filled, s.J)
                        nc.vector.tensor_copy(gate_t[:, :], p_z[0:E, 0:TOK]).then_inc(gate_t_ready, 1)
                    if s.has(0) and s.i == 1:
                        dve.wait_ge(yb_filled, s.J)
                        if s.has(16):
                            dve.wait_ge(acc_ready, s.J * B - B)
                        nc.vector.tensor_copy(yb[:, :], p_z[0:TOK, 0:D]).then_inc(yb_ready, 1)
                    b = s.tile(2)
                    if b is not None:
                        if s.has_m(max(b - 3, -1)):
                            dve.wait_ge(r_ready, s.m(max(b - 3, -1)))
                        dve.wait_ge(sga_ready, s.m(b))
                        nc.vector.tensor_tensor(rs[:, :], bank_za(s)[0:TOK, 0:D], rsg[:, 0, :],
                                                ALU.mult).then_inc(sa_ready, 1)
                        dve.wait_ge(sa_ready, s.m(b))
                        nc.vector.tensor_tensor(q1[:, b % 3, :], qin[:, b % 4, :], rs[:, :],
                                                ALU.add).then_inc(q1_ready, 1)
                    if retrieves(s) and s.i == 15:
                        dve.wait_ge(logits_filled, s.J + 1)
                        soft(1, s, nc.vector.scalar_tensor_tensor(out=logit[:, :], in0=p_z[0:TOK, 0:E],
                                                                  scalar=1.0 / B, in1=br_b[:, :],
                                                                  op0=ALU.mult, op1=ALU.add))
                        soft(2, s, nc.vector.reduce_max(top[:, :], logit[:, :], AX_X))
                        soft(3, s, nc.vector.tensor_scalar(logit[:, :], logit[:, :], top[:, :], None,
                                                           ALU.subtract))
                        dve.wait_ge(sig_ready, s.J + 1)
                        soft(4, s, nc.vector.reciprocal(sig[:, 1, :], sig[:, 1, :]))
                        soft(5, s, nc.vector.tensor_tensor(logit[:, :], sig[:, 0, :], sig[:, 1, :], ALU.mult))
                        soft(6, s, nc.vector.reduce_sum(total[:, :], logit[:, :], AX_X))
                        soft(7, s, nc.vector.reciprocal(total[:, :], total[:, :]))
                        soft(8, s, nc.vector.tensor_scalar(gate_new[:, :], logit[:, :], total[:, :], None,
                                                           ALU.mult))
                    if s.has(2):
                        mix(s, 1)
                    b = s.tile(0)
                    if b is not None:
                        dve.wait_ge(qh_ready, s.m(b))
                        nc.vector.tensor_tensor(qs[:, LO, :], qin[:, b % 4, :], qs[:, HI, :],
                                                ALU.subtract).then_inc(ql_ready, 1)
                    b = s.tile(5)
                    if b is not None:
                        dve.wait_ge(rstd_ready, s.m(b))
                        if s.has_m(b - 2):
                            dve.wait_ge(feat_added, s.J * ADDS + max(b - 2, 1 if b > 1 else 0))
                            dve.wait_ge(xnl_ready, s.m(b - 2))
                        nc.vector.tensor_scalar(xn2[:, b % 2, :], res[:, b, :], mv[:, b % 2, 0:1], rstd[:, b % 2, :],
                                                ALU.subtract, ALU.mult).then_inc(xn_ready, 1)
                    if s.has(1):
                        low(s, 1, h2f, h2s, h2h_ready, h2l_ready)
                    b = s.tile(4)
                    if b is not None:
                        dve.wait_ge(q1_ready, s.m(min(b + 2, B - 1)))
                        dve.wait_ge(sgb_ready, s.m(b))
                        nc.vector.tensor_tensor(rs[:, :], p_z[0:TOK, 0:D], rsg[:, 1, :],
                                                ALU.mult).then_inc(sb_ready, 1)
                        dve.wait_ge(sb_ready, s.m(b))
                        nc.vector.tensor_tensor(rs[:, :], q1[:, b % 3, :], rs[:, :],
                                                ALU.add).then_inc(r_ready, 1)
                        dve.wait_ge(r_ready, s.m(b))
                        dve.wait_ge(h_loaded[b], s.J * 16 + 16)
                        nc.vector.tensor_tensor(res[:, b, :], res[:, b, :], rs[:, :],
                                                ALU.add).then_inc(res_ready, 1)
                        dve.wait_ge(res_ready, s.m(b))
                        nc.vector.bn_stats(stats[:, :], res[:, b, :]).then_inc(stat_ready, 1)
                    b = s.tile(2)
                    if b is not None:
                        dve.wait_ge(q1h_ready, s.m(b))
                        nc.vector.tensor_tensor(q1s[:, LO, :], q1[:, b % 3, :], q1s[:, HI, :],
                                                ALU.subtract).then_inc(q1l_ready, 1)
                    b4 = s.tile(4)
                    if b4 is not None:
                        dve.wait_ge(stat_ready, s.m(b4))
                    b = s.tile(5)
                    if b is not None:
                        dve.wait_ge(xnh_ready, s.m(b))
                        nc.vector.tensor_tensor(xn2s[:, LO, :], xn2[:, b % 2, :], xn2s[:, HI, :],
                                                ALU.subtract).then_inc(xnl_ready, 1)
                    if s.has(0):
                        low(s, 0, h1f, h1s, h1h_ready, h1l_ready)
                    if b4 is not None:
                        nc.vector.bn_aggr(mv[:, b4 % 2, :], stats[:, :]).then_inc(mv_ready, 1)
                    if retrieves(s) and s.i == 13:
                        dve.wait_ge(feath_ready, s.J + 1)
                        nc.vector.tensor_tensor(xn2s[:, LO, :], feat[:, :], xn2s[:, HI, :],
                                                ALU.subtract).then_inc(featl_ready, 1)
                    for n in weight_jobs(s, 1):
                        i, e = jobs[n]
                        if i == 2:
                            dve.wait_ge(w_high, n + 1)
                            nc.vector.tensor_tensor(ffn_w[i][:, e, LO], raw(n), ffn_w[i][:, e, HI],
                                                    ALU.subtract).then_inc(w3_low, 1)

                macros(dve, step)

            @block.tensor
            def _(pe):
                mm = nc.tensor.matmul

                def product(dst, left, right, start=True, stop=True):
                    n = 0
                    for k in range(KT):
                        for h, g in ((HI, HI), (HI, LO), (LO, HI)):
                            n += 1
                            last = mm(dst, left(h, k), right(g, k), start=start and n == 1,
                                      stop=stop and n == 3 * KT, skip_group_check=True)
                    return last

                def transposes(dst, src):
                    for h in (HI, LO):
                        for k in range(KT):
                            at = (h * KT + k) * TP
                            last = mm(dst[:, at:at + TP], src[:, h, k * 128:(k + 1) * 128],
                                      eye_r[0:TOK, :], start=True, stop=True, skip_group_check=True)
                    return last

                def weights_split(s, lag, layer):
                    if isinstance(s.J, int) and s.J == 1 and 0 <= s.i - lag < E:
                        wait_low(pe, 3 * (s.i - lag) + layer)

                def normed_transposes(s):
                    b = s.tile(6)
                    if b is not None:
                        pe.wait_ge(xnl_ready, s.m(b))
                        if alone(s):
                            if b > 0:
                                pe.wait_ge(xt_ready, s.m(b - 1))
                        elif b + 5 < B:
                            pe.wait_ge(qt_ready, s.m(b + 5))
                        elif b + 2 < B:
                            pe.wait_ge(q1t_ready, s.m(b + 2))
                        else:
                            pe.wait_ge(xt_ready, s.m(b - 1))
                        transposes(bank_x(s), xn2s).then_inc(xt_filled, 1)
                    if retrieves(s) and s.i == 14:
                        pe.wait_ge(featl_ready, s.J + 1)
                        pe.wait_ge(xt_ready, s.m(B - 1))
                        transposes(bank_x(s), xn2s).then_inc(featt_filled, 1)

                def layer(s, lag, bank, w, rhs, filled):
                    e = s.expert(lag)
                    weights_split(s, lag, lag)
                    for m in range(KT):
                        cols = slice(m * 128, (m + 1) * 128)
                        product(bank[m][:, 0:NTOK], lambda h, k: w[:, e, h, k, cols], rhs).then_inc(filled, 1)

                def layer3(s, half):
                    e = s.expert(2)
                    weights_split(s, 2, 2)
                    if s.has(3):
                        pe.wait_ge(mixed, s.n(3, 4) - 2 * (1 - half))
                    for t in range(2):
                        at = (2 * half + t) * TOK
                        last = product(p_3[half][0:TOK, t, :], lambda h, k: h2s[:, h, k, at:at + TOK],
                                       lambda h, k: ffn_w[2][:, e, h, k, :])
                    last.then_inc(l3_filled, 1)

                def retrieval_layer(dst, l, src, filled):
                    product(dst[0:TOK, 0:D], lambda h, k: src[:, h, k, 0:TOK],
                            lambda h, k: new_w[:, l, h, k, :], stop=False)
                    mm(dst[0:TOK, 0:D], bias_on[:, :], new_bias[:, l, :], start=False, stop=True,
                       skip_group_check=True).then_inc(filled, 1)

                def step(s):
                    if s.has(2):
                        pe.wait_ge(h2l_ready, s.n(2, 2))
                        layer3(s, 0)
                    if s.has(0) and s.i == 0:
                        pe.wait_ge(soft_v, s.J * SOFT)
                        nc.tensor.transpose(p_z[0:E, 0:TOK], gate_new[:, :],
                                            eye[0:TOK, 0:TOK]).then_inc(gate_t_filled, 1)
                    if s.has(0) and s.i == 1:
                        pe.wait_ge(gate_t_ready, s.J)
                        mm(p_z[0:TOK, 0:D], gate_t[:, :], bo_s[:, :], start=True,
                           stop=True).then_inc(yb_filled, 1)
                    b = s.tile(2)
                    if b is not None:
                        pe.wait_ge(qt_ready, s.m(b))
                        if b == 0:
                            if s.has_m(b - 8):
                                pe.wait_ge(yb_ready, s.J)
                        elif b < 3 or alone(s):
                            pe.wait_ge(sa_ready, s.m(b - 1))
                        else:
                            pe.wait_ge(sb_ready, s.m(b - 3))
                        retrieval_layer(bank_za(s), 0, q_t, za_filled)
                    b = s.tile(1)
                    if b is not None:
                        pe.wait_ge(ql_ready, s.m(b))
                        if b >= 3 and not alone(s):
                            pe.wait_ge(q1t_ready, s.m(b - 3))
                        elif b >= 1:
                            pe.wait_ge(qt_ready, s.m(b - 1))
                        elif s.has_m(-1):
                            pe.wait_ge(featt_ready, s.J)
                        transposes(bank_q(s), qs).then_inc(qt_filled, 1)
                    if s.has(2):
                        layer3(s, 1)
                    if not alone(s):
                        normed_transposes(s)
                    if s.has(1):
                        pe.wait_ge(h1l_ready, s.n(1, 2))
                        if s.has(2):
                            pe.wait_ge(h2h_ready, s.n(2, 2))
                        layer(s, 1, p_2, ffn_w[1], lambda h, k: h1s[:, h, k, :], l2_filled)
                    b = s.tile(4)
                    if b is not None:
                        pe.wait_ge(q1t_ready, s.m(b))
                        if alone(s):
                            if b > 0:
                                pe.wait_ge(sb_ready, s.m(b - 1))
                        elif b + 2 < B:
                            pe.wait_ge(sa_ready, s.m(b + 2))
                        else:
                            pe.wait_ge(sb_ready, s.m(b - 1))
                        retrieval_layer(p_z, 1, q1_t, zb_filled)
                    b = s.tile(3)
                    if b is not None:
                        pe.wait_ge(q1l_ready, s.m(b))
                        if alone(s):
                            if b > 0:
                                pe.wait_ge(q1t_ready, s.m(b - 1))
                        elif b >= 3:
                            pe.wait_ge(xt_ready, s.m(b - 3))
                        else:
                            pe.wait_ge(qt_ready, s.m(b + 2))
                        transposes(p_t, q1s).then_inc(q1t_filled, 1)
                    if s.has(0):
                        g = s.group(0)
                        if s.i % E == 0:
                            pe.wait_ge(copied[g], s.J * 16)
                        if s.has(1):
                            pe.wait_ge(h1h_ready, s.n(1, 2))
                        at = slice(GRP * g, GRP * g + GRP)
                        layer(s, 0, p_1, ffn_w[0],
                              lambda h, k: xt_use[:, h, k, at, :].rearrange("p b t -> p (b t)"), l1_filled)
                    if alone(s):
                        normed_transposes(s)
                    if retrieves(s) and s.i == 14:
                        pe.wait_ge(featt_ready, s.J + 1)
                        pe.wait_ge(sb_ready, s.m(B - 1))
                        pe.wait_ge(const_v, 2)
                        product(p_z[0:TOK, 0:E], lambda h, k: q1_t[:, h, k, 0:TOK],
                                lambda h, k: w_r[:, h, k, :]).then_inc(logits_filled, 1)

                macros(pe, step)


_INS = ['x', 'L0_tok_blur_kernel', 'L0_attn_Wk', 'L0_attn_Wq', 'L0_attn_Wv', 'L0_attn_Wlr', 'L0_attn_blr',
        'L0_attn_Ws', 'L0_attn_bs', 'L0_ffn_Wr', 'L0_ffn_br', 'L0_ffn_W1', 'L0_ffn_b1', 'L0_ffn_g1',
        'L0_ffn_be1', 'L0_ffn_m1', 'L0_ffn_v1', 'L0_ffn_W2', 'L0_ffn_b2', 'L0_ffn_g2', 'L0_ffn_be2',
        'L0_ffn_m2', 'L0_ffn_v2', 'L0_ffn_Wo', 'L0_ffn_bo']
_OUTS = [((B, TOKENS, D), 'float32')]


def kernel(**inputs):
    import numpy as _np
    import concourse.bacc as _bacc
    from concourse import mybir as _mybir
    from concourse.bass_utils import run_bass_kernel_spmd as _run

    nc = _bacc.Bacc("TRN2", target_bir_lowering=False, num_devices=1)
    arrays, args = {}, []
    for name in _INS:
        a = _np.ascontiguousarray(inputs[name])
        arrays[f"in_{name}_dram"] = a
        args.append(nc.dram_tensor(f"in_{name}_dram", a.shape, _mybir.dt.from_np(a.dtype), kind="ExternalInput").ap())
    for i, (shape, dtype) in enumerate(_OUTS):
        dt = _mybir.dt.from_np(_np.dtype(dtype))
        args.append(nc.dram_tensor(f"out_{i}_dram", shape, dt, kind="ExternalOutput").ap())
    audio_tower(nc, *args)
    r = _run(nc, [arrays], core_ids=[0])
    got = tuple(r.results[0][f"out_{i}_dram"] for i in range(len(_OUTS)))
    return got[0]
```
